# Optimizing a Trainium2 kernel written in Bass

```python
import numpy as np
import jax
import jax.numpy as jnp

def _softmax(x, axis=-1):
    return jax.nn.softmax(x, axis=axis)

def _gelu(x):
    return jax.nn.gelu(x, approximate=True)

def _silu(x):
    return jax.nn.silu(x)

def _sigmoid(x):
    return jax.nn.sigmoid(x)

def _layernorm(x, axis=-1, eps=1e-05):
    m = jnp.mean(x, axis=axis, keepdims=True)
    v = jnp.var(x, axis=axis, keepdims=True)
    return (x - m) / jnp.sqrt(v + eps)

def _scatter_add(tgt, idx, src, axis=0):
    return tgt.at[idx].add(src)

def _segment_sum(src, seg, n):
    return jax.ops.segment_sum(src, seg, n)
kernel_name = 'mk_sandwich_d1_jaxref_r8_5be1b3'

def setup_inputs(seed: int=0):
    np.random.seed(seed)
    _w = jnp.asarray

    def _L0_attn_setup():
        import jax, jax.numpy as jnp
        import numpy as np
        B_SZ, SEQ, D_MODEL = (2, 256, 256)
        D_INNER, D_XB, INTER = (512, 128, 1024)
        HEADDIM = 64
        DSTATE = 64
        NHEADS = D_INNER // HEADDIM
        N_XB = D_XB // HEADDIM
        REP = NHEADS // N_XB
        D_IN_PROJ = D_INNER + D_XB + D_XB + D_INNER + NHEADS
        EPS = 1e-05

        def _layernorm(x, w, b):
            mu = jnp.mean(x, -1, keepdims=True)
            var = jnp.mean((x - mu) ** 2, -1, keepdims=True)
            return (x - mu) * jax.lax.rsqrt(var + EPS) * w + b

        def _mamba2(hs, W_in, dt_bias, A_log, D, norm_w, W_out):
            B, L, _ = hs.shape
            zxbcdt = hs @ W_in
            splits = [D_INNER, D_INNER + D_XB, D_INNER + 2 * D_XB, D_INNER + 2 * D_XB + D_INNER]
            z, xb, Bp, Cp, dt = jnp.split(zxbcdt, splits, axis=-1)
            xh = jnp.repeat(xb.reshape(B, L, N_XB, HEADDIM), REP, axis=2)
            Bh = jnp.repeat(Bp.reshape(B, L, N_XB, DSTATE), REP, axis=2)
            Ch = Cp.reshape(B, L, NHEADS, DSTATE)
            dt = jax.nn.softplus(dt + dt_bias)
            A = -jnp.exp(A_log)
            dA = jnp.exp(dt * A)

            def step(state, inp):
                dA_t, dt_t, B_t, x_t, C_t = inp
                dBx = (dt_t[:, :, None] * x_t)[..., None] * B_t[:, :, None, :]
                state = state * dA_t[:, :, None, None] + dBx
                y_t = jnp.einsum('bhpn,bhn->bhp', state, C_t)
                return (state, y_t)
            xs = (jnp.swapaxes(dA, 0, 1), jnp.swapaxes(dt, 0, 1), jnp.swapaxes(Bh, 0, 1), jnp.swapaxes(xh, 0, 1), jnp.swapaxes(Ch, 0, 1))
            state0 = jnp.zeros((B, NHEADS, HEADDIM, DSTATE), hs.dtype)
            _, ys = jax.lax.scan(step, state0, xs)
            y = jnp.swapaxes(ys, 0, 1) + D[None, None, :, None] * xh
            y = y.reshape(B, L, D_INNER)
            yg = y * jax.nn.silu(z)
            yn = yg * jax.lax.rsqrt(jnp.mean(yg * yg, -1, keepdims=True) + EPS) * norm_w
            return yn @ W_out
        key = jax.random.key(seed)
        ks = jax.random.split(key, 10)
        s = 0.02
        return {'hidden_states': jax.random.normal(ks[0], (B_SZ, SEQ, D_MODEL), jnp.float32), 'ln_w': jnp.ones((D_MODEL,), jnp.float32), 'ln_b': jnp.zeros((D_MODEL,), jnp.float32), 'W_in': jax.random.normal(ks[1], (D_MODEL, D_IN_PROJ), jnp.float32) * s, 'dt_bias': jax.random.uniform(ks[2], (NHEADS,), jnp.float32, -4.0, -2.0), 'A_log': jnp.log(jnp.arange(1, NHEADS + 1, dtype=jnp.float32)), 'D': jnp.ones((NHEADS,), jnp.float32), 'norm_w': jnp.ones((D_INNER,), jnp.float32), 'W_out': jax.random.normal(ks[3], (D_INNER, D_MODEL), jnp.float32) * s, 'fc1_w': jax.random.normal(ks[4], (D_MODEL, INTER), jnp.float32) * s, 'fc1_b': jnp.zeros((INTER,), jnp.float32), 'fc2_w': jax.random.normal(ks[5], (INTER, D_MODEL), jnp.float32) * s, 'fc2_b': jnp.zeros((D_MODEL,), jnp.float32)}
    _L0_attn_in = _L0_attn_setup()

    def _L0_ffn_setup():
        import jax, jax.numpy as jnp
        import numpy as np
        E = 8
        K = 2
        C = 256
        I = 176
        IS = I * 2
        B, T = (2, 256)
        key = jax.random.key(seed)
        ks = jax.random.split(key, 9)
        s = 0.02
        return {'x': jax.random.normal(ks[0], (B, T, C), dtype=jnp.float32), 'gate_w': jax.random.normal(ks[1], (E, C), dtype=jnp.float32) * s, 'w1': jax.random.normal(ks[2], (E, I, C), dtype=jnp.float32) * s, 'w2': jax.random.normal(ks[3], (E, I, C), dtype=jnp.float32) * s, 'w3': jax.random.normal(ks[4], (E, C, I), dtype=jnp.float32) * s, 'sw1': jax.random.normal(ks[5], (IS, C), dtype=jnp.float32) * s, 'sw2': jax.random.normal(ks[6], (IS, C), dtype=jnp.float32) * s, 'sw3': jax.random.normal(ks[7], (C, IS), dtype=jnp.float32) * s}
    _L0_ffn_in = _L0_ffn_setup()
    _d = {'L0_attn_hidden_states': _L0_attn_in['hidden_states'], 'L0_attn_ln_w': _L0_attn_in['ln_w'], 'L0_attn_ln_b': _L0_attn_in['ln_b'], 'L0_attn_W_in': _L0_attn_in['W_in'], 'L0_attn_dt_bias': _L0_attn_in['dt_bias'], 'L0_attn_A_log': _L0_attn_in['A_log'], 'L0_attn_D': _L0_attn_in['D'], 'L0_attn_norm_w': _L0_attn_in['norm_w'], 'L0_attn_W_out': _L0_attn_in['W_out'], 'L0_attn_fc1_w': _L0_attn_in['fc1_w'], 'L0_attn_fc1_b': _L0_attn_in['fc1_b'], 'L0_attn_fc2_w': _L0_attn_in['fc2_w'], 'L0_attn_fc2_b': _L0_attn_in['fc2_b'], 'L0_ffn_gate_w': _L0_ffn_in['gate_w'], 'L0_ffn_w1': _L0_ffn_in['w1'], 'L0_ffn_w2': _L0_ffn_in['w2'], 'L0_ffn_w3': _L0_ffn_in['w3'], 'L0_ffn_sw1': _L0_ffn_in['sw1'], 'L0_ffn_sw2': _L0_ffn_in['sw2'], 'L0_ffn_sw3': _L0_ffn_in['sw3']}
    _x0 = _d['L0_attn_hidden_states']
    _d['L0_attn_hidden_states'] = jax.random.normal(jax.random.fold_in(jax.random.key(seed), 1), (2, 2048, 256), dtype=_x0.dtype)
    del _x0
    return _d

def reference(L0_attn_hidden_states, L0_attn_ln_w, L0_attn_ln_b, L0_attn_W_in, L0_attn_dt_bias, L0_attn_A_log, L0_attn_D, L0_attn_norm_w, L0_attn_W_out, L0_attn_fc1_w, L0_attn_fc1_b, L0_attn_fc2_w, L0_attn_fc2_b, L0_ffn_gate_w, L0_ffn_w1, L0_ffn_w2, L0_ffn_w3, L0_ffn_sw1, L0_ffn_sw2, L0_ffn_sw3):

    def _L0_attn_ref(hidden_states, ln_w, ln_b, W_in, dt_bias, A_log, D, norm_w, W_out, fc1_w, fc1_b, fc2_w, fc2_b):
        import jax, jax.numpy as jnp
        import numpy as np
        B_SZ, SEQ, D_MODEL = (2, 256, 256)
        D_INNER, D_XB, INTER = (512, 128, 1024)
        HEADDIM = 64
        DSTATE = 64
        NHEADS = D_INNER // HEADDIM
        N_XB = D_XB // HEADDIM
        REP = NHEADS // N_XB
        D_IN_PROJ = D_INNER + D_XB + D_XB + D_INNER + NHEADS
        EPS = 1e-05

        def _layernorm(x, w, b):
            mu = jnp.mean(x, -1, keepdims=True)
            var = jnp.mean((x - mu) ** 2, -1, keepdims=True)
            return (x - mu) * jax.lax.rsqrt(var + EPS) * w + b

        def _mamba2(hs, W_in, dt_bias, A_log, D, norm_w, W_out):
            B, L, _ = hs.shape
            zxbcdt = hs @ W_in
            splits = [D_INNER, D_INNER + D_XB, D_INNER + 2 * D_XB, D_INNER + 2 * D_XB + D_INNER]
            z, xb, Bp, Cp, dt = jnp.split(zxbcdt, splits, axis=-1)
            xh = jnp.repeat(xb.reshape(B, L, N_XB, HEADDIM), REP, axis=2)
            Bh = jnp.repeat(Bp.reshape(B, L, N_XB, DSTATE), REP, axis=2)
            Ch = Cp.reshape(B, L, NHEADS, DSTATE)
            dt = jax.nn.softplus(dt + dt_bias)
            A = -jnp.exp(A_log)
            dA = jnp.exp(dt * A)

            def step(state, inp):
                dA_t, dt_t, B_t, x_t, C_t = inp
                dBx = (dt_t[:, :, None] * x_t)[..., None] * B_t[:, :, None, :]
                state = state * dA_t[:, :, None, None] + dBx
                y_t = jnp.einsum('bhpn,bhn->bhp', state, C_t)
                return (state, y_t)
            xs = (jnp.swapaxes(dA, 0, 1), jnp.swapaxes(dt, 0, 1), jnp.swapaxes(Bh, 0, 1), jnp.swapaxes(xh, 0, 1), jnp.swapaxes(Ch, 0, 1))
            state0 = jnp.zeros((B, NHEADS, HEADDIM, DSTATE), hs.dtype)
            _, ys = jax.lax.scan(step, state0, xs)
            y = jnp.swapaxes(ys, 0, 1) + D[None, None, :, None] * xh
            y = y.reshape(B, L, D_INNER)
            yg = y * jax.nn.silu(z)
            yn = yg * jax.lax.rsqrt(jnp.mean(yg * yg, -1, keepdims=True) + EPS) * norm_w
            return yn @ W_out
        residual = hidden_states
        hs = _layernorm(hidden_states, ln_w, ln_b)
        attn = _mamba2(hs, W_in, dt_bias, A_log, D, norm_w, W_out)
        mlp = jax.nn.gelu(hs @ fc1_w + fc1_b, approximate=True) @ fc2_w + fc2_b
        return attn + mlp + residual

    def _L0_ffn_ref(x, gate_w, w1, w2, w3, sw1, sw2, sw3):
        import jax, jax.numpy as jnp
        import numpy as np
        E = 8
        K = 2
        C = 256
        I = 176
        IS = I * 2
        B, T = (2, 256)
        Bq, Tq, Cq = x.shape
        xf = x.reshape(-1, Cq)
        logits = xf @ gate_w.T
        probs = jax.nn.softmax(logits.astype(jnp.float32), axis=-1)
        topk_p, topk_i = jax.lax.top_k(probs, K)
        comb = (jax.nn.one_hot(topk_i, E, dtype=jnp.float32) * topk_p[..., None]).sum(axis=1).astype(x.dtype)
        h1 = jnp.einsum('nc,eic->eni', xf, w1)
        h2 = jnp.einsum('nc,eic->eni', xf, w2)
        h = jax.nn.silu(h1) * h2
        eo = jnp.einsum('eni,eci->enc', h, w3)
        y = jnp.einsum('enc,ne->nc', eo, comb).reshape(Bq, Tq, Cq)
        sh = jax.nn.silu(xf @ sw1.T) * (xf @ sw2.T) @ sw3.T
        return y + sh.reshape(Bq, Tq, Cq)
    x = L0_attn_hidden_states
    x = x + _layernorm(_L0_attn_ref(_layernorm(x, axis=-1), L0_attn_ln_w, L0_attn_ln_b, L0_attn_W_in, L0_attn_dt_bias, L0_attn_A_log, L0_attn_D, L0_attn_norm_w, L0_attn_W_out, L0_attn_fc1_w, L0_attn_fc1_b, L0_attn_fc2_w, L0_attn_fc2_b), axis=-1)
    x = x + _layernorm(_L0_ffn_ref(_layernorm(x, axis=-1), L0_ffn_gate_w, L0_ffn_w1, L0_ffn_w2, L0_ffn_w3, L0_ffn_sw1, L0_ffn_sw2, L0_ffn_sw3), axis=-1)
    return x

_drawn_inputs = setup_inputs


def setup_inputs(seed=0):
    import zlib

    import numpy as np

    out = dict(_drawn_inputs(seed))
    spreads = {'L0_attn_ln_w': (1.0, 0.2),
     'L0_attn_ln_b': (0.0, 0.1),
     'L0_attn_D': (1.0, 0.6),
     'L0_attn_norm_w': (1.0, 0.2),
     'L0_attn_fc1_b': (0.0, 0.409),
     'L0_attn_fc2_b': (0.0, 0.1)}
    factors = {'L0_attn_dt_bias': 43.336, 'L0_attn_A_log': 29.568}
    for name, (base, spread) in spreads.items():
        noise = np.random.default_rng([zlib.crc32(name.encode()), seed]).standard_normal(out[name].shape)
        drawn = base * np.exp(spread * noise) if base else spread * noise
        out[name] = jnp.asarray(drawn.astype(out[name].dtype))
    for name, factor in factors.items():
        out[name] = (out[name] * factor).astype(out[name].dtype)
    return out
```

```python
from contextlib import ExitStack

import numpy as np
import concourse.bass as bass
from concourse import mybir

F32 = mybir.dt.float32
BF16 = mybir.dt.bfloat16
I32 = mybir.dt.int32
ALU = mybir.AluOpType
ACT = mybir.ActivationFunctionType
AX_X = mybir.AxisListType.X

P = 128
DM = 256
KD = DM // P
NH, HD, NG, JH = 8, 64, 2, 4
DI = NH * HD
XB = NG * HD
INTER = 1024
KF = INTER // P
CH = 4
TB = CH * P
NE, EI = 8, 176
NX = NE + 2
EK = EI // 2
EPS = 1e-5
XBD = 2 * XB + NH
A_MIN = -200.0
C_ID, C_INCL, C_AFTER, C_ONES, C_LOWER, C_COLS, C_KEEP = 0, 128, 256, 384, 512, 576, 592
NC_C = 600
R_DTB, R_ALOG, R_D, R_FB = 0, 8, 16, 24
NC_R = 24 + DM


class Chain:

    def __init__(self, eng, sem, per):
        self.eng, self.sem, self.per, self.base, self.n = eng, sem, per, 0, 0

    def start(self, base):
        self.base, self.n = base, 0

    def link(self, ins, carry=None):
        self.n += 1
        ins.then_inc(self.sem, 1)
        self.eng.wait_ge(self.sem, self.base + self.n)
        if carry is not None:
            self.eng.sem_inc(carry, 1)

    def end(self):
        assert self.n == self.per, self.n


def build(nc, x, w_in, w_out, fc1, fc2, w12, w3, cst, rows, sel, out):
    NT = x.shape[0] // P
    NB = NT // CH
    W12N = w12.shape[1]

    with ExitStack() as ctx:
        def sb(name, shape, dt=F32):
            return ctx.enter_context(nc.sbuf_tensor(name, shape, dt))

        def bank(name):
            return ctx.enter_context(nc.psum_tensor(name, [P, 512], F32))

        def sem(name):
            return ctx.enter_context(nc.semaphore(name))

        xa = sb("xa", [P, NT + CH, DM])
        win_s = sb("win_s", [P, KD, 2 * DI + XBD])
        late = sb("late", [P, 2 * NX * DM])
        fc1_s = late[:, 0:KD * INTER].rearrange("p (k n) -> p k n", k=KD)
        fc2_s = late[:, KD * INTER:KD * INTER + KF * DM].rearrange("p (k n) -> p k n", k=KF)
        wout_s = late[:, KD * INTER + KF * DM:].rearrange("p (k n) -> p k n", k=DI // P)
        w3_s = late[0:EK, :].rearrange("p (k n) -> p k n", k=2 * NX)
        w12_s = sb("w12_s", [P, KD, W12N])
        cs = sb("cs", [P, NC_C])
        rw = sb("rw", [P, NC_R])
        sel_b = sb("sel_b", [3 * NH, NH, P], BF16)
        ident_b = sb("ident_b", [P, P], BF16)
        ident4 = sb("ident4", [P, CH, P])
        nhalf = sb("nhalf", [P, CH])
        keep = sb("keep", [P, NB], I32)
        a_neg = sb("a_neg", [P, NH])
        ident = cs[:, C_ID:C_ID + P]
        lnw, lnb = cs[:, C_COLS:C_COLS + 2], cs[:, C_COLS + 2:C_COLS + 4]
        nrw, f1b = cs[:, C_COLS + 4:C_COLS + 8], cs[:, C_COLS + 8:C_COLS + 16]

        st1 = sb("st1", [P, CH, 6])
        mvb = sb("mvb", [P, CH, 2])
        mv1 = sb("mv1", [P, NT + CH, 2])
        rs1 = sb("rs1", [P, NT + CH])
        nw = sb("nw", [P, 6, CH])
        v = sb("v", [P, CH, DM])
        hsT = sb("hsT", [P, KD, TB])
        xbd = sb("xbd", [P, CH, XBD])
        cT = sb("cT", [P, JH, TB])
        bT = sb("bT", [P, TB])
        sz = sb("sz", [P, CH, DI])
        gT = sb("gT", [P, KF, TB])
        sel_f = gT[0:3 * NH, 0:NH * P // TB, :].rearrange("p k t -> p (k t)")
        dtw = sb("dtw", [P, 14, CH, NH])
        parts = sb("parts", [P, CH, 3, NH], BF16)
        partsT = sb("partsT", [3 * NH, CH, P], BF16)
        pwd = sb("pwd", [P, 2, CH, NH])
        dec = sb("dec", [P, CH, JH])
        L = sb("L", [P, NH, TB])
        xdt = sb("xdt", [P, 2, DI])
        xw = sb("xw", [P, 2, DI])
        dx = sb("dx", [P, DI])
        M = sb("M", [P, 2, NH, P])
        S = sb("S", [P, JH, P])
        t1 = sb("t1", [P, DI])
        t2 = sb("t2", [P, DI])
        t3 = sb("t3", [P, DI])
        yg = sb("yg", [P, DI])
        ygn = sb("ygn", [P, DI])
        rr = sb("rr", [P, 4])
        ynT = sb("ynT", [P, DI // P, P])
        ub = sb("ub", [P, DM])
        o = sb("o", [P, DM])
        st3 = sb("st3", [P, 6])
        mv3 = sb("mv3", [P, 2])
        r3 = sb("r3", [P, 2])
        xf = sb("xf", [P, DM])
        Mf = M[:].rearrange("p a h t -> p (a h t)")
        xfT = Mf[:, 0:2 * DM].rearrange("p (a k t) -> p a k t", a=2, k=KD)
        heT = Mf[0:EK, 2 * DM:4 * DM].rearrange("p (a k t) -> p a k t", a=2, k=2)
        hs_ = Mf[:, 4 * DM:4 * DM + 2 * EI].rearrange("p (a n) -> p a n", a=2)
        he = Mf[:, 4 * DM + 2 * EI:4 * DM + 4 * EI].rearrange("p (a n) -> p a n", a=2)
        st4 = sb("st4", [P, 6])
        mv4 = sb("mv4", [P, 2])
        r4 = sb("r4", [P, 2])
        gw = sb("gw", [P, 8, NE])
        gs = sb("gs", [P, 4])
        cmp_ = sb("cmp_", [P, 3, NE, NE])
        comb = sb("comb", [P, 2, NE])
        d5 = sb("d5", [P, DM])
        st5 = sb("st5", [P, 6])
        mv5 = sb("mv5", [P, 2])
        r5 = sb("r5", [P, 2])

        W = [bank(f"W{k}") for k in range(3)]
        X = [bank(f"X{k}") for k in range(2)]
        Y, I, O = bank("Y"), bank("I"), bank("O")

        s_x, s_cs, s_rw, s_sel, s_win = sem("s_x"), sem("s_cs"), sem("s_rw"), sem("s_sel"), sem("s_win")
        s_fc1, s_fc2, s_wout, s_w12, s_w3 = sem("s_fc1"), sem("s_fc2"), sem("s_wout"), sem("s_w12"), sem("s_w3")
        s_out = sem("s_out")
        dve_step, pool_step, act_step = sem("dve_step"), sem("pool_step"), sem("act_step")
        dve_step2, pool_step2, act_step2 = sem("dve_step2"), sem("pool_step2"), sem("act_step2")
        consts_ready, aneg_ready, dve_init, pool_init = sem("consts_ready"), sem("aneg_ready"), sem("dve_init"), sem("pool_init")
        mv_ready, dve_carry, pool_carry, sp_carry = sem("mv_ready"), sem("dve_carry"), sem("pool_carry"), sem("sp_carry")
        dve_st, pool_norm, rs1_ready, dx_ready, st4_s = sem("dve_st"), sem("pool_norm"), sem("rs1_ready"), sem("dx_ready"), sem("st4_s")
        vt_done, xb_done, ct_done, bt_done = sem("vt_done"), sem("xb_done"), sem("ct_done"), sem("bt_done")
        z_done, pt_done, cum_done, fc1_done = sem("z_done"), sem("pt_done"), sem("cum_done"), sem("fc1_done")
        bc_done, g_done, inter_done, inc_done = sem("bc_done"), sem("g_done"), sem("inter_done"), sem("inc_done")
        y_done, yt_done, o_done = sem("y_done"), sem("yt_done"), sem("o_done")
        st_ready, rs_ready, v_ready, hst_ready = sem("st_ready"), sem("rs_ready"), sem("v_ready"), sem("hst_ready")
        xb_ready, ct_ready, bt_ready, sz_ready = sem("xb_ready"), sem("ct_ready"), sem("bt_ready"), sem("sz_ready")
        na_ready, e_ready, w1_ready, ln_ready = sem("na_ready"), sem("e_ready"), sem("w1_ready"), sem("ln_ready")
        dt_ready, a_ready, da_ready = sem("dt_ready"), sem("a_ready"), sem("da_ready")
        parts_ready, pt_ready, pwd_ready = sem("parts_ready"), sem("pt_ready"), sem("pwd_ready")
        gelu_ready, scan_done, m_ready = sem("gelu_ready"), sem("scan_done"), sem("m_ready")
        xdt_ready, xw_ready, s_reset = sem("xdt_ready"), sem("xw_ready"), sem("s_reset")
        t1_done, t2_done, s_scaled, s_ready = sem("t1_done"), sem("t2_done"), sem("s_scaled"), sem("s_ready")
        yg_ready, ssq_ready, rr_ready = sem("yg_ready"), sem("ssq_ready"), sem("rr_ready")
        ygn_ready, ynt_ready, o_used, st3_ready, r3_ready = (
            sem("ygn_ready"), sem("ynt_ready"), sem("o_used"), sem("st3_ready"), sem("r3_ready"))
        st4_ready, r4_ready, xf_ready, xft_done, xft_ready = (
            sem("st4_ready"), sem("r4_ready"), sem("xf_ready"), sem("xft_done"), sem("xft_ready"))
        h12_done, silu_ready, he_ready, het_done, het_ready = (
            sem("h12_done"), sem("silu_ready"), sem("he_ready"), sem("het_done"), sem("het_ready"))
        w3_done, lg_ready, ex_ready = sem("w3_done"), sem("lg_ready"), sem("ex_ready")
        st5_ready, r5_ready, out_ready = sem("st5_ready"), sem("r5_ready"), sem("out_ready")

        x_d = x.rearrange("(t p) d -> p t d", p=P)
        out_d = out.rearrange("(t p) d -> p t d", p=P)
        NS = 2 * NX
        ORDER = [NE, NE + 1] + list(range(NE))

        def col12(m):
            return 0 if m == 0 else 2 * EI + NE + (m - 1) * 2 * EI

        block = ctx.enter_context(nc.Block())

        @block.sync
        def _(sp):
            sp.dma_start(cs[:], cst).then_inc(s_cs, 16)
            sp.dma_start(xa[:, 0:CH, :], x_d[:, 0:CH, :]).then_inc(s_x, 16)
            sp.wait_ge(s_x, 16)
            with sp.Fori(1, NB) as i:
                sp.dma_start(xa[:, bass.ts(i, CH), :], x_d[:, bass.ts(i, CH), :]).then_inc(s_x, 16)
                sp.wait_ge(s_x, i * 16 + 16)
                sp.sem_inc(sp_carry, 1)
            sp.dma_start(xa[:, NT:NT + CH, :], x_d[:, 0:CH, :]).then_inc(s_x, 16)
            sp.wait_ge(o_done, NB * CH)
            sp.dma_start(w3_s, w3.rearrange("(k p) n -> p k n", p=EK)).then_inc(s_w3, 16)
            with sp.Fori(0, NT // 2) as j:
                sp.wait_ge(out_ready, j * 2 + 2)
                sp.sem_inc(sp_carry, 1)
                sp.dma_start(out_d[:, bass.ts(j, 2), :], xa[:, bass.ts(j, 2), :]).then_inc(s_out, 16)
            sp.wait_ge(s_out, 16 * (NT // 2))

        @block.tensor
        def _(pe):
            def x_to_v(k, bk):
                for c in range(CH):
                    mm = pe.transpose(bk[:, c * P:(c + 1) * P], v[:, c, k * P:(k + 1) * P], ident)
                mm.then_inc(vt_done, 1)

            def scores(i, c, g):
                n = 2 * c + g
                w = W[n % 2 + 1]
                if n >= 2:
                    pe.wait_ge(m_ready, i * 8 + n - 1)
                mm = pe.matmul(w[:, :], bT[g * HD:(g + 1) * HD, c * P:(c + 1) * P],
                               cT[g * HD:(g + 1) * HD, :, c * P:(c + 1) * P], start=True, stop=True)
                mm.then_inc(g_done, 1)

            def yT(i, c):
                pe.wait_ge(ygn_ready, i * 4 + c + 1)
                bk = X[0] if c < 3 else X[1]
                if c == 3:
                    pe.wait_ge(hst_ready, i * 2 + 3)
                for k in range(DI // P):
                    mm = pe.transpose(bk[:, k * P:(k + 1) * P], ygn[:, k * P:(k + 1) * P], ident)
                mm.then_inc(yt_done, 1)

            def out_proj(i, c):
                pe.wait_ge(ynt_ready, i * 4 + c + 1)
                for k in range(DI // P):
                    mm = pe.matmul(O[:, 0:DM], ynT[:, k, :], wout_s[:, k, :], start=False, stop=(k == DI // P - 1))
                mm.then_inc(o_done, 1)

            pe.wait_ge(s_cs, 16)
            pe.wait_ge(v_ready, CH)
            x_to_v(0, X[1])
            x_to_v(1, X[0])
            pe.wait_ge(s_win, 16)
            pe.wait_ge(consts_ready, 1)
            with pe.Fori(0, NB) as i:
                pe.wait_ge(hst_ready, i * 2 + 2)
                for c in range(CH):
                    if c >= 2:
                        pe.wait_ge(xb_ready, i * 4 + c - 1)
                    for k in range(KD):
                        mm = pe.matmul(X[c % 2][:, 0:XBD], hsT[:, k, c * P:(c + 1) * P],
                                       win_s[:, k, DI:DI + XBD], start=(k == 0), stop=(k == KD - 1))
                    mm.then_inc(xb_done, 1)
                for j in range(JH):
                    if j >= 3:
                        pe.wait_ge(ct_ready, i * 4 + j - 2)
                    for k in range(KD):
                        mm = pe.matmul(W[j % 3][:, :], win_s[:, k, DI + XBD + j * P:DI + XBD + (j + 1) * P],
                                       hsT[:, k, :], start=(k == 0), stop=(k == KD - 1))
                    mm.then_inc(ct_done, 1)
                pe.wait_ge(xb_ready, i * 4 + 4)
                for c in range(CH):
                    mm = pe.transpose(X[0][:, c * P:(c + 1) * P], xbd[:, c, XB:2 * XB], ident)
                mm.then_inc(bt_done, 1)
                for c in range(CH):
                    pe.wait_ge(ct_ready, i * 4 + min(c + 2, 4))
                    if c == 3:
                        pe.wait_ge(sz_ready, i * 4 + 1)
                    for k in range(KD):
                        mm = pe.matmul(W[(c + 1) % 3][:, :], hsT[:, k, c * P:(c + 1) * P], win_s[:, k, 0:DI],
                                       start=(k == 0), stop=(k == KD - 1))
                    mm.then_inc(z_done, 1)
                    if c == 1:
                        pe.wait_ge(parts_ready, i + 1)
                        ptb = X[1][:, :].bitcast(BF16)
                        for q in range(CH):
                            mm = pe.transpose(ptb[0:3 * NH, q * P:(q + 1) * P], parts[:, q, :, :].rearrange("p a h -> p (a h)"), ident_b[:])
                        mm.then_inc(pt_done, 1)
                        pe.wait_ge(bt_ready, i + 1)
                        for q, col in enumerate((C_INCL, C_AFTER, C_ONES)):
                            mm = pe.matmul(X[0][:, q * 32:(q + 1) * 32], cs[:, col:col + P], dtw[:, 12, :, :],
                                           start=True, stop=True)
                        mm.then_inc(cum_done, 1)
                pe.wait_ge(s_fc1, 16)
                for f in range(KF):
                    if f < 3:
                        pe.wait_ge(sz_ready, i * 4 + f + 2)
                    else:
                        pe.wait_ge(gelu_ready, i * 8 + f - 2)
                    for k in range(KD):
                        mm = pe.matmul(W[(f + 2) % 3][:, :], fc1_s[:, k, f * P:(f + 1) * P], hsT[:, k, :],
                                       start=(k == 0), stop=(k == KD - 1))
                    mm.then_inc(fc1_done, 1)
                    if f == 0:
                        pe.wait_ge(pt_ready, i + 1)
                    if f == 1:
                        pe.wait_ge(pwd_ready, i * 3 + 3)
                    if f >= 2:
                        pe.wait_ge(scan_done, i * 8 + f - 1)
                    pe.matmul(X[(f + 1) % 2][:, :], sel_b[:, f, :], partsT[:, :, :].rearrange("p c t -> p (c t)"),
                              start=True, stop=True).then_inc(bc_done, 1)
                pe.wait_ge(s_fc2, 16)
                pe.wait_ge(s_wout, 16)
                pe.wait_ge(gelu_ready, i * 8 + 8)
                scores(i, 0, 0)
                scores(i, 0, 1)
                for c in range(CH):
                    if c == 0:
                        pe.wait_ge(s_reset, i + 1)
                    else:
                        pe.wait_ge(s_ready, i * 8 + 2 * c)
                        pe.wait_ge(t1_done, i * 4 + c)
                    for j in range(JH):
                        mm = pe.matmul(I[:, j * P:(j + 1) * P], cT[:, j, c * P:(c + 1) * P], S[:, j, :],
                                       start=True, stop=True)
                    mm.then_inc(inter_done, 1)
                    pe.wait_ge(xw_ready, i * 4 + c + 1)
                    if c == 0:
                        pe.wait_ge(scan_done, i * 8 + 8)
                    for g in range(NG):
                        mm = pe.matmul(X[1][g * HD:(g + 1) * HD, 0:JH * HD],
                                       xbd[:, c, XB + g * HD:XB + (g + 1) * HD],
                                       xw[:, c % 2, g * JH * HD:(g + 1) * JH * HD], start=True, stop=True)
                    mm.then_inc(inc_done, 1)
                    if c > 0:
                        yT(i, c - 1)
                    pe.wait_ge(m_ready, i * 8 + 2 * c + 2)
                    if c > 0:
                        pe.wait_ge(t2_done, i * 4 + c)
                    for h, at in ((0, 0), (1, 1), (2, 2), (3, 3), (7, 6), (6, 5), (5, 4), (4, None)):
                        lo, n = (h, 1) if at is None else (at, 2)
                        mm = pe.matmul(Y[:, lo * HD:(lo + n) * HD], M[:, c % 2, h, :],
                                       xdt[:, c % 2, lo * HD:(lo + n) * HD], start=True, stop=True)
                    mm.then_inc(y_done, 1)
                    if c > 0:
                        out_proj(i, c - 1)
                    if c < CH - 1:
                        scores(i, c + 1, 0)
                        scores(i, c + 1, 1)
                    if c > 0:
                        pe.wait_ge(o_used, i * 4 + c)
                    for k in range(KF):
                        mm = pe.matmul(O[:, 0:DM], gT[:, k, c * P:(c + 1) * P], fc2_s[:, k, :],
                                       start=(k == 0), stop=False)
                pe.wait_ge(v_ready, i * 4 + 8)
                pe.wait_ge(s_ready, i * 8 + 8)
                x_to_v(0, X[1])
                pe.wait_ge(ynt_ready, i * 4 + 3)
                x_to_v(1, X[0])
                yT(i, 3)
                out_proj(i, 3)

            def turn_xf(n, q):
                pe.wait_ge(xf_ready, n)
                for k in range(KD):
                    mm = pe.transpose(I[:, k * P:(k + 1) * P], xf[:, k * P:(k + 1) * P], ident)
                mm.then_inc(xft_done, 1)

            turn_xf(1, 0)
            pe.wait_ge(o_used, NB * 4)
            pe.wait_ge(s_w12, 16)
            pe.wait_ge(s_w3, 16)
            with pe.Fori(0, NT // 2) as j:
                def first(n):
                    q, m = divmod(n, NX)
                    if m == 0:
                        pe.wait_ge(xft_ready, j * 2 + q + 1)
                    if n >= 2:
                        pe.wait_ge(he_ready, j * NS + n - 1)
                    w = 2 * EI + (NE if m == 0 else 0)
                    for k in range(KD):
                        mm = pe.matmul(W[n % 2][:, 0:w], xfT[:, q, k, :], w12_s[:, k, col12(m):col12(m) + w],
                                       start=(k == 0), stop=(k == KD - 1))
                    mm.then_inc(h12_done, 1)

                def turn(n):
                    pe.wait_ge(he_ready, j * NS + n + 1)
                    if n >= 2:
                        pe.wait_ge(het_ready, j * NS + n - 1)
                    for k in range(2):
                        mm = pe.transpose(X[n % 2][0:EK, k * P:(k + 1) * P], he[:, n % 2, k * EK:(k + 1) * EK], ident)
                    mm.then_inc(het_done, 1)

                def second(n):
                    q, m = divmod(n, NX)
                    pe.wait_ge(het_ready, j * NS + n + 1)
                    for k in range(2):
                        mm = pe.matmul((Y, O)[q][:, 0:DM], heT[:, n % 2, k, :], w3_s[:, 2 * ORDER[m] + k, :],
                                       start=(m == 0 and k == 0), stop=(m == NX - 1 and k == 1))
                    mm.then_inc(w3_done, 1)

                for n in range(NS + 2):
                    if n < NS:
                        first(n)
                    if 1 <= n <= NS:
                        turn(n - 1)
                    if n >= 2:
                        second(n - 2)
                    if n % NX == 6 and n < NS:
                        turn_xf(j * 2 + n // NX + 2, (n // NX + 1) % 2)

        @block.vector
        def _(dve):
            ch = Chain(dve, dve_step, 33)

            def norm(i, n):
                dve.wait_ge(s_x, n * 16 + 16)
                for c in range(CH):
                    dve.bn_stats(st1[:, c, :], xa[:, n * CH + c, :]).then_inc(dve_st, 1)
                dve.wait_ge(dve_st, n * 4 + 4)
                dve.sem_inc(dve_carry, 1)
                for c in range(CH):
                    dve.bn_aggr(mvb[:, c, :], st1[:, c, :]).then_inc(st_ready, 1)
                dve.wait_ge(st_ready, n * 4 + 4)
                dve.tensor_copy(mv1[:, bass.ts(n, CH), :], mvb[:]).then_inc(mv_ready, 1)

            def norm_out(n):
                dve.wait_ge(mv_ready, n + 1)
                dve.wait_ge(rs_ready, n + 1)
                for c in range(CH):
                    dve.tensor_scalar(v[:, c, :], xa[:, n * CH + c, :], mv1[:, n * CH + c, 0:1], nw[:, 5, c:c + 1],
                                      ALU.subtract, ALU.mult).then_inc(v_ready, 1)

            norm(0, 0)
            dve.wait_ge(s_cs, 16)
            dve.wait_ge(s_sel, 16)
            dve.tensor_copy(sel_b[:, :, :].rearrange("p h m -> p (h m)"), sel_f).then_inc(dve_init, 1)
            dve.tensor_copy(ident_b[:], ident).then_inc(dve_init, 1)
            for c in range(CH):
                dve.tensor_copy(ident4[:, c, :], ident).then_inc(dve_init, 1)
            dve.memset(S[:], 0.0).then_inc(dve_init, 1)
            dve.memset(partsT[:, :, 0:1], 0.0).then_inc(dve_init, 1)
            dve.wait_ge(aneg_ready, 1)
            dve.tensor_scalar(a_neg[:], a_neg[:], -1.0, None, ALU.mult).then_inc(dve_init, 1)
            dve.tensor_scalar(keep[:], cs[:, C_KEEP:C_KEEP + NB], -1.0, None, ALU.mult).then_inc(dve_init, 1)
            dve.wait_ge(dve_init, 10)
            dve.memset(gs[:, 3:4], 0.0).then_inc(consts_ready, 1)
            norm_out(0)

            with dve.Fori(0, NB) as i:
                ch.start(i * ch.per)
                for c in range(CH):
                    dve.wait_ge(xb_done, i * 4 + c + 1)
                    dve.tensor_copy(xbd[:, c, :], X[c % 2][:, 0:XBD]).then_inc(xb_ready, 1)
                dve.wait_ge(xb_ready, i * 4 + 4)
                D = [dtw[:, q, :, :] for q in range(14)]
                ch.link(dve.tensor_tensor(D[0], xbd[:, :, 2 * XB:XBD],
                                          rw[:, R_DTB:R_DTB + NH].unsqueeze(1).broadcast_to([P, CH, NH]), ALU.add))
                dve.scalar_tensor_tensor(D[1], D[0], -1.0, D[0], ALU.mult, ALU.min).then_inc(na_ready, 1)
                dve.wait_ge(e_ready, i + 1)
                dve.tensor_scalar(D[3], D[2], 1.0, None, ALU.add).then_inc(w1_ready, 1)
                dve.wait_ge(w1_ready, i + 1)
                ch.link(dve.tensor_scalar(D[4], D[3], -1.0, None, ALU.add))
                ch.link(dve.tensor_scalar(D[5], D[4], 0.0, None, ALU.is_equal))
                ch.link(dve.tensor_tensor(D[6], D[4], D[5], ALU.add))
                ch.link(dve.reciprocal(D[7], D[6]))
                ch.link(dve.tensor_tensor(D[8], D[2], D[7], ALU.mult))
                dve.wait_ge(ln_ready, i + 1)
                ch.link(dve.tensor_tensor(D[9], D[13], D[5], ALU.add))
                ch.link(dve.tensor_tensor(D[10], D[8], D[9], ALU.mult))
                dve.scalar_tensor_tensor(D[11], D[0], 0.0, D[10], ALU.max, ALU.add).then_inc(dt_ready, 1)
                dve.wait_ge(dt_ready, i + 1)
                ch.link(dve.tensor_tensor(D[9], D[11], a_neg[:].unsqueeze(1).broadcast_to([P, CH, NH]), ALU.mult))
                dve.tensor_scalar(D[12], D[9], A_MIN, None, ALU.max).then_inc(a_ready, 1)
                for j in range(JH):
                    dve.wait_ge(ct_done, i * 4 + j + 1)
                    dve.tensor_copy(cT[:, j, :], W[j % 3][:, :]).then_inc(ct_ready, 1)
                dve.wait_ge(da_ready, i + 1)
                ch.link(dve.tensor_copy(parts[:, :, 0, :], D[4]))
                ch.link(dve.tensor_tensor(D[6], D[4], parts[:, :, 0, :], ALU.subtract))
                ch.link(dve.tensor_copy(parts[:, :, 1, :], D[6]))
                ch.link(dve.tensor_tensor(D[7], D[6], parts[:, :, 1, :], ALU.subtract))
                dve.tensor_copy(parts[:, :, 2, :], D[7]).then_inc(parts_ready, 1)
                dve.wait_ge(pt_done, i + 1)
                ptv = X[1][:, :].bitcast(BF16)[0:3 * NH, 0:TB].rearrange("p (c t) -> p c t", c=CH)
                dve.tensor_copy(partsT[:, :, 1:P], ptv[:, :, 1:P]).then_inc(pt_ready, 1)
                norm(i, i + 1)
                for h in range(NH):
                    dve.wait_ge(bc_done, i * 8 + h + 1)
                    dve.tensor_tensor_scan(L[:, h, :], X[(h + 1) % 2][:, :], ident4[:, :, :].rearrange("p c t -> p (c t)"),
                                           0.0, ALU.mult, ALU.add).then_inc(scan_done, 1)
                norm_out(i + 1)
                dve.tensor_tensor(S[:].bitcast(I32).rearrange("p j m -> p (j m)"), S[:].bitcast(I32).rearrange("p j m -> p (j m)"),
                                  keep[:, bass.ds(i, 1)].broadcast_to([P, JH * P]),
                                  ALU.bitwise_and).then_inc(s_reset, 1)

                def mask(c, g):
                    dve.wait_ge(g_done, i * 8 + 2 * c + g + 1)
                    if c == 0 and g == 0:
                        dve.wait_ge(scan_done, i * 8 + 8)
                    if c >= 2:
                        dve.wait_ge(y_done, i * 4 + c - 1)
                    dve.tensor_tensor(M[:, c % 2, g * JH:(g + 1) * JH, :],
                                      W[(2 * c + g) % 2 + 1][:, :].rearrange("p (h t) -> p h t", h=JH),
                                      L[:, g * JH:(g + 1) * JH, c * P:(c + 1) * P], ALU.mult).then_inc(m_ready, 1)

                def finish_a(c):
                    t = i * CH + c
                    ch.link(dve.tensor_scalar(ub[:], xa[:, t, :], mv1[:, t, 0:1], rs1[:, bass.ds(t, 1)],
                                              ALU.subtract, ALU.mult))
                    ch.link(dve.tensor_tensor(ub[:], ub[:], rw[:, R_FB:R_FB + DM], ALU.add))
                    dve.wait_ge(o_done, i * 4 + c + 1)
                    dve.tensor_tensor(o[:], O[:, 0:DM], ub[:], ALU.add).then_inc(o_used, 1)
                    dve.wait_ge(o_used, i * 4 + c + 1)
                    ch.link(dve.bn_stats(st3[:], o[:]), dve_carry)
                    dve.bn_aggr(mv3[:], st3[:]).then_inc(st3_ready, 1)

                def finish_b(c):
                    t = i * CH + c
                    dve.wait_ge(r3_ready, i * 4 + c + 1)
                    ch.link(dve.tensor_scalar(ub[:], o[:], mv3[:, 0:1], r3[:, 1:2], ALU.subtract, ALU.mult))
                    ch.link(dve.tensor_tensor(xa[:, t, :], xa[:, t, :], ub[:], ALU.add))

                mask(0, 0)
                mask(0, 1)
                for c in range(CH):
                    dve.wait_ge(inter_done, i * 4 + c + 1)
                    dve.wait_ge(pwd_ready, i * 3 + 3)
                    if c > 0:
                        dve.wait_ge(t2_done, i * 4 + c)
                    dve.tensor_tensor(
                        t1[:].rearrange("p (g j d) -> p g j d", g=NG, j=JH),
                        I[:, :].rearrange("p (j g d) -> p g j d", g=NG, j=JH),
                        pwd[:, 0, c, :].rearrange("p (g j) -> p g j", g=NG).unsqueeze(3).broadcast_to([P, NG, JH, HD]),
                        ALU.mult).then_inc(t1_done, 1)
                    dve.wait_ge(inc_done, i * 4 + c + 1)
                    dve.wait_ge(s_scaled, i * 4 + c + 1)
                    for g in range(NG):
                        q = slice(g * HD, (g + 1) * HD)
                        dve.tensor_tensor(S[q, :, g * HD:(g + 1) * HD], S[q, :, g * HD:(g + 1) * HD],
                                          X[1][q, 0:JH * HD].rearrange("p (j d) -> p j d", j=JH),
                                          ALU.add).then_inc(s_ready, 1)
                    dve.wait_ge(y_done, i * 4 + c + 1)
                    dve.wait_ge(t1_done, i * 4 + c + 1)
                    if c > 0:
                        dve.wait_ge(yg_ready, i * 4 + c)
                    dve.tensor_tensor(t2[:], t1[:], Y[:, :], ALU.add).then_inc(t2_done, 1)
                    if c > 0:
                        finish_a(c - 1)
                    if c < CH - 1:
                        mask(c + 1, 0)
                        mask(c + 1, 1)
                    if c > 0:
                        finish_b(c - 1)
                finish_a(CH - 1)
                finish_b(CH - 1)
                ch.n -= 0
                ch.end()

            c2 = Chain(dve, dve_step2, 2 * (1 + 8 + 2))
            c2.start(0)

            def prep_a(t, n):
                dve.bn_stats(st4[:], xa[:, t, :]).then_inc(st4_s, 1)
                dve.wait_ge(st4_s, n)
                dve.sem_inc(dve_carry, 1)
                dve.bn_aggr(mv4[:], st4[:]).then_inc(st4_ready, 1)

            def prep_b(t, n):
                dve.wait_ge(r4_ready, n)
                dve.tensor_scalar(xf[:], xa[:, t, :], mv4[:, 0:1], r4[:, 1:2], ALU.subtract, ALU.mult).then_inc(xf_ready, 1)

            prep_a(0, 1)
            prep_b(0, 1)
            with dve.Fori(0, NT // 2) as j:
                c2.start(j * c2.per)

                def gate(n):
                    q, m = divmod(n, NX)
                    dve.wait_ge(silu_ready, j * NS + n + 1)
                    if n >= 2:
                        dve.wait_ge(het_done, j * NS + n - 1)
                    wgt = 1.0 if m < 2 else comb[:, q, m - 2:m - 1]
                    dve.scalar_tensor_tensor(he[:, n % 2, :], hs_[:, n % 2, :], wgt, W[n % 2][:, EI:2 * EI],
                                             ALU.mult, ALU.mult).then_inc(he_ready, 1)

                def route_a(q):
                    dve.wait_ge(silu_ready, j * NS + q * NX + 1)
                    lg = W[(q * NX) % 2][:, 2 * EI:2 * EI + NE]
                    c2.link(dve.tensor_reduce(gs[:, 0:1], lg, AX_X, ALU.max))
                    dve.tensor_scalar(gw[:, 0, :], lg, gs[:, 0:1], None, ALU.subtract).then_inc(lg_ready, 1)

                def route_b(q):
                    dve.wait_ge(ex_ready, j * 2 + q + 1)
                    c2.link(dve.reciprocal(gs[:, 2:3], gs[:, 1:2]))
                    pr = gw[:, 2, :]
                    c2.link(dve.tensor_scalar(pr, gw[:, 1, :], gs[:, 2:3], None, ALU.mult))
                    other = pr.unsqueeze(1).broadcast_to([P, NE, NE])
                    own = pr.unsqueeze(2).broadcast_to([P, NE, NE])
                    c2.link(dve.tensor_tensor(cmp_[:, 0], other, own, ALU.is_gt))
                    c2.link(dve.tensor_tensor(cmp_[:, 1], other, own, ALU.is_equal))
                    c2.link(dve.tensor_tensor(cmp_[:, 1], cmp_[:, 1],
                                              cs[:, C_LOWER:C_LOWER + NE * NE].rearrange("p (a b) -> p a b", a=NE), ALU.mult))
                    c2.link(dve.tensor_tensor(cmp_[:, 2], cmp_[:, 0], cmp_[:, 1], ALU.add))
                    c2.link(dve.tensor_reduce(gw[:, 3, :], cmp_[:, 2], AX_X, ALU.add))
                    c2.link(dve.scalar_tensor_tensor(comb[:, q, :], gw[:, 3, :], 2.0, pr, ALU.is_lt, ALU.mult))

                def finish(q):
                    t = j * 2 + q
                    bk = (Y, O)[q]
                    dve.wait_ge(w3_done, j * NS + (q + 1) * NX)
                    c2.link(dve.bn_stats(st5[:], bk[:, 0:DM]), dve_carry)
                    dve.bn_aggr(mv5[:], st5[:]).then_inc(st5_ready, 1)
                    dve.wait_ge(r5_ready, j * 2 + q + 1)
                    c2.link(dve.tensor_scalar(d5[:], bk[:, 0:DM], mv5[:, 0:1], r5[:, 1:2], ALU.subtract, ALU.mult))
                    dve.tensor_tensor(xa[:, t, :], xa[:, t, :], d5[:], ALU.add).then_inc(out_ready, 1)

                for n in range(NS):
                    q, m = divmod(n, NX)
                    if m == 0:
                        route_a(q)
                    gate(n)
                    if m == 1:
                        route_b(q)
                    if q == 1 and m == 2:
                        finish(0)
                    if m == 4:
                        prep_a(j * 2 + q + 1, j * 2 + q + 2)
                    if m == 5:
                        prep_b(j * 2 + q + 1, j * 2 + q + 2)
                finish(1)
                c2.end()

        @block.scalar
        def _(act):
            act.dma_start(win_s[:], w_in.rearrange("(k p) n -> p k n", p=P)).then_inc(s_win, 16)
            act.dma_start(rw[:], rows.broadcast_to([P, NC_R])).then_inc(s_rw, 16)
            act.dma_start(sel_f, sel).then_inc(s_sel, 16)
            act.dma_start(fc1_s, fc1.rearrange("(k p) n -> p k n", p=P)).then_inc(s_fc1, 16)
            act.dma_start(fc2_s, fc2.rearrange("(k p) n -> p k n", p=P)).then_inc(s_fc2, 16)
            act.dma_start(wout_s, w_out.rearrange("(k p) n -> p k n", p=P)).then_inc(s_wout, 16)
            act.dma_start(w12_s[:], w12.rearrange("(k p) n -> p k n", p=P)).then_inc(s_w12, 16)
            act.wait_ge(s_rw, 16)
            act.activation(a_neg[:], rw[:, R_ALOG:R_ALOG + NH], ACT.Exp).then_inc(aneg_ready, 1)
            act.wait_ge(s_cs, 16)

            def take_hs(n, k):
                act.wait_ge(vt_done, n * 2 + k + 1)
                act.activation(hsT[:, k, :], X[1 - k][:, :], ACT.Identity, bias=lnb[:, k:k + 1],
                               scale=lnw[:, k:k + 1]).then_inc(hst_ready, 1)

            take_hs(0, 0)
            take_hs(0, 1)
            with act.Fori(0, NB) as i:
                act.wait_ge(na_ready, i + 1)
                act.activation(dtw[:, 2, :, :], dtw[:, 1, :, :], ACT.Exp).then_inc(e_ready, 1)
                act.wait_ge(w1_ready, i + 1)
                act.activation(dtw[:, 13, :, :], dtw[:, 3, :, :], ACT.Ln).then_inc(ln_ready, 1)
                act.wait_ge(a_ready, i + 1)
                act.activation(dtw[:, 4, :, :], dtw[:, 12, :, :], ACT.Exp).then_inc(da_ready, 1)
                act.wait_ge(bt_done, i + 1)
                act.activation(bT[:], X[0][:, :], ACT.Copy).then_inc(bt_ready, 1)
                for c in range(CH):
                    act.wait_ge(z_done, i * 4 + c + 1)
                    act.activation(sz[:, c, :], W[(c + 1) % 3][:, :], ACT.Silu).then_inc(sz_ready, 1)
                act.wait_ge(cum_done, i + 1)
                act.activation(pwd[:].rearrange("p a c h -> p (a c h)"), X[0][:, 0:2 * CH * NH], ACT.Exp).then_inc(pwd_ready, 1)
                for g in range(NG):
                    q = slice(g * HD, (g + 1) * HD)
                    act.activation(dec[q, :, :], X[0][q, 2 * CH * NH:3 * CH * NH].rearrange("p (c g j) -> p g c j", c=CH, g=NG)[:, g],
                                   ACT.Exp).then_inc(pwd_ready, 1)
                for f in range(KF):
                    act.wait_ge(fc1_done, i * 8 + f + 1)
                    act.activation(gT[:, f, :], W[(f + 2) % 3][:, :], ACT.Gelu_apprx_tanh,
                                   bias=f1b[:, f:f + 1]).then_inc(gelu_ready, 1)

                def take_y(c):
                    act.wait_ge(yt_done, i * 4 + c + 1)
                    bk = X[0] if c < 3 else X[1]
                    for k in range(DI // P):
                        ins = act.activation(ynT[:, k, :], bk[:, k * P:(k + 1) * P], ACT.Copy, scale=nrw[:, k:k + 1])
                    ins.then_inc(ynt_ready, 1)

                for c in range(CH):
                    if c > 0:
                        take_y(c - 1)
                    act.wait_ge(yg_ready, i * 4 + c + 1)
                    act.activation(ygn[:], yg[:], ACT.Square, accum_out=rr[:, 0:1]).then_inc(ssq_ready, 1)
                    if c == CH - 1:
                        take_hs(i + 1, 0)
                        take_hs(i + 1, 1)
                    act.wait_ge(rr_ready, i * 4 + c + 1)
                    act.activation(ygn[:], yg[:], ACT.Copy, scale=rr[:, 3:4]).then_inc(ygn_ready, 1)
                take_y(CH - 1)

            def take_xf(n, q):
                act.wait_ge(xft_done, n)
                act.activation(xfT[:, q].rearrange("p k t -> p (k t)"), I[:, 0:DM], ACT.Copy).then_inc(xft_ready, 1)

            take_xf(1, 0)
            with act.Fori(0, NT // 2) as j:
                def take_h(n):
                    act.wait_ge(het_done, j * NS + n + 1)
                    if n >= 2:
                        act.wait_ge(w3_done, j * NS + n - 1)
                    act.activation(heT[:, n % 2].rearrange("p k t -> p (k t)"), X[n % 2][0:EK, 0:2 * P],
                                   ACT.Copy).then_inc(het_ready, 1)

                for n in range(NS + 1):
                    if n < NS:
                        act.wait_ge(h12_done, j * NS + n + 1)
                        if n >= 2:
                            act.wait_ge(he_ready, j * NS + n - 1)
                        act.activation(hs_[:, n % 2, :], W[n % 2][:, 0:EI], ACT.Silu).then_inc(silu_ready, 1)
                        if n % NX == 0:
                            act.wait_ge(lg_ready, j * 2 + n // NX + 1)
                            act.activation(gw[:, 1, :], gw[:, 0, :], ACT.Exp, accum_out=gs[:, 1:2]).then_inc(ex_ready, 1)
                    if n >= 1:
                        take_h(n - 1)
                    if n % NX == 7:
                        take_xf(j * 2 + n // NX + 2, (n // NX + 1) % 2)

        @block.gpsimd
        def _(pool):
            pc = Chain(pool, pool_step, CH * 3)
            pool.memset(nhalf[:], -0.5).then_inc(pool_init, 1)
            pool.wait_ge(pool_init, 1)

            def rsqrt(link, dst, tmp, var, width=1):
                link(pool.tensor_scalar(tmp, var, EPS, 1.0, ALU.add, ALU.mult))
                return pool.tensor_tensor(dst, tmp, nhalf[:, 0:width], ALU.pow)

            def norm_scales(n, link):
                pool.wait_ge(st_ready, n * 4 + 4)
                pool.sem_inc(pool_carry, 1)
                link(pool.tensor_copy(nw[:, 0, :], mvb[:, :, 1]), pool_carry)
                link(rsqrt(link, nw[:, 2, :], nw[:, 1, :], nw[:, 0, :], CH))
                link(pool.tensor_tensor(nw[:, 3, :], nw[:, 2, :], nw[:, 2, :], ALU.mult))
                link(pool.tensor_tensor(nw[:, 3, :], nw[:, 3, :], nw[:, 0, :], ALU.mult), pool_carry)
                pool.tensor_copy(rs1[:, bass.ts(n, CH)], nw[:, 2, :]).then_inc(rs1_ready, 1)
                link(rsqrt(link, nw[:, 4, :], nw[:, 1, :], nw[:, 3, :], CH))
                pool.wait_ge(rs1_ready, n + 1)
                pool.tensor_tensor(nw[:, 5, :], nw[:, 4, :], nw[:, 2, :], ALU.mult).then_inc(rs_ready, 1)

            PN = 7
            pn = Chain(pool, pool_norm, PN)
            norm_scales(0, pn.link)
            pool.wait_ge(s_rw, 16)
            with pool.Fori(0, NB) as i:
                pc.start(i * pc.per)
                pn.start(i * PN + PN)

                def heads(ap):
                    return ap.rearrange("p (g j d) -> p g j d", g=NG, j=JH)

                def bc(ap):
                    return ap.rearrange("p (g j) -> p g j", g=NG).unsqueeze(3).broadcast_to([P, NG, JH, HD])

                def steps(c):
                    xh = xbd[:, c, 0:XB].rearrange("p (g d) -> p g d", g=NG).unsqueeze(2).broadcast_to([P, NG, JH, HD])
                    pool.tensor_tensor(heads(xdt[:, c % 2, :]), xh, bc(dtw[:, 11, c, :]), ALU.mult).then_inc(xdt_ready, 1)
                    pool.wait_ge(pwd_ready, i * 3 + 3)
                    pool.wait_ge(xdt_ready, i * 4 + c + 1)
                    pool.tensor_tensor(heads(xw[:, c % 2, :]), heads(xdt[:, c % 2, :]), bc(pwd[:, 1, c, :]),
                                       ALU.mult).then_inc(xw_ready, 1)

                pool.wait_ge(dt_ready, i + 1)
                norm_scales(i + 1, pn.link)
                pn.end()
                steps(0)
                steps(1)

                def finish(c):
                    pool.wait_ge(st3_ready, i * 4 + c + 1)
                    pool.sem_inc(pool_carry, 1)
                    rsqrt(pc.link, r3[:, 1:2], r3[:, 0:1], mv3[:, 1:2]).then_inc(r3_ready, 1)

                for c in range(CH):
                    pool.wait_ge(inter_done, i * 4 + c + 1)
                    pool.tensor_tensor(S[:], S[:], dec[:, c, :].unsqueeze(2).broadcast_to([P, JH, P]),
                                       ALU.mult).then_inc(s_scaled, 1)
                    xh = xbd[:, c, 0:XB].rearrange("p (g d) -> p g d", g=NG).unsqueeze(2).broadcast_to([P, NG, JH, HD])
                    pool.tensor_tensor(heads(dx[:]), xh, bc(rw[:, R_D:R_D + NH]), ALU.mult).then_inc(dx_ready, 1)
                    pool.wait_ge(dx_ready, i * 4 + c + 1)
                    pool.wait_ge(t2_done, i * 4 + c + 1)
                    pc.link(pool.tensor_tensor(t3[:], t2[:], dx[:], ALU.add))
                    if c > 0:
                        pool.wait_ge(ygn_ready, i * 4 + c)
                    pool.wait_ge(sz_ready, i * 4 + 4)
                    pool.tensor_tensor(yg[:], t3[:], sz[:, c, :], ALU.mult).then_inc(yg_ready, 1)
                    if c < 2:
                        steps(c + 2)
                    if c > 0:
                        finish(c - 1)
                    pool.wait_ge(ssq_ready, i * 4 + c + 1)
                    pool.sem_inc(pool_carry, 1)
                    pc.link(pool.tensor_scalar(rr[:, 1:2], rr[:, 0:1], 1.0 / DI, EPS, ALU.mult, ALU.add))
                    pool.tensor_tensor(rr[:, 3:4], rr[:, 1:2], nhalf[:, 0:1], ALU.pow).then_inc(rr_ready, 1)
                finish(CH - 1)
                pc.end()

            p2 = Chain(pool, pool_step2, 2 * 2)

            def prep(n, link):
                pool.wait_ge(st4_ready, n)
                pool.sem_inc(pool_carry, 1)
                rsqrt(link, r4[:, 1:2], r4[:, 0:1], mv4[:, 1:2]).then_inc(r4_ready, 1)

            p2.start(0)
            prep(1, p2.link)
            with pool.Fori(0, NT // 2) as j:
                p2.start(j * p2.per + 1)

                def last(q):
                    pool.wait_ge(st5_ready, j * 2 + q + 1)
                    pool.sem_inc(pool_carry, 1)
                    rsqrt(p2.link, r5[:, 1:2], r5[:, 0:1], mv5[:, 1:2]).then_inc(r5_ready, 1)

                prep(j * 2 + 2, p2.link)
                last(0)
                prep(j * 2 + 3, p2.link)
                last(1)
                p2.end()


def kernel(**inputs):
    import concourse.bacc as _bacc
    from concourse.bass_utils import run_bass_kernel_spmd as _run

    a = {k: np.asarray(v) for k, v in inputs.items()}
    g = lambda n: a["L0_attn_" + n]
    f = lambda n: a["L0_ffn_" + n]
    xs = g("hidden_states")
    w_in = g("W_in")
    zc, xc, bcol, cc = DI, XB, XB, DI
    o1 = zc + xc + bcol
    c_cols = w_in[:, o1:o1 + cc].reshape(DM, NG, JH, HD).transpose(0, 2, 1, 3).reshape(DM, cc)
    w_in = np.concatenate([w_in[:, :o1], w_in[:, o1 + cc:], c_cols], 1)
    s1 = f("sw1").reshape(2, EI, DM)
    s2 = f("sw2").reshape(2, EI, DM)
    gates = [s1[0], s2[0], f("gate_w"), s1[1], s2[1]]
    for e in range(NE):
        gates += [f("w1")[e], f("w2")[e]]
    w12 = np.ascontiguousarray(np.concatenate(gates, 0).T)
    w3 = np.concatenate([f("w3").transpose(0, 2, 1).reshape(NE * EI, DM), f("sw3").T], 0)
    cols = np.concatenate([g("ln_w").reshape(KD, P).T, g("ln_b").reshape(KD, P).T,
                           g("norm_w").reshape(DI // P, P).T, g("fc1_b").reshape(KF, P).T], 1)
    r = np.arange(P)
    masks = np.concatenate([np.eye(P), r[:, None] <= r[None, :], r[:, None] > r[None, :], np.ones((P, P))], 1)
    e8 = np.arange(NE)
    lower = np.broadcast_to((e8[None, :] < e8[:, None]).reshape(1, NE * NE), (P, NE * NE))
    per_seq = xs.shape[1] // TB
    keep = np.where(np.arange(8) % per_seq == 0, 0, 1).astype(np.float32)
    cst = np.concatenate([masks.astype(np.float32), lower.astype(np.float32), cols,
                          np.broadcast_to(keep[None], (P, 8))], 1)
    rows = np.concatenate([g("dt_bias"), g("A_log"), g("D"), g("fc2_b")])[None]
    sel = np.zeros((3, NH, NH, P), np.float32)
    sel[:, e8, e8] = 1
    arrays = {"x": xs.reshape(-1, DM), "w_in": w_in, "w_out": g("W_out"), "fc1": g("fc1_w"), "fc2": g("fc2_w"),
              "w12": w12, "w3": w3, "cst": cst, "rows": rows, "sel": sel.reshape(3 * NH, NH * P)}
    arrays = {k: np.ascontiguousarray(v) for k, v in arrays.items()}
    nc = _bacc.Bacc("TRN2", target_bir_lowering=False, num_devices=1)
    args = [nc.dram_tensor(n, v.shape, mybir.dt.from_np(v.dtype), kind="ExternalInput").ap() for n, v in arrays.items()]
    out = nc.dram_tensor("out", arrays["x"].shape, F32, kind="ExternalOutput").ap()
    build(nc, *args, out)
    got = _run(nc, [arrays], core_ids=[0])
    return got.results[0]["out"].reshape(xs.shape)
```

```python
from contextlib import ExitStack

import numpy as np
import concourse.bass as bass
from concourse import mybir

F32 = mybir.dt.float32
BF16 = mybir.dt.bfloat16
I32 = mybir.dt.int32
U32 = mybir.dt.uint32
ALU = mybir.AluOpType
ACT = mybir.ActivationFunctionType
AX_X = mybir.AxisListType.X

P = 128
DM = 256
KD = DM // P
NH, HD, NG, JH = 8, 64, 2, 4
DI = NH * HD
XB = NG * HD
INTER = 1024
KF = INTER // P
CH = 4
TB = CH * P
NE, EI = 8, 176
NX = NE + 2
EK = EI // 2
EPS = 1e-5
XBD = 2 * XB + NH
A_MIN = -200.0
C_ID, C_INCL, C_AFTER, C_ONES, C_IOTA, C_FIRST, C_COLS, C_KEEP = 0, 128, 256, 384, 512, 640, 648, 664
NC_C = 672
R_DTB, R_ALOG, R_D, R_FB = 0, 8, 16, 24
NC_R = 24 + DM


class Chain:

    def __init__(self, eng, sem, per):
        self.eng, self.sem, self.per, self.base, self.n = eng, sem, per, 0, 0

    def start(self, base):
        self.base, self.n = base, 0

    def link(self, ins, carry=None):
        self.n += 1
        ins.then_inc(self.sem, 1)
        self.eng.wait_ge(self.sem, self.base + self.n)
        if carry is not None:
            self.eng.sem_inc(carry, 1)

    def mark(self, ins):
        self.n += 1
        ins.then_inc(self.sem, 1)

    def wait(self, carry=None):
        self.eng.wait_ge(self.sem, self.base + self.n)
        if carry is not None:
            self.eng.sem_inc(carry, 1)

    def end(self):
        assert self.n == self.per, self.n


def slot_tiles(tokens):
    most = (2 * tokens + NE * (P - 1)) // P
    return -(-most // 4) * 4


def build(nc, x, w_in, w_out, fc1, fc2, w12, w3, cst, rows, sel, out):
    NT = x.shape[0] // P
    NB = NT // CH
    W12N = w12.shape[1]
    HT = NT // 2
    SJ = slot_tiles(x.shape[0])
    SLOTS = (SJ + 4) * P
    xs_dram = nc.dram_tensor("slots_x", (SLOTS, DM), F32, kind="Internal").ap()
    eo_dram = nc.dram_tensor("slots_y", (SJ * P, DM), F32, kind="Internal").ap()

    with ExitStack() as ctx:
        def sb(name, shape, dt=F32):
            return ctx.enter_context(nc.sbuf_tensor(name, shape, dt))

        def bank(name):
            return ctx.enter_context(nc.psum_tensor(name, [P, 512], F32))

        def sem(name):
            return ctx.enter_context(nc.semaphore(name))

        xa = sb("xa", [P, NT + CH, DM])
        win_s = sb("win_s", [P, KD, 2 * DI + XBD])
        late = sb("late", [P, 2 * NX * DM])
        fc1_s = late[:, 0:KD * INTER].rearrange("p (k n) -> p k n", k=KD)
        fc2_s = late[:, KD * INTER:KD * INTER + KF * DM].rearrange("p (k n) -> p k n", k=KF)
        wout_s = late[:, KD * INTER + KF * DM:].rearrange("p (k n) -> p k n", k=DI // P)
        w3_s = late[0:EK, :].rearrange("p (k n) -> p k n", k=2 * NX)
        w12_s = sb("w12_s", [P, KD, W12N])
        cs = sb("cs", [P, NC_C])
        rw = sb("rw", [P, NC_R])
        sel_b = sb("sel_b", [3 * NH, NH, P], BF16)
        ident_b = sb("ident_b", [P, P], BF16)
        ident4 = sb("ident4", [P, CH, P])
        nhalf = sb("nhalf", [P, CH])
        keep = sb("keep", [P, NB], I32)
        a_neg = sb("a_neg", [P, NH])
        ident = cs[:, C_ID:C_ID + P]
        lnw, lnb = cs[:, C_COLS:C_COLS + 2], cs[:, C_COLS + 2:C_COLS + 4]
        nrw, f1b = cs[:, C_COLS + 4:C_COLS + 8], cs[:, C_COLS + 8:C_COLS + 16]

        st1 = sb("st1", [P, CH, 6])
        mvb = sb("mvb", [P, CH, 2])
        mv1 = sb("mv1", [P, NT + CH, 2])
        rs1 = sb("rs1", [P, NT + CH])
        nw = sb("nw", [P, 6, CH])
        v = sb("v", [P, CH, DM])
        hsT = sb("hsT", [P, KD, TB])
        xbd = sb("xbd", [P, CH, XBD])
        cT = sb("cT", [P, JH, TB])
        bT = sb("bT", [P, TB])
        sz = sb("sz", [P, CH, DI])
        mid = sb("mid", [P, 2 * KF * TB])
        gT = mid[:, 0:KF * TB].rearrange("p (f t) -> p f t", f=KF)
        sel_f = gT[0:3 * NH, 0:NH * P // TB, :].rearrange("p k t -> p (k t)")
        dtw = sb("dtw", [P, 14, CH, NH])
        parts = sb("parts", [P, CH, 3, NH], BF16)
        partsT = sb("partsT", [3 * NH, CH, P], BF16)
        pwd = sb("pwd", [P, 2, CH, NH])
        dec = sb("dec", [P, CH, JH])
        L = mid[:, KF * TB:].rearrange("p (h t) -> p h t", h=NH)
        xdt = sb("xdt", [P, 2, DI])
        xw = sb("xw", [P, 2, DI])
        dx = sb("dx", [P, DI])
        M = sb("M", [P, 2, NH, P])
        S = sb("S", [P, JH, P])
        t1 = sb("t1", [P, DI])
        t2 = sb("t2", [P, DI])
        t3 = sb("t3", [P, DI])
        yg = sb("yg", [P, DI])
        ygn = sb("ygn", [P, DI])
        rr = sb("rr", [P, 4])
        ynT = sb("ynT", [P, DI // P, P])
        ub = sb("ub", [P, DM])
        o = sb("o", [P, DM])
        st3 = sb("st3", [P, 6])
        mv3 = sb("mv3", [P, 2])
        r3 = sb("r3", [P, 2])
        mvf = sb("mvf", [P, NT + CH, 2])
        rsf = sb("rsf", [P, NT + CH])
        nmf = sb("nmf", [P, NT + CH])
        posb = sb("posb", [P, 4, 2, 2], I32)
        zero = sb("zero", [P, 1, DM])
        Mf = M[:].rearrange("p a h t -> p (a h t)")
        xfT = Mf[:, 0:DM].rearrange("p (k t) -> p k t", k=KD)
        xsT = Mf[:, DM:3 * DM].rearrange("p (a k t) -> p a k t", a=2, k=KD)
        heT = Mf[0:EK, 3 * DM:5 * DM].rearrange("p (a k t) -> p a k t", a=2, k=2)
        hs_ = Mf[:, 5 * DM:5 * DM + 2 * EI].rearrange("p (a n) -> p a n", a=2)
        he = Mf[:, 5 * DM + 2 * EI:5 * DM + 4 * EI].rearrange("p (a n) -> p a n", a=2)
        ysh = mid[:, 0:HT * DM].rearrange("p (t d) -> p t d", t=HT)
        xf = win_s[:].rearrange("p k n -> p (k n)")[:, 0:8 * DM].rearrange("p (b s d) -> p b s d", b=2, s=4)
        behind = mid[:, KF * TB:]
        xl = behind[:, 0:4 * DM].rearrange("p (s d) -> p s d", s=4)
        ob = behind[:, 4 * DM:8 * DM].rearrange("p (s d) -> p s d", s=4)
        acc = behind[:, 8 * DM:12 * DM].rearrange("p (u b d) -> p u b d", u=2, b=2)
        fT = [hsT, cT]
        RT = [sz[:].rearrange("p c d -> p (c d)")[:, q * NT * NE:(q + 1) * NT * NE] for q in range(8)]
        RC = [cT[:].rearrange("p c d -> p (c d)")[:, q * NT * NE:(q + 1) * NT * NE] for q in range(5)]
        gath = cT[:].rearrange("p c d -> p (c d)")[:, 0:8 * DM].rearrange("p (u b k d) -> p u b k d", u=2, b=2, k=2)
        grid = cT[:].rearrange("p c d -> p (c d)")[:, 5 * NT * NE:5 * NT * NE + SJ * NE]
        rsm = sb("rsm", [P, 4, NT])
        cw = sb("cw", [P, 2, NT])
        posf = sb("posf", [P, 2, NT])
        pos = sb("pos", [P, 2, NT], I32)
        tl = sb("tl", [P, 5, NE])
        eidf = sb("eidf", [P, SJ + 4])
        eid = sb("eid", [P, SJ + 4], I32)
        st4 = sb("st4", [P, 2, 6])
        mv5 = sb("mv5", [P, 2, 2, 2])
        r5 = sb("r5", [P, 2, 2, 2])

        W = [bank(f"W{k}") for k in range(3)]
        X = [bank(f"X{k}") for k in range(2)]
        Y, I, O = bank("Y"), bank("I"), bank("O")
        OB = [W[0], O]
        YO = [O, Y]

        s_x, s_cs, s_rw, s_sel, s_win = sem("s_x"), sem("s_cs"), sem("s_rw"), sem("s_sel"), sem("s_win")
        s_fc1, s_fc2, s_wout, s_w12, s_w3 = sem("s_fc1"), sem("s_fc2"), sem("s_wout"), sem("s_w12"), sem("s_w3")
        s_out = sem("s_out")
        dve_step, pool_step = sem("dve_step"), sem("pool_step")
        dve_step2, pool_step2 = sem("dve_step2"), sem("pool_step2")
        consts_ready, aneg_ready, dve_init, pool_init = sem("consts_ready"), sem("aneg_ready"), sem("dve_init"), sem("pool_init")
        mv_ready = sem("mv_ready")
        carry = sem("carry")
        dve_st, pool_norm, rs1_ready, dx_ready = sem("dve_st"), sem("pool_norm"), sem("rs1_ready"), sem("dx_ready")
        vt_done, xb_done, ct_done, bt_done = sem("vt_done"), sem("xb_done"), sem("ct_done"), sem("bt_done")
        z_done, pt_done, cum_done, fc1_done = sem("z_done"), sem("pt_done"), sem("cum_done"), sem("fc1_done")
        bc_done, g_done, inter_done, inc_done = sem("bc_done"), sem("g_done"), sem("inter_done"), sem("inc_done")
        y_done, yt_done, o_done = sem("y_done"), sem("yt_done"), sem("o_done")
        st_ready, rs_ready, v_ready, hst_ready = sem("st_ready"), sem("rs_ready"), sem("v_ready"), sem("hst_ready")
        xb_ready, ct_ready, bt_ready, sz_ready = sem("xb_ready"), sem("ct_ready"), sem("bt_ready"), sem("sz_ready")
        na_ready, e_ready, w1_ready, ln_ready = sem("na_ready"), sem("e_ready"), sem("w1_ready"), sem("ln_ready")
        dt_ready, a_ready, da_ready = sem("dt_ready"), sem("a_ready"), sem("da_ready")
        parts_ready, pt_ready, pwd_ready = sem("parts_ready"), sem("pt_ready"), sem("pwd_ready")
        gelu_ready, scan_done, m_ready = sem("gelu_ready"), sem("scan_done"), sem("m_ready")
        xdt_ready, xw_ready, s_reset = sem("xdt_ready"), sem("xw_ready"), sem("s_reset")
        t1_done, t2_done, s_scaled, s_ready = sem("t1_done"), sem("t2_done"), sem("s_scaled"), sem("s_ready")
        yg_ready, ssq_ready, rr_ready = sem("yg_ready"), sem("ssq_ready"), sem("rr_ready")
        ygn_ready, ynt_ready, o_used, st3_ready, r3_ready = (
            sem("ygn_ready"), sem("ynt_ready"), sem("o_used"), sem("st3_ready"), sem("r3_ready"))
        zf_ready, s_zero, vf_ready, lg_done, lg_ready = sem("zf_ready"), sem("s_zero"), sem("vf_ready"), sem("lg_done"), sem("lg_ready")
        ft_done, ft_ready, mx_ready, ex_ready, mm_ready = sem("ft_done"), sem("ft_ready"), sem("mx_ready"), sem("ex_ready"), sem("mm_ready")
        stf_ready, rsf_ready, mvf_ready, rk_done, pos_ready, eid_ready = (
            sem("stf_ready"), sem("rsf_ready"), sem("mvf_ready"), sem("rk_done"), sem("pos_ready"), sem("eid_ready"))
        dve_route, dve_eid, dve_st2, rsn_ready = sem("dve_route"), sem("dve_eid"), sem("dve_st2"), sem("rsn_ready")
        posb_ready, ve5_ready, xg_ready = sem("posb_ready"), sem("ve5_ready"), sem("xg_ready")
        nmf_ready = sem("nmf_ready")
        s_scat = [[sem(f"s_scat{b}{q}") for q in range(4)] for b in range(2)]
        phase = []
        for ph in "bde":
            phase.append({n: sem(f"{n}_{ph}") for n in (
                "xt_done", "xt_ready", "h12_done", "silu_ready", "he_ready", "het_done", "het_ready",
                "y_done", "y_used") + {"b": ("xf_ready",), "d": (), "e": ("xf_ready", "step")}[ph]})
        s_load = [sem(f"s_load{k}") for k in range(4)]
        s_store = [sem(f"s_store{k}") for k in range(4)]
        s_gath = [[sem(f"s_gath{u}{b}") for b in range(2)] for u in range(2)]
        gath_used, st5_ready, r5_ready, out_ready = sem("gath_used"), sem("st5_ready"), sem("r5_ready"), sem("out_ready")

        x_d = x.rearrange("(t p) d -> p t d", p=P)
        out_d = out.rearrange("(t p) d -> p t d", p=P)
        SHARED = 2
        GATE = 2 * EI

        def col12(m):
            return m * 2 * EI + NE * (m > 0)

        xs_d = xs_dram.rearrange("(s p) d -> p s d", p=P)
        eo_d = eo_dram.rearrange("(s p) d -> p s d", p=P)

        block = ctx.enter_context(nc.Block())

        B, D, E = phase

        @block.sync
        def _(sp):
            sp.dma_start(cs[:], cst).then_inc(s_cs, 16)
            sp.dma_start(xa[:, 0:CH, :], x_d[:, 0:CH, :]).then_inc(s_x, 16)
            sp.wait_ge(s_x, 16)
            with sp.Fori(1, NB) as i:
                sp.dma_start(xa[:, bass.ts(i, CH), :], x_d[:, bass.ts(i, CH), :]).then_inc(s_x, 16)
                sp.wait_ge(s_x, i * 16 + 16)
                sp.sem_inc(carry, 1)
            sp.dma_start(xa[:, NT:NT + CH, :], x_d[:, 0:CH, :]).then_inc(s_x, 16)
            sp.wait_ge(zf_ready, 1)
            zr = SLOTS // P
            sp.dma_start(xs_dram.rearrange("(p r) d -> p r d", p=P), zero[:].broadcast_to([P, zr, DM])).then_inc(s_zero, 16)
            sp.wait_ge(o_done, NB * CH)
            sp.dma_start(w3_s, w3.rearrange("(k p) n -> p k n", p=EK)).then_inc(s_w3, 16)
            for landed in s_scat[0] + s_scat[1]:
                sp.wait_ge(landed, 32 * HT // 4)
            for q in range(4):
                sp.dma_start(xl[:, q, :], xs_dram[q * P:(q + 1) * P, :]).then_inc(s_load[q], 16)
            with sp.Fori(0, SJ // 4) as j:
                for q in range(4):
                    sp.wait_ge(D["xt_done"], j * 4 + q + 1)
                    sp.dma_start(xl[:, q, :], xs_d[:, bass.ds(j * 4 + q + 4, 1), :].rearrange("p s d -> p (s d)")).then_inc(s_load[q], 16)
                for q in range(4):
                    sp.wait_ge(D["y_used"], j * 4 + q + 3)
                    sp.dma_start(eo_d[:, bass.ds(j * 4 + q, 1), :].rearrange("p s d -> p (s d)"), ob[:, q, :]).then_inc(s_store[q], 16)
            with sp.Fori(0, HT) as j:
                sp.wait_ge(out_ready, j * 2 + 2)
                sp.sem_inc(carry, 1)
                for b in range(2):
                    sp.dma_start(out_d[:, bass.ds(b * HT + j, 1), :].rearrange("p s d -> p (s d)"),
                                 xa[:, bass.ds(b * HT + j, 1), :].rearrange("p s d -> p (s d)")).then_inc(s_out, 16)
            sp.wait_ge(s_out, 16 * NT)

        @block.tensor
        def _(pe):
            def x_to_v(k, bk):
                for c in range(CH):
                    mm = pe.transpose(bk[:, c * P:(c + 1) * P], v[:, c, k * P:(k + 1) * P], ident)
                mm.then_inc(vt_done, 1)

            def scores(i, c, g):
                n = 2 * c + g
                w = W[n % 2 + 1]
                if n >= 2:
                    pe.wait_ge(m_ready, i * 8 + n - 1)
                mm = pe.matmul(w[:, :], bT[g * HD:(g + 1) * HD, c * P:(c + 1) * P],
                               cT[g * HD:(g + 1) * HD, :, c * P:(c + 1) * P], start=True, stop=True)
                mm.then_inc(g_done, 1)

            def yT(i, c):
                pe.wait_ge(ygn_ready, i * 4 + c + 1)
                bk = X[0] if c < 3 else W[2]
                for k in range(DI // P):
                    mm = pe.transpose(bk[:, k * P:(k + 1) * P], ygn[:, k * P:(k + 1) * P], ident)
                mm.then_inc(yt_done, 1)

            def out_proj(i, c):
                pe.wait_ge(ynt_ready, i * 4 + c + 1)
                for k in range(DI // P):
                    mm = pe.matmul(OB[c % 2][:, 0:DM], ynT[:, k, :], wout_s[:, k, :], start=False, stop=(k == DI // P - 1))
                mm.then_inc(o_done, 1)

            def xbd_of(n, c):
                for k in range(KD):
                    mm = pe.matmul(X[c % 2][:, 0:XBD], hsT[:, k, c * P:(c + 1) * P],
                                   win_s[:, k, DI:DI + XBD], start=(k == 0), stop=(k == KD - 1))
                mm.then_inc(xb_done, 1)

            def ct_of(n, j):
                for k in range(KD):
                    mm = pe.matmul(W[j % 3][:, :], win_s[:, k, DI + XBD + j * P:DI + XBD + (j + 1) * P],
                                   hsT[:, k, :], start=(k == 0), stop=(k == KD - 1))
                mm.then_inc(ct_done, 1)

            pe.wait_ge(s_cs, 16)
            pe.wait_ge(v_ready, CH)
            x_to_v(0, X[1])
            x_to_v(1, X[0])
            pe.wait_ge(s_win, 16)
            pe.wait_ge(consts_ready, 1)
            pe.wait_ge(hst_ready, 2)
            xbd_of(0, 0)
            xbd_of(0, 1)
            ct_of(0, 0)
            with pe.Fori(0, NB) as i:
                for c in range(2, CH):
                    pe.wait_ge(xb_ready, i * 4 + c - 1)
                    xbd_of(i, c)
                for j in range(1, JH):
                    if j == 3:
                        pe.wait_ge(ct_ready, i * 4 + 1)
                    ct_of(i, j)
                pe.wait_ge(xb_ready, i * 4 + 4)
                for c in range(CH):
                    mm = pe.transpose(X[0][:, c * P:(c + 1) * P], xbd[:, c, XB:2 * XB], ident)
                mm.then_inc(bt_done, 1)
                for c in range(CH):
                    pe.wait_ge(ct_ready, i * 4 + min(c + 2, 4))
                    if c == 3:
                        pe.wait_ge(sz_ready, i * 4 + 1)
                    for k in range(KD):
                        mm = pe.matmul(W[(c + 1) % 3][:, :], hsT[:, k, c * P:(c + 1) * P], win_s[:, k, 0:DI],
                                       start=(k == 0), stop=(k == KD - 1))
                    mm.then_inc(z_done, 1)
                    if c == 1:
                        pe.wait_ge(parts_ready, i + 1)
                        ptb = X[1][:, :].bitcast(BF16)
                        for q in range(CH):
                            mm = pe.transpose(ptb[0:3 * NH, q * P:(q + 1) * P], parts[:, q, :, :].rearrange("p a h -> p (a h)"), ident_b[:])
                        mm.then_inc(pt_done, 1)
                        pe.wait_ge(bt_ready, i + 1)
                        for q, col in enumerate((C_INCL, C_AFTER, C_ONES)):
                            mm = pe.matmul(X[0][:, q * 32:(q + 1) * 32], cs[:, col:col + P], dtw[:, 12, :, :],
                                           start=True, stop=True)
                        mm.then_inc(cum_done, 1)
                pe.wait_ge(s_fc1, 16)
                for f in range(KF):
                    if f < 3:
                        pe.wait_ge(sz_ready, i * 4 + f + 2)
                    else:
                        pe.wait_ge(gelu_ready, i * 8 + f - 2)
                    for k in range(KD):
                        mm = pe.matmul(W[(f + 2) % 3][:, :], fc1_s[:, k, f * P:(f + 1) * P], hsT[:, k, :],
                                       start=(k == 0), stop=(k == KD - 1))
                    mm.then_inc(fc1_done, 1)
                    if f == 0:
                        pe.wait_ge(pt_ready, i + 1)
                    if f == 1:
                        pe.wait_ge(pwd_ready, i * 3 + 3)
                    if f >= 2:
                        pe.wait_ge(scan_done, i * 8 + f - 1)
                    pe.matmul(X[(f + 1) % 2][:, :], sel_b[:, f, :], partsT[:, :, :].rearrange("p c t -> p (c t)"),
                              start=True, stop=True).then_inc(bc_done, 1)
                pe.wait_ge(s_fc2, 16)
                pe.wait_ge(s_wout, 16)
                pe.wait_ge(gelu_ready, i * 8 + 8)
                scores(i, 0, 0)
                scores(i, 0, 1)
                for c in range(CH):
                    if c == 0:
                        pe.wait_ge(s_reset, i + 1)
                    else:
                        pe.wait_ge(s_ready, i * 8 + 2 * c)
                        pe.wait_ge(t1_done, i * 4 + c)
                    for j in range(JH):
                        mm = pe.matmul(I[:, j * P:(j + 1) * P], cT[:, j, c * P:(c + 1) * P], S[:, j, :],
                                       start=True, stop=True)
                    mm.then_inc(inter_done, 1)
                    pe.wait_ge(xw_ready, i * 4 + c + 1)
                    if c == 0:
                        pe.wait_ge(scan_done, i * 8 + 8)
                    for g in range(NG):
                        mm = pe.matmul(X[1][g * HD:(g + 1) * HD, 0:JH * HD],
                                       xbd[:, c, XB + g * HD:XB + (g + 1) * HD],
                                       xw[:, c % 2, g * JH * HD:(g + 1) * JH * HD], start=True, stop=True)
                    mm.then_inc(inc_done, 1)
                    if c > 0:
                        yT(i, c - 1)
                    pe.wait_ge(m_ready, i * 8 + 2 * c + 2)
                    if c > 0:
                        pe.wait_ge(t2_done, i * 4 + c)
                    for h, at in ((0, 0), (1, 1), (2, 2), (3, 3), (7, 6), (6, 5), (5, 4), (4, None)):
                        lo, n = (h, 1) if at is None else (at, 2)
                        mm = pe.matmul(Y[:, lo * HD:(lo + n) * HD], M[:, c % 2, h, :],
                                       xdt[:, c % 2, lo * HD:(lo + n) * HD], start=True, stop=True)
                    mm.then_inc(y_done, 1)
                    if c == CH - 1:
                        pe.wait_ge(v_ready, i * 4 + 8)
                        pe.wait_ge(s_ready, i * 8 + 8)
                        x_to_v(0, X[1])
                    if c > 0:
                        out_proj(i, c - 1)
                    if c < CH - 1:
                        scores(i, c + 1, 0)
                        scores(i, c + 1, 1)
                    else:
                        x_to_v(1, X[0])
                    if c >= 2:
                        pe.wait_ge(o_used, i * 4 + c - 1)
                    for k in range(KF):
                        mm = pe.matmul(OB[c % 2][:, 0:DM], gT[:, k, c * P:(c + 1) * P], fc2_s[:, k, :],
                                       start=(k == 0), stop=False)
                pe.wait_ge(hst_ready, i * 2 + 4)
                xbd_of(i + 1, 0)
                xbd_of(i + 1, 1)
                yT(i, 3)
                pe.wait_ge(o_used, i * 4 + 3)
                ct_of(i + 1, 0)
                out_proj(i, 3)

            def turn_block(n):
                pe.wait_ge(vf_ready, n * 4 + 4)
                for k in range(KD):
                    for c in range(CH):
                        mm = pe.transpose(X[1 - k][:, c * P:(c + 1) * P], v[:, c, k * P:(k + 1) * P], ident)
                    mm.then_inc(ft_done, 1)

            def router(n, u):
                pe.wait_ge(ft_ready, n * 2 + 2)
                for c in range(CH):
                    for k in range(KD):
                        mm = pe.matmul(W[0][:, bass.ds((n * CH + c) * NE, NE)], fT[u][:, k, c * P:(c + 1) * P],
                                       w12_s[:, k, GATE:GATE + NE], start=(k == 0), stop=(k == KD - 1))
                mm.then_inc(lg_done, 1)

            turn_block(0)
            pe.wait_ge(s_w12, 16)
            with pe.Fori(0, NB // 2 - 1) as i:
                for u in range(2):
                    pe.wait_ge(ft_ready, (i * 2 + u) * 2 + 2)
                    turn_block(i * 2 + u + 1)
                    router(i * 2 + u, u)
            pe.wait_ge(ft_ready, (NB - 2) * 2 + 2)
            turn_block(NB - 1)
            router(NB - 2, 0)
            router(NB - 1, 1)

            def first(S_, n, bk, xT, cols, w):
                for k in range(KD):
                    mm = pe.matmul(bk[:, 0:w], xT[:, k, :], w12_s[:, k, cols], start=(k == 0), stop=(k == KD - 1))
                mm.then_inc(S_["h12_done"], 1)

            def turn(S_, n, a):
                pe.wait_ge(S_["he_ready"], n)
                for k in range(2):
                    mm = pe.transpose(X[a][0:EK, k * P:(k + 1) * P], he[:, a, k * EK:(k + 1) * EK], ident)
                mm.then_inc(S_["het_done"], 1)

            def turn_x(S_, n, src):
                pe.wait_ge(S_["xf_ready"], n)
                for k in range(KD):
                    mm = pe.transpose(I[:, k * P:(k + 1) * P], src[:, k * P:(k + 1) * P], ident)
                mm.then_inc(S_["xt_done"], 1)

            def half_first(S_, m):
                first(S_, None, W[m], xfT, slice(col12(m), col12(m) + 2 * EI), 2 * EI)

            def shared(S_, meanwhile=None):
                turn_x(S_, 1, xf[:, 0, 0, :])
                pe.wait_ge(S_["xt_ready"], 1)
                half_first(S_, 0)
                half_first(S_, 1)
                if meanwhile is not None:
                    meanwhile()
                turn(S_, 1, 0)
                turn_x(S_, 2, xf[:, 0, 1, :])
                with pe.Fori(0, HT // 4) as r:
                    for q in range(4):
                        j = r * 4 + q
                        pe.wait_ge(S_["xt_ready"], j + 2)
                        pe.wait_ge(S_["he_ready"], j * 2 + 1)
                        half_first(S_, 0)
                        pe.wait_ge(S_["het_ready"], j * 2 + 1)
                        turn(S_, j * 2 + 2, 1)
                        pe.wait_ge(S_["y_used"], j + 1)
                        for k in range(2):
                            pe.matmul(YO[q % 2][:, 0:DM], heT[:, 0, k, :], w3_s[:, k, :], start=(k == 0), stop=False)
                        pe.wait_ge(S_["het_ready"], j * 2 + 2)
                        half_first(S_, 1)
                        turn_x(S_, j + 3, xf[:, 0, (q + 2) % 4, :])
                        turn(S_, j * 2 + 3, 0)
                        for k in range(2):
                            mm = pe.matmul(YO[q % 2][:, 0:DM], heT[:, 1, k, :], w3_s[:, 2 + k, :], start=False, stop=(k == 1))
                        mm.then_inc(S_["y_done"], 1)

            def ranks():
                pe.wait_ge(mm_ready, 1)
                pe.matmul(Y[:, 0:NT * NE], cs[:, C_INCL:C_INCL + P], RT[7], start=True, stop=True).then_inc(rk_done, 1)
                pe.matmul(W[2][:, 0:NT * NE], cs[:, C_ONES:C_ONES + P], RT[7], start=True, stop=True).then_inc(rk_done, 1)

            def banks_free(S_, tiles, firsts):
                pe.wait_ge(S_["he_ready"], firsts)
                pe.wait_ge(S_["het_ready"], firsts - 1)
                pe.wait_ge(S_["y_used"], tiles + 2)

            pe.wait_ge(lg_ready, 1)
            pe.wait_ge(s_w3, 16)
            shared(B, ranks)
            banks_free(B, HT, 2 * HT + 2)
            pe.wait_ge(B["xt_ready"], HT + 2)

            def expert_of(n):
                return pe.value_load(eid[0:1, bass.ds(n, 1)], min_val=0, max_val=NE - 1)

            def eid_first(e, q):
                first(D, n, W[q % 2], xsT[:, q % 2], bass.ds(e * (2 * EI) + col12(SHARED), 2 * EI), 2 * EI)

            pe.wait_ge(eid_ready, 1)
            pe.wait_ge(s_load[0], 16)
            for q in range(3):
                pe.wait_ge(s_load[q], 16)
                for k in range(KD):
                    mm = pe.transpose(I[:, k * P:(k + 1) * P], xl[:, q, k * P:(k + 1) * P], ident)
                mm.then_inc(D["xt_done"], 1)
                e = expert_of(q)
                pe.wait_ge(D["xt_ready"], q + 1)
                if q == 2:
                    pe.wait_ge(D["he_ready"], 1)
                eid_first(e, q)
            turn(D, 1, 0)
            with pe.Fori(0, SJ // 4) as j:
                for q in range(4):
                    n = j * 4 + q
                    e = expert_of(n)
                    pe.wait_ge(s_load[(q + 3) % 4], j * 16 + (32 if q + 3 >= 4 else 16))
                    for k in range(KD):
                        mm = pe.transpose(I[:, k * P:(k + 1) * P], xl[:, (q + 3) % 4, k * P:(k + 1) * P], ident)
                    mm.then_inc(D["xt_done"], 1)
                    e3 = expert_of(n + 3)
                    pe.wait_ge(D["het_ready"], n + 1)
                    turn(D, n + 2, (q + 1) % 2)
                    pe.wait_ge(D["y_used"], n + 1)
                    for k in range(2):
                        mm = pe.matmul(YO[q % 2][:, 0:DM], heT[:, q % 2, k, :],
                                       w3_s[:, bass.ds(e * 2 + 2 * SHARED + k, 1), :].rearrange("p s d -> p (s d)"),
                                       start=(k == 0), stop=(k == 1))
                    mm.then_inc(D["y_done"], 1)
                    pe.wait_ge(D["xt_ready"], n + 4)
                    pe.wait_ge(D["he_ready"], n + 2)
                    eid_first(e3, q + 3)
            banks_free(D, SJ, SJ + 2)
            pe.wait_ge(D["xt_ready"], SJ + 3)
            shared(E)

        @block.vector
        def _(dve):
            ch = Chain(dve, dve_step, 33)

            def norm(i, n):
                dve.wait_ge(s_x, n * 16 + 16)
                for c in range(CH):
                    dve.bn_stats(st1[:, c, :], xa[:, n * CH + c, :]).then_inc(dve_st, 1)
                dve.wait_ge(dve_st, n * 4 + 4)
                dve.sem_inc(carry, 1)
                for c in range(CH):
                    dve.bn_aggr(mvb[:, c, :], st1[:, c, :]).then_inc(st_ready, 1)
                dve.wait_ge(st_ready, n * 4 + 4)
                dve.tensor_copy(mv1[:, bass.ts(n, CH), :], mvb[:]).then_inc(mv_ready, 1)

            def norm_out(n):
                dve.wait_ge(mv_ready, n + 1)
                dve.wait_ge(rs_ready, n + 1)
                for c in range(CH):
                    dve.tensor_scalar(v[:, c, :], xa[:, n * CH + c, :], mv1[:, n * CH + c, 0:1], nw[:, 5, c:c + 1],
                                      ALU.subtract, ALU.mult).then_inc(v_ready, 1)

            norm(0, 0)
            dve.wait_ge(s_cs, 16)
            dve.wait_ge(s_sel, 16)
            dve.tensor_copy(sel_b[:, :, :].rearrange("p h m -> p (h m)"), sel_f).then_inc(dve_init, 1)
            dve.tensor_copy(ident_b[:], ident).then_inc(dve_init, 1)
            for c in range(CH):
                dve.tensor_copy(ident4[:, c, :], ident).then_inc(dve_init, 1)
            dve.memset(S[:], 0.0).then_inc(dve_init, 1)
            dve.memset(partsT[:, :, 0:1], 0.0).then_inc(dve_init, 1)
            dve.wait_ge(aneg_ready, 1)
            dve.tensor_scalar(a_neg[:], a_neg[:], -1.0, None, ALU.mult).then_inc(dve_init, 1)
            dve.tensor_scalar(keep[:], cs[:, C_KEEP:C_KEEP + NB], -1.0, None, ALU.mult).then_inc(dve_init, 1)
            dve.memset(mvf[:, NT:, :], 0.0).then_inc(dve_init, 1)
            dve.memset(rsf[:, NT:], 0.0).then_inc(dve_init, 1)
            dve.memset(zero[:], 0.0).then_inc(zf_ready, 1)
            dve.wait_ge(dve_init, 12)
            dve.memset(rsm[:, 0, 0:1], 0.0).then_inc(consts_ready, 1)
            norm_out(0)

            def take_xbd(n, c):
                dve.wait_ge(xb_done, n * 4 + c + 1)
                dve.tensor_copy(xbd[:, c, :], X[c % 2][:, 0:XBD]).then_inc(xb_ready, 1)

            def take_ct(n, j):
                dve.wait_ge(ct_done, n * 4 + j + 1)
                dve.tensor_copy(cT[:, j, :], W[j % 3][:, :]).then_inc(ct_ready, 1)

            take_xbd(0, 0)
            take_xbd(0, 1)
            take_ct(0, 0)
            with dve.Fori(0, NB) as i:
                ch.start(i * ch.per)
                for c in range(2, CH):
                    take_xbd(i, c)
                dve.wait_ge(xb_ready, i * 4 + 4)
                V = [dtw[:, q, :, :] for q in range(14)]
                ch.link(dve.tensor_tensor(V[0], xbd[:, :, 2 * XB:XBD],
                                          rw[:, R_DTB:R_DTB + NH].unsqueeze(1).broadcast_to([P, CH, NH]), ALU.add))
                dve.scalar_tensor_tensor(V[1], V[0], -1.0, V[0], ALU.mult, ALU.min).then_inc(na_ready, 1)
                take_ct(i, 1)
                dve.wait_ge(e_ready, i + 1)
                dve.tensor_scalar(V[3], V[2], 1.0, None, ALU.add).then_inc(w1_ready, 1)
                dve.wait_ge(w1_ready, i + 1)
                ch.link(dve.tensor_scalar(V[4], V[3], -1.0, None, ALU.add))
                ch.link(dve.tensor_scalar(V[5], V[4], 0.0, None, ALU.is_equal))
                ch.link(dve.tensor_tensor(V[6], V[4], V[5], ALU.add))
                ch.link(dve.reciprocal(V[7], V[6]))
                ch.link(dve.tensor_tensor(V[8], V[2], V[7], ALU.mult))
                take_ct(i, 2)
                dve.wait_ge(ln_ready, i + 1)
                ch.link(dve.tensor_tensor(V[9], V[13], V[5], ALU.add))
                ch.link(dve.tensor_tensor(V[10], V[8], V[9], ALU.mult))
                dve.scalar_tensor_tensor(V[11], V[0], 0.0, V[10], ALU.max, ALU.add).then_inc(dt_ready, 1)
                dve.wait_ge(dt_ready, i + 1)
                ch.link(dve.tensor_tensor(V[9], V[11], a_neg[:].unsqueeze(1).broadcast_to([P, CH, NH]), ALU.mult))
                dve.tensor_scalar(V[12], V[9], A_MIN, None, ALU.max).then_inc(a_ready, 1)
                take_ct(i, 3)
                dve.wait_ge(da_ready, i + 1)
                ch.link(dve.tensor_copy(parts[:, :, 0, :], V[4]))
                ch.link(dve.tensor_tensor(V[6], V[4], parts[:, :, 0, :], ALU.subtract))
                ch.link(dve.tensor_copy(parts[:, :, 1, :], V[6]))
                ch.link(dve.tensor_tensor(V[7], V[6], parts[:, :, 1, :], ALU.subtract))
                dve.tensor_copy(parts[:, :, 2, :], V[7]).then_inc(parts_ready, 1)
                dve.wait_ge(pt_done, i + 1)
                ptv = X[1][:, :].bitcast(BF16)[0:3 * NH, 0:TB].rearrange("p (c t) -> p c t", c=CH)
                dve.tensor_copy(partsT[:, :, 1:P], ptv[:, :, 1:P]).then_inc(pt_ready, 1)
                norm(i, i + 1)
                for h in range(NH):
                    dve.wait_ge(bc_done, i * 8 + h + 1)
                    dve.tensor_tensor_scan(L[:, h, :], X[(h + 1) % 2][:, :], ident4[:, :, :].rearrange("p c t -> p (c t)"),
                                           0.0, ALU.mult, ALU.add).then_inc(scan_done, 1)
                norm_out(i + 1)
                dve.tensor_tensor(S[:].bitcast(I32).rearrange("p j m -> p (j m)"), S[:].bitcast(I32).rearrange("p j m -> p (j m)"),
                                  keep[:, bass.ds(i, 1)].broadcast_to([P, JH * P]),
                                  ALU.bitwise_and).then_inc(s_reset, 1)

                def mask(c, g):
                    dve.wait_ge(g_done, i * 8 + 2 * c + g + 1)
                    if c == 0 and g == 0:
                        dve.wait_ge(scan_done, i * 8 + 8)
                    if c >= 2:
                        dve.wait_ge(y_done, i * 4 + c - 1)
                    dve.tensor_tensor(M[:, c % 2, g * JH:(g + 1) * JH, :],
                                      W[(2 * c + g) % 2 + 1][:, :].rearrange("p (h t) -> p h t", h=JH),
                                      L[:, g * JH:(g + 1) * JH, c * P:(c + 1) * P], ALU.mult).then_inc(m_ready, 1)

                def finish_a(c):
                    t = i * CH + c
                    ch.link(dve.tensor_scalar(ub[:], xa[:, t, :], mv1[:, t, 0:1], rs1[:, bass.ds(t, 1)],
                                              ALU.subtract, ALU.mult))
                    ch.link(dve.tensor_tensor(ub[:], ub[:], rw[:, R_FB:R_FB + DM], ALU.add))
                    dve.wait_ge(o_done, i * 4 + c + 1)
                    dve.tensor_tensor(o[:], OB[c % 2][:, 0:DM], ub[:], ALU.add).then_inc(o_used, 1)
                    dve.wait_ge(o_used, i * 4 + c + 1)
                    ch.link(dve.bn_stats(st3[:], o[:]), carry)
                    dve.bn_aggr(mv3[:], st3[:]).then_inc(st3_ready, 1)

                def finish_b(c):
                    t = i * CH + c
                    dve.wait_ge(r3_ready, i * 4 + c + 1)
                    ch.link(dve.tensor_scalar(ub[:], o[:], mv3[:, 0:1], r3[:, 1:2], ALU.subtract, ALU.mult))
                    ch.link(dve.tensor_tensor(xa[:, t, :], xa[:, t, :], ub[:], ALU.add))

                mask(0, 0)
                mask(0, 1)
                for c in range(CH):
                    dve.wait_ge(inter_done, i * 4 + c + 1)
                    dve.wait_ge(pwd_ready, i * 3 + 3)
                    if c > 0:
                        dve.wait_ge(t2_done, i * 4 + c)
                    dve.tensor_tensor(
                        t1[:].rearrange("p (g j d) -> p g j d", g=NG, j=JH),
                        I[:, :].rearrange("p (j g d) -> p g j d", g=NG, j=JH),
                        pwd[:, 0, c, :].rearrange("p (g j) -> p g j", g=NG).unsqueeze(3).broadcast_to([P, NG, JH, HD]),
                        ALU.mult).then_inc(t1_done, 1)
                    dve.wait_ge(inc_done, i * 4 + c + 1)
                    dve.wait_ge(s_scaled, i * 4 + c + 1)
                    for g in range(NG):
                        q = slice(g * HD, (g + 1) * HD)
                        dve.tensor_tensor(S[q, :, g * HD:(g + 1) * HD], S[q, :, g * HD:(g + 1) * HD],
                                          X[1][q, 0:JH * HD].rearrange("p (j d) -> p j d", j=JH),
                                          ALU.add).then_inc(s_ready, 1)
                    dve.wait_ge(y_done, i * 4 + c + 1)
                    dve.wait_ge(t1_done, i * 4 + c + 1)
                    if c > 0:
                        dve.wait_ge(yg_ready, i * 4 + c)
                    dve.tensor_tensor(t2[:], t1[:], Y[:, :], ALU.add).then_inc(t2_done, 1)
                    if c > 0:
                        finish_a(c - 1)
                    if c < CH - 1:
                        mask(c + 1, 0)
                        mask(c + 1, 1)
                    if c > 0:
                        finish_b(c - 1)
                take_xbd(i + 1, 0)
                take_xbd(i + 1, 1)
                take_ct(i + 1, 0)
                finish_a(CH - 1)
                finish_b(CH - 1)
                ch.end()

            for S_ in phase:
                dve.sem_inc(S_["y_used"], 2)
            cf = Chain(dve, dve_step2, CH)

            def tile_stats(n):
                for c in range(CH):
                    dve.bn_stats(st1[:, c, :], xa[:, n * CH + c, :]).then_inc(dve_st2, 1)

            def block_stats(n):
                cf.start(n * cf.per)
                dve.wait_ge(dve_st2, n * 4 + 4)
                dve.sem_inc(carry, 1)
                for c in range(CH):
                    cf.link(dve.bn_aggr(mvb[:, c, :], st1[:, c, :]), carry)
                dve.tensor_copy(mvf[:, bass.ds(n * CH, CH), :], mvb[:]).then_inc(mvf_ready, 1)
                dve.wait_ge(mvf_ready, n + 1)
                dve.sem_inc(stf_ready, 1)

            def normed(n):
                dve.wait_ge(rsf_ready, n + 1)
                for c in range(CH):
                    t = n * CH + c
                    dve.tensor_scalar(v[:, c, :], xa[:, t, :], mvf[:, t, 0:1], rsf[:, bass.ds(t, 1)],
                                      ALU.subtract, ALU.mult).then_inc(vf_ready, 1)

            tile_stats(0)
            block_stats(0)
            tile_stats(1)
            normed(0)
            block_stats(1)
            with dve.Fori(1, NB - 1) as i:
                tile_stats(i + 1)
                dve.wait_ge(ft_done, i * 2)
                normed(i)
                block_stats(i + 1)
            dve.wait_ge(ft_done, NB * 2 - 2)
            normed(NB - 1)

            def x_to_xf(S_, t, b, s):
                dve.tensor_scalar(xf[:, b, s, :], xa[:, t, :], mvf[:, t, 0:1], rsf[:, bass.ds(t, 1)],
                                  ALU.subtract, ALU.mult).then_inc(xg_ready if b else S_["xf_ready"], 1)

            dve.scalar_tensor_tensor(nmf[:], mvf[:, :, 0], -1.0, rsf[:], ALU.mult, ALU.mult).then_inc(nmf_ready, 1)
            x_to_xf(B, 0, 0, 0)
            x_to_xf(B, 1, 0, 1)
            x_to_xf(B, HT, 1, 0)
            dve.wait_ge(lg_done, NB)
            dve.tensor_copy(RT[0], W[0][:, 0:NT * NE]).then_inc(lg_ready, 1)
            dve.wait_ge(lg_ready, 1)
            rc = Chain(dve, dve_route, 31)
            link = rc.link
            te = lambda ap: ap.rearrange("p (t e) -> p t e", e=NE)
            by_t = lambda ap: ap.unsqueeze(2).broadcast_to([P, NT, NE])
            first8 = cs[:, C_FIRST:C_FIRST + NE].unsqueeze(1).broadcast_to([P, NT, NE])
            LG, PR, EQ, KY, OH0, OH1, PM, MM = RT
            link(dve.tensor_reduce(rsm[:, 0, :], te(LG), AX_X, ALU.max))
            dve.tensor_tensor(te(PM), te(LG), by_t(rsm[:, 0, :]), ALU.subtract).then_inc(mx_ready, 1)
            dve.wait_ge(ex_ready, 1)
            link(dve.tensor_reduce(rsm[:, 1, :], te(EQ), AX_X, ALU.add))
            link(dve.reciprocal(rsm[:, 2, :], rsm[:, 1, :]))
            link(dve.tensor_tensor(te(PR), te(EQ), by_t(rsm[:, 2, :]), ALU.mult))

            def pick(k, src, mark):
                link(dve.tensor_reduce(cw[:, k, :], te(src), AX_X, ALU.max))
                link(dve.tensor_tensor(te(EQ), te(src), by_t(cw[:, k, :]), ALU.is_equal))
                link(dve.tensor_tensor(te(KY), te(EQ), first8, ALU.mult))
                link(dve.tensor_reduce(rsm[:, 3, :], te(KY), AX_X, ALU.max))
                link(dve.tensor_tensor(te(mark), first8, by_t(rsm[:, 3, :]), ALU.is_equal))

            pick(0, PR, OH0)
            link(dve.scalar_tensor_tensor(PM, OH0, -4.0, PR, ALU.mult, ALU.add))
            pick(1, PM, OH1)
            dve.tensor_tensor(MM, OH0, OH1, ALU.add).then_inc(mm_ready, 1)
            TOT, INC, RST, OFF, POSA = RC
            et = lambda ap: ap.rearrange("p (e t) -> p e t", e=NE)
            link(dve.memset(RST, 1.0))
            link(dve.memset(et(RST)[:, :, 0:1], 0.0))
            dve.wait_ge(rk_done, 2)
            link(dve.tensor_copy(et(TOT), W[2][:, 0:NT * NE].rearrange("p (t e) -> p e t", e=NE)))
            link(dve.tensor_tensor_scan(INC, RST, TOT, 0.0, ALU.mult, ALU.add))
            cnt, tiles, ends, starts, one = (tl[:, q, :] for q in range(5))
            link(dve.tensor_scalar(cnt, et(INC)[:, :, NT - 1], 1.0 / P, None, ALU.mult))
            iota = cs[:, C_IOTA:C_IOTA + P]
            KT = x.shape[0] // P
            g1 = grid[:, 0:NE * KT].rearrange("p (e k) -> p e k", e=NE)
            link(dve.tensor_tensor(g1, cnt.unsqueeze(2).broadcast_to([P, NE, KT]),
                                   iota[:, 0:KT].unsqueeze(1).broadcast_to([P, NE, KT]), ALU.is_gt))
            link(dve.tensor_reduce(tiles, g1, AX_X, ALU.add))
            link(dve.memset(one, 1.0))
            link(dve.tensor_tensor_scan(ends, one, tiles, 0.0, ALU.mult, ALU.add))
            link(dve.tensor_tensor(starts, ends, tiles, ALU.subtract))
            link(dve.tensor_scalar(cnt, starts, float(P), -1.0, ALU.mult, ALU.add))
            link(dve.tensor_tensor(OFF, INC, TOT, ALU.subtract))
            link(dve.tensor_tensor(et(OFF), et(OFF), cnt.unsqueeze(2).broadcast_to([P, NE, NT]), ALU.add))
            link(dve.tensor_tensor(te(POSA), te(Y[:, 0:NT * NE]), OFF.rearrange("p (e t) -> p t e", e=NE), ALU.add))
            for k, mark in enumerate((OH0, OH1)):
                link(dve.tensor_tensor(KY, mark, POSA, ALU.mult))
                link(dve.tensor_reduce(posf[:, k, :], te(KY), AX_X, ALU.add))
            dve.tensor_copy(pos[:], posf[:]).then_inc(pos_ready, 1)

            def tile_experts():
                gj = grid.rearrange("p (j e) -> p j e", e=NE)
                ce.link(dve.tensor_tensor(gj, ends.unsqueeze(1).broadcast_to([P, SJ, NE]),
                                          iota[:, 0:SJ].unsqueeze(2).broadcast_to([P, SJ, NE]), ALU.is_le))
                ce.link(dve.memset(eidf[:, SJ:], 0.0))
                ce.link(dve.tensor_reduce(eidf[:, 0:SJ], gj, AX_X, ALU.add))
                ce.link(dve.tensor_scalar(eidf[:, 0:SJ], eidf[:, 0:SJ], NE - 1.0, None, ALU.min))
                dve.tensor_copy(eid[:], eidf[:]).then_inc(eid_ready, 1)

            def gate(S_, a, n):
                dve.wait_ge(S_["silu_ready"], n)
                dve.tensor_tensor(he[:, a, :], hs_[:, a, :], W[a][:, EI:2 * EI], ALU.mult).then_inc(S_["he_ready"], 1)

            ce = Chain(dve, dve_eid, 4)
            gate(B, 0, 1)
            gate(B, 1, 2)
            tile_experts()

            def first_half(r, begun):
                for q in range(4):
                    j = r * 4 + q
                    dve.wait_ge(B["het_done"], j * 2 + 1)
                    gate(B, 0, j * 2 + 3)
                    if begun or q >= 2:
                        dve.wait_ge(s_scat[0][(q + 2) % 4], r * 32 + (32 if q >= 2 else 0))
                    x_to_xf(B, j + 2, 0, (q + 2) % 4)
                    dve.wait_ge(B["het_done"], j * 2 + 2)
                    gate(B, 1, j * 2 + 4)
                    if begun or q == 3:
                        dve.wait_ge(s_scat[1][(q + 1) % 4], r * 32 + (32 if q == 3 else 0))
                    x_to_xf(B, j + HT + 1, 1, (q + 1) % 4)
                    dve.wait_ge(B["y_done"], j + 1)
                    dve.tensor_copy(ysh[:, bass.ds(j, 1), :].rearrange("p s d -> p (s d)"), YO[q % 2][:, 0:DM]).then_inc(B["y_used"], 1)

            first_half(0, False)
            with dve.Fori(1, HT // 4) as r:
                first_half(r, True)

            gate(D, 0, 1)
            gate(D, 1, 2)
            def four_tiles(j, begun):
                for q in range(4):
                    n = j * 4 + q
                    dve.wait_ge(D["het_done"], n + 1)
                    gate(D, q % 2, n + 3)
                    dve.wait_ge(D["y_done"], n + 1)
                    if begun:
                        dve.wait_ge(s_store[q], j * 16)
                    dve.tensor_copy(ob[:, q, :], YO[q % 2][:, 0:DM]).then_inc(D["y_used"], 1)

            four_tiles(0, False)
            with dve.Fori(1, SJ // 4) as j:
                four_tiles(j, True)

            gate(E, 0, 1)
            gate(E, 1, 2)
            c5 = Chain(dve, E["step"], 10)

            def mix(m, u):
                j = m * 2 + u
                a = [acc[:, u, b, :] for b in range(2)]
                w = [[cw[:, k, bass.ds(j + b * HT, 1)] for k in range(2)] for b in range(2)]
                dve.wait_ge(s_gath[u][0], m * 32 + 32)
                c5.mark(dve.scalar_tensor_tensor(a[0], gath[:, u, 0, 0, :], w[0][0], ysh[:, bass.ds(j, 1), :].rearrange("p s d -> p (s d)"),
                                                 ALU.mult, ALU.add))
                dve.wait_ge(s_gath[u][1], m * 32 + 32)
                dve.wait_ge(E["y_done"], j + 1)
                dve.scalar_tensor_tensor(a[1], gath[:, u, 1, 0, :], w[1][0], YO[u][:, 0:DM], ALU.mult, ALU.add).then_inc(E["y_used"], 1)
                c5.wait()
                dve.scalar_tensor_tensor(a[0], gath[:, u, 0, 1, :], w[0][1], a[0], ALU.mult, ALU.add).then_inc(gath_used, 1)
                dve.wait_ge(E["y_used"], j + 3)
                dve.scalar_tensor_tensor(a[1], gath[:, u, 1, 1, :], w[1][1], a[1], ALU.mult, ALU.add).then_inc(gath_used, 1)
                for b in range(2):
                    dve.wait_ge(gath_used, j * 2 + b + 1)
                    c5.mark(dve.bn_stats(st4[:, b, :], a[b]))
                c5.wait(carry)
                for b in range(2):
                    dve.bn_aggr(mv5[:, u, b, :], st4[:, b, :]).then_inc(st5_ready, 1)

            def finish_out(m, u):
                j = m * 2 + u
                dve.wait_ge(r5_ready, j + 1)
                for b in range(2):
                    c5.mark(dve.tensor_scalar(acc[:, u, b, :], acc[:, u, b, :], mv5[:, u, b, 0:1], r5[:, u, 1, b:b + 1],
                                              ALU.subtract, ALU.mult))
                c5.wait()
                for b in range(2):
                    t = j + b * HT
                    dve.tensor_tensor(xa[:, t, :], xa[:, t, :], acc[:, u, b, :], ALU.add).then_inc(out_ready, 1)

            def last_half(m, u, mixes, finishes):
                j = m * 2 + u
                dve.wait_ge(E["het_done"], j * 2 + 1)
                gate(E, 0, j * 2 + 3)
                if mixes:
                    mix(m + u - 1, 1 - u)
                dve.wait_ge(E["het_done"], j * 2 + 2)
                gate(E, 1, j * 2 + 4)
                if finishes:
                    finish_out(m - 1, u)
                    dve.wait_ge(out_ready, j * 2 - 2)

            last_half(0, 0, False, False)
            last_half(0, 1, True, False)
            with dve.Fori(1, HT // 2) as m:
                c5.start(m * 10 - 7)
                last_half(m, 0, True, True)
                last_half(m, 1, True, True)
                assert c5.n == 10
            c5.start(HT * 5 - 7)
            mix(HT // 2 - 1, 1)
            finish_out(HT // 2 - 1, 0)
            finish_out(HT // 2 - 1, 1)

        @block.scalar
        def _(act):
            act.dma_start(win_s[:], w_in.rearrange("(k p) n -> p k n", p=P)).then_inc(s_win, 16)
            act.dma_start(rw[:], rows.broadcast_to([P, NC_R])).then_inc(s_rw, 16)
            act.dma_start(sel_f, sel).then_inc(s_sel, 16)
            act.dma_start(fc1_s, fc1.rearrange("(k p) n -> p k n", p=P)).then_inc(s_fc1, 16)
            act.dma_start(fc2_s, fc2.rearrange("(k p) n -> p k n", p=P)).then_inc(s_fc2, 16)
            act.dma_start(wout_s, w_out.rearrange("(k p) n -> p k n", p=P)).then_inc(s_wout, 16)
            act.dma_start(w12_s[:], w12.rearrange("(k p) n -> p k n", p=P)).then_inc(s_w12, 16)
            act.wait_ge(s_rw, 16)
            act.activation(a_neg[:], rw[:, R_ALOG:R_ALOG + NH], ACT.Exp).then_inc(aneg_ready, 1)
            act.wait_ge(s_cs, 16)

            def take_hs(n, k):
                act.wait_ge(vt_done, n * 2 + k + 1)
                act.activation(hsT[:, k, :], X[1 - k][:, :], ACT.Identity, bias=lnb[:, k:k + 1],
                               scale=lnw[:, k:k + 1]).then_inc(hst_ready, 1)

            take_hs(0, 0)
            take_hs(0, 1)
            with act.Fori(0, NB) as i:
                act.wait_ge(na_ready, i + 1)
                act.activation(dtw[:, 2, :, :], dtw[:, 1, :, :], ACT.Exp).then_inc(e_ready, 1)
                act.wait_ge(w1_ready, i + 1)
                act.activation(dtw[:, 13, :, :], dtw[:, 3, :, :], ACT.Ln).then_inc(ln_ready, 1)
                act.wait_ge(a_ready, i + 1)
                act.activation(dtw[:, 4, :, :], dtw[:, 12, :, :], ACT.Exp).then_inc(da_ready, 1)
                act.wait_ge(bt_done, i + 1)
                act.activation(bT[:], X[0][:, :], ACT.Copy).then_inc(bt_ready, 1)
                for c in range(CH):
                    act.wait_ge(z_done, i * 4 + c + 1)
                    act.activation(sz[:, c, :], W[(c + 1) % 3][:, :], ACT.Silu).then_inc(sz_ready, 1)
                act.wait_ge(cum_done, i + 1)
                act.activation(pwd[:].rearrange("p a c h -> p (a c h)"), X[0][:, 0:2 * CH * NH], ACT.Exp).then_inc(pwd_ready, 1)
                for g in range(NG):
                    q = slice(g * HD, (g + 1) * HD)
                    act.activation(dec[q, :, :], X[0][q, 2 * CH * NH:3 * CH * NH].rearrange("p (c g j) -> p g c j", c=CH, g=NG)[:, g],
                                   ACT.Exp).then_inc(pwd_ready, 1)
                for f in range(KF):
                    act.wait_ge(fc1_done, i * 8 + f + 1)
                    act.activation(gT[:, f, :], W[(f + 2) % 3][:, :], ACT.Gelu_apprx_tanh,
                                   bias=f1b[:, f:f + 1]).then_inc(gelu_ready, 1)

                def take_y(c):
                    act.wait_ge(yt_done, i * 4 + c + 1)
                    bk = X[0] if c < 3 else W[2]
                    for k in range(DI // P):
                        ins = act.activation(ynT[:, k, :], bk[:, k * P:(k + 1) * P], ACT.Copy, scale=nrw[:, k:k + 1])
                    ins.then_inc(ynt_ready, 1)

                for c in range(CH):
                    if c > 0:
                        take_y(c - 1)
                    act.wait_ge(yg_ready, i * 4 + c + 1)
                    act.activation(ygn[:], yg[:], ACT.Square, accum_out=rr[:, 0:1]).then_inc(ssq_ready, 1)
                    if c == CH - 1:
                        take_hs(i + 1, 0)
                        take_hs(i + 1, 1)
                    act.wait_ge(rr_ready, i * 4 + c + 1)
                    act.activation(ygn[:], yg[:], ACT.Copy, scale=rr[:, 3:4]).then_inc(ygn_ready, 1)
                take_y(CH - 1)

            def two_blocks(i, begun):
                for u in range(2):
                    n = i * 2 + u
                    if begun:
                        act.wait_ge(lg_done, n - 1)
                    for k in range(KD):
                        act.wait_ge(ft_done, n * 2 + k + 1)
                        act.activation(fT[u][:, k, :], X[1 - k][:, :], ACT.Copy).then_inc(ft_ready, 1)

            two_blocks(0, False)
            with act.Fori(1, NB // 2) as i:
                two_blocks(i, True)
            act.wait_ge(mx_ready, 1)
            act.activation(RT[2], RT[6], ACT.Exp).then_inc(ex_ready, 1)

            def silu(S_, a, n):
                act.wait_ge(S_["h12_done"], n)
                act.activation(hs_[:, a, :], W[a][:, 0:EI], ACT.Silu).then_inc(S_["silu_ready"], 1)

            def take_h(S_, a, n):
                act.wait_ge(S_["het_done"], n)
                act.activation(heT[:, a].rearrange("p k t -> p (k t)"), X[a][0:EK, 0:2 * P],
                               ACT.Copy).then_inc(S_["het_ready"], 1)

            def take_x(S_, dst, n):
                act.wait_ge(S_["xt_done"], n)
                act.activation(dst.rearrange("p k t -> p (k t)"), I[:, 0:DM], ACT.Copy).then_inc(S_["xt_ready"], 1)

            def normed(j, s):
                t = j + HT
                act.activation(xf[:, 0, s, :], xa[:, bass.ds(t, 1), :].rearrange("p s d -> p (s d)"), ACT.Identity,
                               bias=nmf[:, bass.ds(t, 1)], scale=rsf[:, bass.ds(t, 1)]).then_inc(E["xf_ready"], 1)

            def shared(S_):
                take_x(S_, xfT, 1)
                silu(S_, 0, 1)
                silu(S_, 1, 2)
                take_h(S_, 0, 1)
                take_x(S_, xfT, 2)
                with act.Fori(0, HT // 4) as r:
                    for q in range(4):
                        j = r * 4 + q
                        silu(S_, 0, j * 2 + 3)
                        take_h(S_, 1, j * 2 + 2)
                        if S_ is E:
                            normed(j + 3, (q + 3) % 4)
                        silu(S_, 1, j * 2 + 4)
                        take_x(S_, xfT, j + 3)
                        take_h(S_, 0, j * 2 + 3)

            shared(B)
            for q in range(2):
                take_x(D, xsT[:, q], q + 1)
                silu(D, q, q + 1)
            take_x(D, xsT[:, 0], 3)
            take_h(D, 0, 1)
            with act.Fori(0, SJ // 4) as j:
                for q in range(4):
                    n = j * 4 + q
                    silu(D, q % 2, n + 3)
                    take_x(D, xsT[:, (q + 1) % 2], n + 4)
                    take_h(D, (q + 1) % 2, n + 2)
            for q in range(3):
                normed(q, q)
            shared(E)

        @block.gpsimd
        def _(pool):
            pc = Chain(pool, pool_step, CH * 3)
            pool.memset(nhalf[:], -0.5).then_inc(pool_init, 1)
            pool.wait_ge(pool_init, 1)

            def rsqrt(link, dst, tmp, var, width=1):
                link(pool.tensor_scalar(tmp, var, EPS, 1.0, ALU.add, ALU.mult))
                return pool.tensor_tensor(dst, tmp, nhalf[:, 0:width], ALU.pow)

            def norm_scales(n, link):
                pool.wait_ge(st_ready, n * 4 + 4)
                pool.sem_inc(carry, 1)
                link(pool.tensor_copy(nw[:, 0, :], mvb[:, :, 1]), carry)
                link(rsqrt(link, nw[:, 2, :], nw[:, 1, :], nw[:, 0, :], CH))
                link(pool.tensor_tensor(nw[:, 3, :], nw[:, 2, :], nw[:, 2, :], ALU.mult))
                link(pool.tensor_tensor(nw[:, 3, :], nw[:, 3, :], nw[:, 0, :], ALU.mult), carry)
                pool.tensor_copy(rs1[:, bass.ts(n, CH)], nw[:, 2, :]).then_inc(rs1_ready, 1)
                link(rsqrt(link, nw[:, 4, :], nw[:, 1, :], nw[:, 3, :], CH))
                pool.wait_ge(rs1_ready, n + 1)
                pool.tensor_tensor(nw[:, 5, :], nw[:, 4, :], nw[:, 2, :], ALU.mult).then_inc(rs_ready, 1)

            PN = 7
            pn = Chain(pool, pool_norm, PN)
            norm_scales(0, pn.link)
            pool.wait_ge(s_rw, 16)
            with pool.Fori(0, NB) as i:
                pc.start(i * pc.per)
                pn.start(i * PN + PN)

                def heads(ap):
                    return ap.rearrange("p (g j d) -> p g j d", g=NG, j=JH)

                def bc(ap):
                    return ap.rearrange("p (g j) -> p g j", g=NG).unsqueeze(3).broadcast_to([P, NG, JH, HD])

                def steps(c):
                    xh = xbd[:, c, 0:XB].rearrange("p (g d) -> p g d", g=NG).unsqueeze(2).broadcast_to([P, NG, JH, HD])
                    pool.tensor_tensor(heads(xdt[:, c % 2, :]), xh, bc(dtw[:, 11, c, :]), ALU.mult).then_inc(xdt_ready, 1)
                    pool.wait_ge(pwd_ready, i * 3 + 3)
                    pool.wait_ge(xdt_ready, i * 4 + c + 1)
                    pool.tensor_tensor(heads(xw[:, c % 2, :]), heads(xdt[:, c % 2, :]), bc(pwd[:, 1, c, :]),
                                       ALU.mult).then_inc(xw_ready, 1)

                pool.wait_ge(dt_ready, i + 1)
                norm_scales(i + 1, pn.link)
                pn.end()
                steps(0)
                steps(1)

                def finish(c):
                    pool.wait_ge(st3_ready, i * 4 + c + 1)
                    pool.sem_inc(carry, 1)
                    rsqrt(pc.link, r3[:, 1:2], r3[:, 0:1], mv3[:, 1:2]).then_inc(r3_ready, 1)

                for c in range(CH):
                    pool.wait_ge(inter_done, i * 4 + c + 1)
                    pool.tensor_tensor(S[:], S[:], dec[:, c, :].unsqueeze(2).broadcast_to([P, JH, P]),
                                       ALU.mult).then_inc(s_scaled, 1)
                    xh = xbd[:, c, 0:XB].rearrange("p (g d) -> p g d", g=NG).unsqueeze(2).broadcast_to([P, NG, JH, HD])
                    pool.tensor_tensor(heads(dx[:]), xh, bc(rw[:, R_D:R_D + NH]), ALU.mult).then_inc(dx_ready, 1)
                    pool.wait_ge(dx_ready, i * 4 + c + 1)
                    pool.wait_ge(t2_done, i * 4 + c + 1)
                    pc.link(pool.tensor_tensor(t3[:], t2[:], dx[:], ALU.add))
                    if c > 0:
                        pool.wait_ge(ygn_ready, i * 4 + c)
                    pool.wait_ge(sz_ready, i * 4 + 4)
                    pool.tensor_tensor(yg[:], t3[:], sz[:, c, :], ALU.mult).then_inc(yg_ready, 1)
                    if c < 2:
                        steps(c + 2)
                    if c > 0:
                        finish(c - 1)
                    pool.wait_ge(ssq_ready, i * 4 + c + 1)
                    pool.sem_inc(carry, 1)
                    pc.link(pool.tensor_scalar(rr[:, 1:2], rr[:, 0:1], 1.0 / DI, EPS, ALU.mult, ALU.add))
                    pool.tensor_tensor(rr[:, 3:4], rr[:, 1:2], nhalf[:, 0:1], ALU.pow).then_inc(rr_ready, 1)
                finish(CH - 1)
                pc.end()

            cf = Chain(pool, pool_step2, 1)
            with pool.Fori(0, NB) as i:
                cf.start(i * cf.per)
                pool.wait_ge(stf_ready, i + 1)
                pool.sem_inc(carry, 1)
                cf.link(pool.tensor_scalar(nw[:, 0, :], mvb[:, :, 1], EPS, 1.0, ALU.add, ALU.mult))
                pool.tensor_tensor(nw[:, 1, :], nw[:, 0, :], nhalf[:], ALU.pow).then_inc(rsn_ready, 1)
                pool.wait_ge(rsn_ready, i + 1)
                pool.sem_inc(carry, 1)
                pool.tensor_copy(rsf[:, bass.ts(i, CH)], nw[:, 1, :]).then_inc(rsf_ready, 1)

            def places(j, s, n):
                pool.tensor_copy(posb[:, s], pos[:].rearrange("p k (b t) -> p k b t", b=2)[:, :, :, bass.ds(j, 1)].rearrange("p k b o -> p k (b o)")
                                 ).then_inc(posb_ready, 1)
                pool.wait_ge(posb_ready, n)

            def place(s, b, k):
                return bass.IndirectOffsetOnAxis(ap=posb[:, s, k, b:b + 1].bitcast(U32), axis=0)

            def scatter_four(r, begun):
                for q in range(4):
                    j = r * 4 + q
                    if begun:
                        pool.wait_ge(s_scat[0][q], r * 32)
                        pool.wait_ge(s_scat[1][q], r * 32)
                        pool.sem_inc(carry, 1)
                    places(j, q, j + 1)
                    for b in range(2):
                        pool.wait_ge(xg_ready if b else B["xf_ready"], j + 1)
                        pool.sem_inc(carry, 1)
                        for k in range(2):
                            pool.indirect_dma_start(xs_dram, place(q, b, k), xf[:, b, q, :], None).then_inc(s_scat[b][q], 16)

            pool.wait_ge(pos_ready, 1)
            pool.wait_ge(s_zero, 16)
            scatter_four(0, False)
            with pool.Fori(1, HT // 4) as r:
                scatter_four(r, True)
            for landed in s_scat[0] + s_scat[1]:
                pool.wait_ge(landed, 32 * HT // 4)

            for q in range(4):
                pool.wait_ge(s_store[q], 16 * (SJ // 4))

            def gather(u, b):
                for k in range(2):
                    pool.indirect_dma_start(gath[:, u, b, k, :], None, eo_dram, place(u, b, k)).then_inc(s_gath[u][b], 16)

            def last_scales(j, u):
                pool.wait_ge(st5_ready, j * 2 + 2)
                pool.sem_inc(carry, 1)
                pool.tensor_scalar(r5[:, u, 0, :], mv5[:, u, :, 1], EPS, 1.0, ALU.add, ALU.mult).then_inc(ve5_ready, 1)
                pool.wait_ge(ve5_ready, j + 1)
                pool.tensor_tensor(r5[:, u, 1, :], r5[:, u, 0, :], nhalf[:, 0:2], ALU.pow).then_inc(r5_ready, 1)

            for u in range(2):
                places(u, u, HT + u + 1)
                gather(u, 0)
                gather(u, 1)
            with pool.Fori(0, HT // 2 - 1) as m:
                for u in range(2):
                    j = m * 2 + u
                    pool.wait_ge(gath_used, j * 2 + 2)
                    pool.sem_inc(carry, 1)
                    places(j + 2, u, j + HT + 3)
                    pool.sem_inc(carry, 1)
                    gather(u, 0)
                    last_scales(j, u)
                    gather(u, 1)
            last_scales(HT - 2, 0)
            last_scales(HT - 1, 1)

def kernel(**inputs):
    import concourse.bacc as _bacc
    from concourse.bass_utils import run_bass_kernel_spmd as _run

    a = {k: np.asarray(v) for k, v in inputs.items()}
    g = lambda n: a["L0_attn_" + n]
    f = lambda n: a["L0_ffn_" + n]
    xs = g("hidden_states")
    w_in = g("W_in")
    zc, xc, bcol, cc = DI, XB, XB, DI
    o1 = zc + xc + bcol
    c_cols = w_in[:, o1:o1 + cc].reshape(DM, NG, JH, HD).transpose(0, 2, 1, 3).reshape(DM, cc)
    w_in = np.concatenate([w_in[:, :o1], w_in[:, o1 + cc:], c_cols], 1)
    s1 = f("sw1").reshape(2, EI, DM)
    s2 = f("sw2").reshape(2, EI, DM)
    gates = [s1[0], s2[0], f("gate_w"), s1[1], s2[1]]
    for e in range(NE):
        gates += [f("w1")[e], f("w2")[e]]
    w12 = np.ascontiguousarray(np.concatenate(gates, 0).T)
    w3 = np.concatenate([f("sw3").T, f("w3").transpose(0, 2, 1).reshape(NE * EI, DM)], 0)
    cols = np.concatenate([g("ln_w").reshape(KD, P).T, g("ln_b").reshape(KD, P).T,
                           g("norm_w").reshape(DI // P, P).T, g("fc1_b").reshape(KF, P).T], 1)
    r = np.arange(P)
    masks = np.concatenate([np.eye(P), r[:, None] <= r[None, :], r[:, None] > r[None, :], np.ones((P, P))], 1)
    e8 = np.arange(NE)
    iota = np.broadcast_to(np.concatenate([r, NE - e8])[None], (P, P + NE))
    per_seq = xs.shape[1] // TB
    keep = np.where(np.arange(8) % per_seq == 0, 0, 1).astype(np.float32)
    cst = np.concatenate([masks.astype(np.float32), iota.astype(np.float32), cols,
                          np.broadcast_to(keep[None], (P, 8))], 1)
    rows = np.concatenate([g("dt_bias"), g("A_log"), g("D"), g("fc2_b")])[None]
    sel = np.zeros((3, NH, NH, P), np.float32)
    sel[:, e8, e8] = 1
    arrays = {"x": xs.reshape(-1, DM), "w_in": w_in, "w_out": g("W_out"), "fc1": g("fc1_w"), "fc2": g("fc2_w"),
              "w12": w12, "w3": w3, "cst": cst, "rows": rows, "sel": sel.reshape(3 * NH, NH * P)}
    arrays = {k: np.ascontiguousarray(v) for k, v in arrays.items()}
    nc = _bacc.Bacc("TRN2", target_bir_lowering=False, num_devices=1)
    args = [nc.dram_tensor(n, v.shape, mybir.dt.from_np(v.dtype), kind="ExternalInput").ap() for n, v in arrays.items()]
    out = nc.dram_tensor("out", arrays["x"].shape, F32, kind="ExternalOutput").ap()
    build(nc, *args, out)
    got = _run(nc, [arrays], core_ids=[0])
    return got.results[0]["out"].reshape(xs.shape)
```

```python
from contextlib import ExitStack

import numpy as np
import concourse.bass as bass
from concourse import mybir

F32 = mybir.dt.float32
F32R = mybir.dt.float32r
BF16 = mybir.dt.bfloat16
I32 = mybir.dt.int32
U32 = mybir.dt.uint32
ALU = mybir.AluOpType
ACT = mybir.ActivationFunctionType
AX_X = mybir.AxisListType.X

P = 128
DM = 256
KD = DM // P
NH, HD, NG, JH = 8, 64, 2, 4
DI = NH * HD
XB = NG * HD
INTER = 1024
KF = INTER // P
CH = 4
TB = CH * P
NE, EI = 8, 176
NX = NE + 2
EK = EI // 2
EPS = 1e-5
XBD = 2 * XB + NH
A_MIN = -200.0
C_ID, C_INCL, C_AFTER, C_ONES, C_IOTA, C_FIRST, C_COLS, C_KEEP = 0, 128, 256, 384, 512, 640, 648, 664
NC_C = 672
HIGH = -(1 << 12)
WEIGHT_SPLITS = 3
R_DTB, R_ALOG, R_D, R_FB = 0, 8, 16, 24
NC_R = 24 + DM


class Chain:

    def __init__(self, eng, sem, per):
        self.eng, self.sem, self.per, self.base, self.n = eng, sem, per, 0, 0

    def start(self, base):
        self.base, self.n = base, 0

    def link(self, ins, carry=None):
        self.n += 1
        ins.then_inc(self.sem, 1)
        self.eng.wait_ge(self.sem, self.base + self.n)
        if carry is not None:
            self.eng.sem_inc(carry, 1)

    def mark(self, ins):
        self.n += 1
        ins.then_inc(self.sem, 1)

    def wait(self, carry=None):
        self.eng.wait_ge(self.sem, self.base + self.n)
        if carry is not None:
            self.eng.sem_inc(carry, 1)

    def end(self):
        assert self.n == self.per, self.n


def slot_tiles(tokens):
    most = (2 * tokens + NE * (P - 1)) // P
    return -(-most // 8) * 8


def build(nc, x, w_in, w_out, fc1, fc2, w12, w3, cst, rows, sel, out):
    NT = x.shape[0] // P
    NB = NT // CH
    W12N = w12.shape[1]
    HT = NT // 2
    SJ = slot_tiles(x.shape[0])
    SLOTS = (SJ + 8) * P
    xs_dram = nc.dram_tensor("slots_x", (SLOTS, DM), F32, kind="Internal").ap()
    eo_dram = nc.dram_tensor("slots_y", (SJ * P, DM), F32, kind="Internal").ap()

    with ExitStack() as ctx:
        def sb(name, shape, dt=F32):
            return ctx.enter_context(nc.sbuf_tensor(name, shape, dt))

        def bank(name):
            return ctx.enter_context(nc.psum_tensor(name, [P, 512], F32))

        def sem(name):
            return ctx.enter_context(nc.semaphore(name))

        xa = sb("xa", [P, NT + CH, DM])
        win_s = sb("win_s", [P, KD, XBD + P])
        late = sb("late", [P, 2 * NX * DM])
        fc2_s = late[:, 0:KF * DM].rearrange("p (k n) -> p k n", k=KF)
        wout_s = late[:, KF * DM:KF * DM + DI // P * DM].rearrange("p (k n) -> p k n", k=DI // P)
        w3_s = late[0:EK, :].rearrange("p (k n) -> p k n", k=2 * NX)
        SPLIT = [TB, DI, DI - P, INTER]
        with nc.sbuf_tensor("split_s", [P, 2 * KD * sum(SPLIT)], F32R) as split_s:
            at = [2 * KD * sum(SPLIT[:q]) for q in range(len(SPLIT) + 1)]
            hr, z_r, c_r, fc1_r = (split_s[:, at[q]:at[q + 1]].rearrange("p (a k n) -> p a k n", a=2, k=KD)
                                   for q in range(len(SPLIT)))
        w12_s = sb("w12_s", [P, KD, W12N])
        xf = sb("xf", [P, 2, 4, DM])
        rsm = sb("rsm", [P, 4, NT])
        cw = sb("cw", [P, 2, NT])
        posf = sb("posf", [P, 2, NT])
        pos = sb("pos", [P, 2, NT], I32)
        tl = sb("tl", [P, 5, NE])
        eidf = sb("eidf", [P, SJ + 4])
        eid = sb("eid", [P, SJ + 4], I32)
        posb = sb("posb", [P, 4, 2, 2], I32)
        nmf = sb("nmf", [P, NT + CH])
        st4 = sb("st4", [P, 2, 6])
        mv5 = sb("mv5", [P, 4, 2, 2])
        r5 = sb("r5", [P, 2, 4, 2])
        taken = KD * W12N + 8 * DM + 10 * NT + 5 * NE + 2 * (SJ + 4) + 16 + NT + CH + 12 + 32
        split_rest = sb("split_rest", [P, at[-1] - taken])
        gate_s = sb("gate_s", [P, KD, NE])
        cs = sb("cs", [P, NC_C])
        rw = sb("rw", [P, NC_R])
        sel_b = sb("sel_b", [3 * NH, NH, P], BF16)
        ident_b = sb("ident_b", [P, P], BF16)
        ident4 = sb("ident4", [P, CH, P])
        nhalf = sb("nhalf", [P, CH])
        keep = sb("keep", [P, NB], I32)
        a_neg = sb("a_neg", [P, NH])
        ident = cs[:, C_ID:C_ID + P]
        lnw, lnb = cs[:, C_COLS:C_COLS + 2], cs[:, C_COLS + 2:C_COLS + 4]
        nrw, f1b = cs[:, C_COLS + 4:C_COLS + 8], cs[:, C_COLS + 8:C_COLS + 16]

        st1 = sb("st1", [P, CH, 6])
        mvb = sb("mvb", [P, CH, 2])
        mv1 = sb("mv1", [P, NT + CH, 2])
        rs1 = sb("rs1", [P, NT + CH])
        nw = sb("nw", [P, 6, CH])
        v = sb("v", [P, CH, DM])
        hsT = sb("hsT", [P, KD, TB])
        high = sb("high", [P, 1], I32)
        xbd = sb("xbd", [P, CH, XBD])
        cT = sb("cT", [P, JH, TB])
        bT = sb("bT", [P, TB])
        sz = sb("sz", [P, CH, DI])
        mid = sb("mid", [P, 2 * KF * TB])
        gT = mid[:, 0:KF * TB].rearrange("p (f t) -> p f t", f=KF)
        sel_f = gT[0:3 * NH, 0:NH * P // TB, :].rearrange("p k t -> p (k t)")
        dtw = sb("dtw", [P, 14, CH, NH])
        parts = sb("parts", [P, CH, 3, NH], BF16)
        partsT = sb("partsT", [3 * NH, CH, P], BF16)
        pwd = sb("pwd", [P, 2, CH, NH])
        dec = sb("dec", [P, CH, JH])
        L = mid[:, KF * TB:].rearrange("p (h t) -> p h t", h=NH)
        xdt = sb("xdt", [P, 2, DI])
        xw = sb("xw", [P, 2, DI])
        dx = sb("dx", [P, DI])
        M = sb("M", [P, 2, NH, P])
        raw = mid[:, KF * TB:KF * TB + KD * sum(SPLIT[1:])]
        made = mid[:, NH * P:NH * P + KD * (SPLIT[1] + SPLIT[2])]
        two = lambda ap: ap.rearrange("p (k n) -> p k n", k=KD)
        z_w, c_w, fc1_w = (two(raw[:, o:o + KD * n]) for o, n in (
            (0, DI), (KD * DI, DI - P), (KD * (2 * DI - P), INTER)))
        weight_splits = [(z_w, two(made[:, 0:KD * DI]), z_r), (c_w, two(made[:, KD * DI:]), c_r),
                         (fc1_w, two(M[:].rearrange("p a h t -> p (a h t)")), fc1_r)]
        hs_made = M[:, 0].rearrange("p h t -> p (h t)").rearrange("p (k n) -> p k n", k=KD)
        S = sb("S", [P, JH, P])
        t1 = sb("t1", [P, DI])
        t2 = sb("t2", [P, DI])
        t3 = sb("t3", [P, DI])
        yg = sb("yg", [P, DI])
        ygn = sb("ygn", [P, DI])
        rr = sb("rr", [P, 4])
        ynT = sb("ynT", [P, DI // P, P])
        ub = sb("ub", [P, DM])
        o = sb("o", [P, DM])
        st3 = sb("st3", [P, 6])
        mv3 = sb("mv3", [P, 2])
        r3 = sb("r3", [P, 2])
        stf = sb("stf", [P, CH, 6])
        mvg = sb("mvg", [P, CH, 2])
        nf = sb("nf", [P, 2, CH])
        mvf_all = sb("mvf_all", [P, CH + NT + CH, 2])
        rsf_all = sb("rsf_all", [P, CH + NT + CH])
        mvf, rsf = mvf_all[:, CH:, :], rsf_all[:, CH:]
        zero = sb("zero", [P, 1, DM])
        Mf = M[:].rearrange("p a h t -> p (a h t)")
        xfT = Mf[:, 0:DM].rearrange("p (k t) -> p k t", k=KD)
        xsT = Mf[:, DM:3 * DM].rearrange("p (a k t) -> p a k t", a=2, k=KD)
        heT = Mf[0:EK, 3 * DM:5 * DM].rearrange("p (a k t) -> p a k t", a=2, k=2)
        hs_ = Mf[:, 5 * DM:5 * DM + 2 * EI].rearrange("p (a n) -> p a n", a=2)
        he = Mf[:, 5 * DM + 2 * EI:5 * DM + 4 * EI].rearrange("p (a n) -> p a n", a=2)
        ysh = mid[:, 0:HT * DM].rearrange("p (t d) -> p t d", t=HT)
        behind = mid[:, KF * TB:]
        xl = behind[:, 0:4 * DM].rearrange("p (s d) -> p s d", s=4)
        ob = behind[:, 4 * DM:8 * DM].rearrange("p (s d) -> p s d", s=4)
        acc = behind[:, 8 * DM:16 * DM].rearrange("p (u b d) -> p u b d", u=4, b=2)
        fT = [hsT, cT]
        RT = [sz[:].rearrange("p c d -> p (c d)")[:, q * NT * NE:(q + 1) * NT * NE] for q in range(8)]
        RC = [cT[:].rearrange("p c d -> p (c d)")[:, q * NT * NE:(q + 1) * NT * NE] for q in range(5)]
        gath = [part[:].rearrange("p c d -> p (c d)").rearrange("p (u b k d) -> p u b k d", u=2, b=2, k=2)[:, u]
                for part in (cT, sz) for u in range(2)]
        grid = cT[:].rearrange("p c d -> p (c d)")[:, 5 * NT * NE:5 * NT * NE + SJ * NE]

        W = [bank(f"W{k}") for k in range(3)]
        X = [bank(f"X{k}") for k in range(2)]
        Y, I, O = bank("Y"), bank("I"), bank("O")
        OB = [W[0], O]
        YO = [O, Y]

        s_x, s_cs, s_rw, s_sel, s_win = sem("s_x"), sem("s_cs"), sem("s_rw"), sem("s_sel"), sem("s_win")
        s_fc1, s_fc2, s_wout, s_w12, s_w3 = sem("s_fc1"), sem("s_fc2"), sem("s_wout"), sem("s_w12"), sem("s_w3")
        s_out = sem("s_out")
        dve_step, pool_step = sem("dve_step"), sem("pool_step")
        consts_ready, aneg_ready, dve_init, pool_init = sem("consts_ready"), sem("aneg_ready"), sem("dve_init"), sem("pool_init")
        mv_ready = sem("mv_ready")
        made_ready, lo_ready, hi_ready = sem("made_ready"), sem("lo_ready"), sem("hi_ready")
        carry = sem("carry")
        dve_st, pool_norm, rs1_ready, dx_ready = sem("dve_st"), sem("pool_norm"), sem("rs1_ready"), sem("dx_ready")
        vt_done, xb_done, ct_done, bt_done = sem("vt_done"), sem("xb_done"), sem("ct_done"), sem("bt_done")
        z_done, pt_done, cum_done, fc1_done = sem("z_done"), sem("pt_done"), sem("cum_done"), sem("fc1_done")
        bc_done, g_done, inter_done, inc_done = sem("bc_done"), sem("g_done"), sem("inter_done"), sem("inc_done")
        y_done, yt_done, o_done = sem("y_done"), sem("yt_done"), sem("o_done")
        st_ready, rs_ready, v_ready, hst_ready = sem("st_ready"), sem("rs_ready"), sem("v_ready"), sem("hst_ready")
        xb_ready, ct_ready, bt_ready, sz_ready = sem("xb_ready"), sem("ct_ready"), sem("bt_ready"), sem("sz_ready")
        na_ready, e_ready, w1_ready, ln_ready = sem("na_ready"), sem("e_ready"), sem("w1_ready"), sem("ln_ready")
        dt_ready, a_ready, da_ready = sem("dt_ready"), sem("a_ready"), sem("da_ready")
        parts_ready, pt_ready, pwd_ready = sem("parts_ready"), sem("pt_ready"), sem("pwd_ready")
        gelu_ready, scan_done, m_ready = sem("gelu_ready"), sem("scan_done"), sem("m_ready")
        xdt_ready, xw_ready, s_reset = sem("xdt_ready"), sem("xw_ready"), sem("s_reset")
        t1_done, t2_done, s_scaled, s_ready = sem("t1_done"), sem("t2_done"), sem("s_scaled"), sem("s_ready")
        yg_ready, ssq_ready, rr_ready = sem("yg_ready"), sem("ssq_ready"), sem("rr_ready")
        ygn_ready, ynt_ready, o_used, st3_ready, r3_ready = (
            sem("ygn_ready"), sem("ynt_ready"), sem("o_used"), sem("st3_ready"), sem("r3_ready"))
        zf_ready, s_zero, vf_ready, lg_done, lg_ready = sem("zf_ready"), sem("s_zero"), sem("vf_ready"), sem("lg_done"), sem("lg_ready")
        ft_done, ft_ready, mx_ready, ex_ready, mm_ready = sem("ft_done"), sem("ft_ready"), sem("mx_ready"), sem("ex_ready"), sem("mm_ready")
        stf_ready, rsf_ready, mvf_ready, rk_done, pos_ready, eid_ready = (
            sem("stf_ready"), sem("rsf_ready"), sem("mvf_ready"), sem("rk_done"), sem("pos_ready"), sem("eid_ready"))
        dve_route = sem("dve_route")
        posb_ready, ve5_ready, xg_ready = sem("posb_ready"), sem("ve5_ready"), sem("xg_ready")
        nmf_ready, ct2_ready = sem("nmf_ready"), sem("ct2_ready")
        s_scat = [[sem(f"s_scat{b}{q}") for q in range(4)] for b in range(2)]
        phase = []
        for ph in "bde":
            phase.append({n: sem(f"{n}_{ph}") for n in (
                "xt_done", "xt_ready", "h12_done", "silu_ready", "he_ready", "het_done", "het_ready",
                "y_done", "y_used") + {"b": ("xf_ready",), "d": (), "e": ("xf_ready", "step")}[ph]})
        s_load = [sem(f"s_load{k}") for k in range(4)]
        s_store = [sem(f"s_store{k}") for k in range(4)]
        s_gath = [[sem(f"s_gath{u}{b}") for b in range(2)] for u in range(4)]
        gath_used, st5_ready, r5_ready, out_ready = sem("gath_used"), sem("st5_ready"), sem("r5_ready"), sem("out_ready")

        x_d = x.rearrange("(t p) d -> p t d", p=P)
        out_d = out.rearrange("(t p) d -> p t d", p=P)
        SHARED = 2
        GATE = 2 * EI

        def col12(m):
            return m * 2 * EI + NE * (m > 0)

        xs_d = xs_dram.rearrange("(s p) d -> p s d", p=P)
        eo_d = eo_dram.rearrange("(s p) d -> p s d", p=P)

        block = ctx.enter_context(nc.Block())

        B, D, E = phase

        @block.sync
        def _(sp):
            sp.dma_start(cs[:], cst).then_inc(s_cs, 16)
            sp.dma_start(xa[:, 0:CH, :], x_d[:, 0:CH, :]).then_inc(s_x, 16)
            sp.wait_ge(s_x, 16)
            with sp.Fori(1, NB) as i:
                sp.dma_start(xa[:, bass.ts(i, CH), :], x_d[:, bass.ts(i, CH), :]).then_inc(s_x, 16)
                sp.wait_ge(s_x, i * 16 + 16)
                sp.sem_inc(carry, 1)
            sp.dma_start(xa[:, NT:NT + CH, :], x_d[:, 0:CH, :]).then_inc(s_x, 16)
            sp.wait_ge(zf_ready, 1)
            zr = SLOTS // P
            sp.dma_start(xs_dram.rearrange("(p r) d -> p r d", p=P), zero[:].broadcast_to([P, zr, DM])).then_inc(s_zero, 16)
            sp.wait_ge(o_done, NB * CH)
            sp.dma_start(w3_s, w3.rearrange("(k p) n -> p k n", p=EK)).then_inc(s_w3, 16)
            sp.wait_ge(lo_ready, NB + WEIGHT_SPLITS + 1)
            sp.wait_ge(hi_ready, NB + WEIGHT_SPLITS + 1)
            sp.dma_start(w12_s[:], w12.rearrange("(k p) n -> p k n", p=P)).then_inc(s_w12, 16)
            for landed in s_scat[0] + s_scat[1]:
                sp.wait_ge(landed, 32 * HT // 4)
            def load_slot(n, q):
                sp.dma_start(xl[:, q, :], xs_d[:, bass.ds(n, 1), :].rearrange("p s d -> p (s d)")).then_inc(s_load[q], 16)

            for n in range(4):
                load_slot(n, n)
            for n in range(4, 7):
                sp.wait_ge(D["xt_done"], n - 3)
                load_slot(n, n - 4)
            with sp.Fori(0, SJ // 4) as j:
                for q in range(4):
                    n = j * 4 + q
                    sp.wait_ge(D["xt_done"], n + 4)
                    load_slot(n + 7, (q + 3) % 4)
                    sp.wait_ge(D["y_used"], n + 3)
                    sp.dma_start(eo_d[:, bass.ds(n, 1), :].rearrange("p s d -> p (s d)"), ob[:, q, :]).then_inc(s_store[q], 16)
            with sp.Fori(0, HT) as j:
                sp.wait_ge(out_ready, j * 2 + 2)
                sp.sem_inc(carry, 1)
                for b in range(2):
                    sp.dma_start(out_d[:, bass.ds(b * HT + j, 1), :].rearrange("p s d -> p (s d)"),
                                 xa[:, bass.ds(b * HT + j, 1), :].rearrange("p s d -> p (s d)")).then_inc(s_out, 16)
            sp.wait_ge(s_out, 16 * NT)

        @block.tensor
        def _(pe):
            def x_to_v(k, bk):
                for c in range(CH):
                    mm = pe.transpose(bk[:, c * P:(c + 1) * P], v[:, c, k * P:(k + 1) * P], ident)
                mm.then_inc(vt_done, 1)

            def scores(i, c, g):
                n = 2 * c + g
                w = W[n % 2 + 1]
                if n >= 2:
                    pe.wait_ge(m_ready, i * 8 + n - 1)
                mm = pe.matmul(w[:, :], bT[g * HD:(g + 1) * HD, c * P:(c + 1) * P],
                               cT[g * HD:(g + 1) * HD, :, c * P:(c + 1) * P], start=True, stop=True)
                mm.then_inc(g_done, 1)

            def yT(i, c):
                pe.wait_ge(ygn_ready, i * 4 + c + 1)
                bk = X[0] if c < 3 else W[2]
                for k in range(DI // P):
                    mm = pe.transpose(bk[:, k * P:(k + 1) * P], ygn[:, k * P:(k + 1) * P], ident)
                mm.then_inc(yt_done, 1)

            def out_proj(i, c):
                pe.wait_ge(ynt_ready, i * 4 + c + 1)
                for k in range(DI // P):
                    mm = pe.matmul(OB[c % 2][:, 0:DM], ynT[:, k, :], wout_s[:, k, :], start=False, stop=(k == DI // P - 1))
                mm.then_inc(o_done, 1)

            def xbd_of(n, c):
                for k in range(KD):
                    mm = pe.matmul(X[c % 2][:, 0:XBD], hsT[:, k, c * P:(c + 1) * P],
                                   win_s[:, k, 0:XBD], start=(k == 0), stop=(k == KD - 1))
                mm.then_inc(xb_done, 1)

            def three(bk, pairs):
                for k, (a, a_lo, b, b_lo) in enumerate(pairs):
                    pe.matmul(bk[:, :], a, b, start=(k == 0), stop=False)
                    pe.matmul(bk[:, :], a_lo, b, start=False, stop=False)
                    mm = pe.matmul(bk[:, :], a, b_lo, start=False, stop=(k == KD - 1))
                return mm

            def by_weights(w, n):
                return [(w[:, 0, k, n], w[:, 1, k, n], hr[:, 0, k, :], hr[:, 1, k, :]) for k in range(KD)]

            def ct_of(n, j):
                if j > 0:
                    three(W[j % 3], by_weights(c_r, slice((j - 1) * P, j * P))).then_inc(ct_done, 1)
                    return
                for k in range(KD):
                    mm = pe.matmul(W[j % 3][:, :], win_s[:, k, XBD:XBD + P],
                                   hsT[:, k, :], start=(k == 0), stop=(k == KD - 1))
                mm.then_inc(ct_done, 1)

            pe.wait_ge(s_cs, 16)
            pe.wait_ge(v_ready, CH)
            x_to_v(0, X[1])
            x_to_v(1, X[0])
            pe.wait_ge(s_win, 48)
            pe.wait_ge(consts_ready, 1)
            pe.wait_ge(hst_ready, 2)
            xbd_of(0, 0)
            xbd_of(0, 1)
            ct_of(0, 0)
            with pe.Fori(0, NB) as i:
                for c in range(2, CH):
                    pe.wait_ge(xb_ready, i * 4 + c - 1)
                    xbd_of(i, c)
                pe.wait_ge(lo_ready, i + WEIGHT_SPLITS + 1)
                pe.wait_ge(hi_ready, i + WEIGHT_SPLITS + 1)
                for j in range(1, JH):
                    if j == 3:
                        pe.wait_ge(ct_ready, i * 3 + 1)
                    ct_of(i, j)
                pe.wait_ge(xb_ready, i * 4 + 4)
                for c in range(CH):
                    mm = pe.transpose(X[0][:, c * P:(c + 1) * P], xbd[:, c, XB:2 * XB], ident)
                mm.then_inc(bt_done, 1)
                for c in range(CH):
                    if c == 1:
                        pe.wait_ge(ct2_ready, i + 1)
                    elif c < CH - 1:
                        pe.wait_ge(ct_ready, i * 3 + (2 if c == 0 else 3))
                    if c == 3:
                        pe.wait_ge(sz_ready, i * 4 + 1)
                    t = slice(c * P, (c + 1) * P)
                    three(W[(c + 1) % 3], [(hr[:, 0, k, t], hr[:, 1, k, t], z_r[:, 0, k, :], z_r[:, 1, k, :])
                                           for k in range(KD)]).then_inc(z_done, 1)
                    if c == 2:
                        pe.wait_ge(parts_ready, i + 1)
                        ptb = X[1][:, :].bitcast(BF16)
                        for q in range(CH):
                            mm = pe.transpose(ptb[0:3 * NH, q * P:(q + 1) * P], parts[:, q, :, :].rearrange("p a h -> p (a h)"), ident_b[:])
                        mm.then_inc(pt_done, 1)
                        pe.wait_ge(bt_ready, i + 1)
                        for q, col in enumerate((C_INCL, C_AFTER, C_ONES)):
                            mm = pe.matmul(X[0][:, q * 32:(q + 1) * 32], cs[:, col:col + P], dtw[:, 12, :, :],
                                           start=True, stop=True)
                        mm.then_inc(cum_done, 1)
                pe.wait_ge(s_fc1, 16)
                for f in range(KF):
                    if f < 3:
                        pe.wait_ge(sz_ready, i * 4 + f + 2)
                    else:
                        pe.wait_ge(gelu_ready, i * 8 + f - 2)
                    three(W[(f + 2) % 3], by_weights(fc1_r, slice(f * P, (f + 1) * P))).then_inc(fc1_done, 1)
                    if f == 0:
                        pe.wait_ge(pt_ready, i + 1)
                    if f == 1:
                        pe.wait_ge(pwd_ready, i * 3 + 3)
                    if f >= 2:
                        pe.wait_ge(scan_done, i * 8 + f - 1)
                    pe.matmul(X[(f + 1) % 2][:, :], sel_b[:, f, :], partsT[:, :, :].rearrange("p c t -> p (c t)"),
                              start=True, stop=True).then_inc(bc_done, 1)
                pe.wait_ge(s_fc2, 16)
                pe.wait_ge(s_wout, 16)
                pe.wait_ge(gelu_ready, i * 8 + 6)
                scores(i, 0, 0)
                pe.wait_ge(gelu_ready, i * 8 + 7)
                scores(i, 0, 1)
                for c in range(CH):
                    if c == 0:
                        pe.wait_ge(s_reset, i + 1)
                    else:
                        pe.wait_ge(s_ready, i * 8 + 2 * c)
                        pe.wait_ge(t1_done, i * 4 + c)
                    for j in range(JH):
                        mm = pe.matmul(I[:, j * P:(j + 1) * P], cT[:, j, c * P:(c + 1) * P], S[:, j, :],
                                       start=True, stop=True)
                    mm.then_inc(inter_done, 1)
                    pe.wait_ge(xw_ready, i * 4 + c + 1)
                    if c == 0:
                        pe.wait_ge(scan_done, i * 8 + 8)
                    for g in range(NG):
                        mm = pe.matmul(X[1][g * HD:(g + 1) * HD, 0:JH * HD],
                                       xbd[:, c, XB + g * HD:XB + (g + 1) * HD],
                                       xw[:, c % 2, g * JH * HD:(g + 1) * JH * HD], start=True, stop=True)
                    mm.then_inc(inc_done, 1)
                    if c == CH - 1:
                        yT(i, c - 1)
                    pe.wait_ge(m_ready, i * 8 + 2 * c + 2)
                    if c > 0:
                        pe.wait_ge(t2_done, i * 4 + c)
                    for h, at in ((0, 0), (1, 1), (2, 2), (3, 3), (7, 6), (6, 5), (5, 4), (4, None)):
                        lo, n = (h, 1) if at is None else (at, 2)
                        mm = pe.matmul(Y[:, lo * HD:(lo + n) * HD], M[:, c % 2, h, :],
                                       xdt[:, c % 2, lo * HD:(lo + n) * HD], start=True, stop=True)
                    mm.then_inc(y_done, 1)
                    if c == CH - 1:
                        pe.wait_ge(v_ready, i * 4 + 8)
                        pe.wait_ge(s_ready, i * 8 + 8)
                        x_to_v(0, X[1])
                        out_proj(i, c - 1)
                        x_to_v(1, X[0])
                    else:
                        if c > 0:
                            yT(i, c - 1)
                        scores(i, c + 1, 0)
                        scores(i, c + 1, 1)
                        if c > 0:
                            out_proj(i, c - 1)
                    if c == 0:
                        pe.wait_ge(gelu_ready, i * 8 + 8)
                    if c >= 2:
                        pe.wait_ge(o_used, i * 4 + c - 1)
                    for k in range(KF):
                        mm = pe.matmul(OB[c % 2][:, 0:DM], gT[:, k, c * P:(c + 1) * P], fc2_s[:, k, :],
                                       start=(k == 0), stop=False)
                pe.wait_ge(hst_ready, i * 2 + 4)
                xbd_of(i + 1, 0)
                xbd_of(i + 1, 1)
                yT(i, 3)
                pe.wait_ge(o_used, i * 4 + 3)
                ct_of(i + 1, 0)
                out_proj(i, 3)

            def turn_block(n):
                pe.wait_ge(vf_ready, n * 4 + 4)
                for k in range(KD):
                    for c in range(CH):
                        mm = pe.transpose(X[1 - k][:, c * P:(c + 1) * P], v[:, c, k * P:(k + 1) * P], ident)
                    mm.then_inc(ft_done, 1)

            def router(n, u):
                pe.wait_ge(ft_ready, n * 2 + 2)
                for c in range(CH):
                    for k in range(KD):
                        mm = pe.matmul(W[0][:, bass.ds((n * CH + c) * NE, NE)], fT[u][:, k, c * P:(c + 1) * P],
                                       gate_s[:, k, :], start=(k == 0), stop=(k == KD - 1))
                mm.then_inc(lg_done, 1)

            turn_block(0)
            pe.wait_ge(s_sel, 32)
            with pe.Fori(0, NB // 2 - 1) as i:
                for u in range(2):
                    pe.wait_ge(ft_ready, (i * 2 + u) * 2 + 2)
                    turn_block(i * 2 + u + 1)
                    router(i * 2 + u, u)
            pe.wait_ge(ft_ready, (NB - 2) * 2 + 2)
            turn_block(NB - 1)
            router(NB - 2, 0)
            router(NB - 1, 1)

            def first(S_, n, bk, xT, cols, w):
                for k in range(KD):
                    mm = pe.matmul(bk[:, 0:w], xT[:, k, :], w12_s[:, k, cols], start=(k == 0), stop=(k == KD - 1))
                mm.then_inc(S_["h12_done"], 1)

            def turn(S_, n, a):
                pe.wait_ge(S_["he_ready"], n)
                for k in range(2):
                    mm = pe.transpose(X[a][0:EK, k * P:(k + 1) * P], he[:, a, k * EK:(k + 1) * EK], ident)
                mm.then_inc(S_["het_done"], 1)

            def turn_x(S_, n, src):
                pe.wait_ge(S_["xf_ready"], n)
                for k in range(KD):
                    mm = pe.transpose(I[:, k * P:(k + 1) * P], src[:, k * P:(k + 1) * P], ident)
                mm.then_inc(S_["xt_done"], 1)

            def half_first(S_, m):
                first(S_, None, W[m], xfT, slice(col12(m), col12(m) + 2 * EI), 2 * EI)

            def shared(S_, meanwhile=None):
                turn_x(S_, 1, xf[:, 0, 0, :])
                pe.wait_ge(S_["xt_ready"], 1)
                half_first(S_, 0)
                half_first(S_, 1)
                if meanwhile is not None:
                    meanwhile()
                turn(S_, 1, 0)
                turn_x(S_, 2, xf[:, 0, 1, :])
                with pe.Fori(0, HT // 4) as r:
                    for q in range(4):
                        j = r * 4 + q
                        pe.wait_ge(S_["xt_ready"], j + 2)
                        pe.wait_ge(S_["he_ready"], j * 2 + 1)
                        half_first(S_, 0)
                        pe.wait_ge(S_["het_ready"], j * 2 + 1)
                        turn(S_, j * 2 + 2, 1)
                        pe.wait_ge(S_["y_used"], j + 1)
                        for k in range(2):
                            pe.matmul(YO[q % 2][:, 0:DM], heT[:, 0, k, :], w3_s[:, k, :], start=(k == 0), stop=False)
                        pe.wait_ge(S_["het_ready"], j * 2 + 2)
                        half_first(S_, 1)
                        turn_x(S_, j + 3, xf[:, 0, (q + 2) % 4, :])
                        turn(S_, j * 2 + 3, 0)
                        for k in range(2):
                            mm = pe.matmul(YO[q % 2][:, 0:DM], heT[:, 1, k, :], w3_s[:, 2 + k, :], start=False, stop=(k == 1))
                        mm.then_inc(S_["y_done"], 1)

            def ranks():
                pe.wait_ge(mm_ready, 1)
                pe.matmul(Y[:, 0:NT * NE], cs[:, C_INCL:C_INCL + P], RT[7], start=True, stop=True).then_inc(rk_done, 1)
                pe.matmul(W[2][:, 0:NT * NE], cs[:, C_ONES:C_ONES + P], RT[7], start=True, stop=True).then_inc(rk_done, 1)

            def banks_free(S_, tiles, firsts):
                pe.wait_ge(S_["he_ready"], firsts)
                pe.wait_ge(S_["het_ready"], firsts - 1)
                pe.wait_ge(S_["y_used"], tiles + 2)

            pe.wait_ge(lg_ready, 1)
            pe.wait_ge(s_w3, 16)
            pe.wait_ge(s_w12, 16)
            shared(B, ranks)
            banks_free(B, HT, 2 * HT + 2)
            pe.wait_ge(B["xt_ready"], HT + 2)

            def expert_of(n):
                return pe.value_load(eid[0:1, bass.ds(n, 1)], min_val=0, max_val=NE - 1)

            def eid_first(e, q):
                first(D, n, W[q % 2], xsT[:, q % 2], bass.ds(e * (2 * EI) + col12(SHARED), 2 * EI), 2 * EI)

            pe.wait_ge(eid_ready, 1)
            pe.wait_ge(s_load[0], 16)
            for q in range(3):
                pe.wait_ge(s_load[q], 16)
                for k in range(KD):
                    mm = pe.transpose(I[:, k * P:(k + 1) * P], xl[:, q, k * P:(k + 1) * P], ident)
                mm.then_inc(D["xt_done"], 1)
                e = expert_of(q)
                pe.wait_ge(D["xt_ready"], q + 1)
                if q == 2:
                    pe.wait_ge(D["he_ready"], 1)
                eid_first(e, q)
            turn(D, 1, 0)
            held = [pe.alloc_register(f"expert{k}") for k in range(3)]

            def held_value(k):
                return pe.snap(held[k]).with_bounds(min_val=0, max_val=NE - 1)

            for k in range(3):
                pe.reg_load(held[k], eid[0:1, k:k + 1])
            with pe.Fori(0, SJ // 8) as j:
                es = {k: held_value(k) for k in range(3)}
                for q in range(8):
                    n = j * 8 + q
                    e = es[q]
                    if q + 3 < 8:
                        e3 = es[q + 3] = expert_of(n + 3)
                    else:
                        pe.reg_load(held[q + 3 - 8], eid[0:1, bass.ds(n + 3, 1)])
                        e3 = held_value(q + 3 - 8)
                    pe.wait_ge(s_load[(q + 3) % 4], j * 32 + 16 * ((q + 3) // 4 + 1))
                    for k in range(KD):
                        mm = pe.transpose(I[:, k * P:(k + 1) * P], xl[:, (q + 3) % 4, k * P:(k + 1) * P], ident)
                    mm.then_inc(D["xt_done"], 1)
                    pe.wait_ge(D["het_ready"], n + 1)
                    turn(D, n + 2, (q + 1) % 2)
                    pe.wait_ge(D["y_used"], n + 1)
                    for k in range(2):
                        mm = pe.matmul(YO[q % 2][:, 0:DM], heT[:, q % 2, k, :],
                                       w3_s[:, bass.ds(e * 2 + 2 * SHARED + k, 1), :].rearrange("p s d -> p (s d)"),
                                       start=(k == 0), stop=(k == 1))
                    mm.then_inc(D["y_done"], 1)
                    pe.wait_ge(D["xt_ready"], n + 4)
                    pe.wait_ge(D["he_ready"], n + 2)
                    eid_first(e3, q + 3)
            banks_free(D, SJ, SJ + 2)
            pe.wait_ge(D["xt_ready"], SJ + 3)
            shared(E)

        @block.vector
        def _(dve):
            ch = Chain(dve, dve_step, 37)

            def norm(i, n):
                dve.wait_ge(s_x, n * 16 + 16)
                for c in range(CH):
                    dve.bn_stats(st1[:, c, :], xa[:, n * CH + c, :]).then_inc(dve_st, 1)
                dve.wait_ge(dve_st, n * 4 + 4)
                dve.sem_inc(carry, 1)
                for c in range(CH):
                    dve.bn_aggr(mvb[:, c, :], st1[:, c, :]).then_inc(st_ready, 1)
                dve.wait_ge(st_ready, n * 4 + 4)
                dve.tensor_copy(mv1[:, bass.ts(n, CH), :], mvb[:]).then_inc(mv_ready, 1)

            def second_stats(n):
                for c in range(CH):
                    dve.bn_aggr(mvg[:, c, :], stf[:, c, :]).then_inc(stf_ready, 1)
                dve.wait_ge(stf_ready, n * 4 + 4)
                dve.tensor_copy(mvf_all[:, bass.ds(n * CH, CH), :], mvg[:]).then_inc(mvf_ready, 1)

            def norm_out(n):
                dve.wait_ge(mv_ready, n + 1)
                dve.wait_ge(rs_ready, n + 1)
                for c in range(CH):
                    dve.tensor_scalar(v[:, c, :], xa[:, n * CH + c, :], mv1[:, n * CH + c, 0:1], nw[:, 5, c:c + 1],
                                      ALU.subtract, ALU.mult).then_inc(v_ready, 1)

            norm(0, 0)
            dve.wait_ge(s_cs, 16)
            dve.wait_ge(s_sel, 32)
            dve.tensor_copy(sel_b[:, :, :].rearrange("p h m -> p (h m)"), sel_f).then_inc(dve_init, 1)
            dve.tensor_copy(ident_b[:], ident).then_inc(dve_init, 1)
            for c in range(CH):
                dve.tensor_copy(ident4[:, c, :], ident).then_inc(dve_init, 1)
            dve.memset(S[:], 0.0).then_inc(dve_init, 1)
            dve.memset(partsT[:, :, 0:1], 0.0).then_inc(dve_init, 1)
            dve.wait_ge(aneg_ready, 1)
            dve.tensor_scalar(a_neg[:], a_neg[:], -1.0, None, ALU.mult).then_inc(dve_init, 1)
            dve.tensor_scalar(keep[:], cs[:, C_KEEP:C_KEEP + NB], -1.0, None, ALU.mult).then_inc(dve_init, 1)
            dve.memset(mvf[:, NT:, :], 0.0).then_inc(dve_init, 1)
            dve.memset(rsf[:, NT:], 0.0).then_inc(dve_init, 1)
            dve.memset(high[:], HIGH).then_inc(dve_init, 1)
            dve.memset(stf[:], 1.0).then_inc(dve_init, 1)
            dve.memset(zero[:], 0.0).then_inc(zf_ready, 1)
            dve.wait_ge(dve_init, 14)
            dve.memset(st3[:, 0:1], 0.0).then_inc(consts_ready, 1)
            norm_out(0)

            def take_xbd(n, c):
                dve.wait_ge(xb_done, n * 4 + c + 1)
                dve.tensor_copy(xbd[:, c, :], X[c % 2][:, 0:XBD]).then_inc(xb_ready, 1)

            def take_ct(n, j):
                dve.wait_ge(ct_done, n * 4 + j + 1)
                dve.tensor_copy(cT[:, j, :], W[j % 3][:, :]).then_inc(ct_ready, 1)

            def split(src, made, two_parts, n):
                cols = src.shape[2]
                dve.tensor_tensor(made.bitcast(I32), src.bitcast(I32), high[:].unsqueeze(2).broadcast_to([P, KD, cols]),
                                  ALU.bitwise_and).then_inc(made_ready, 1)
                dve.wait_ge(made_ready, n + 1)
                dve.tensor_tensor(two_parts[:, 1], src, made, ALU.subtract).then_inc(lo_ready, 1)

            for n in range(WEIGHT_SPLITS):
                dve.wait_ge(*((s_fc1, 16) if n == 2 else (s_win, 48)))
                split(*weight_splits[n], n)
            take_xbd(0, 0)
            take_xbd(0, 1)
            dve.wait_ge(hst_ready, 2)
            dve.wait_ge(hi_ready, WEIGHT_SPLITS)
            split(hsT[:], hs_made, hr, WEIGHT_SPLITS)
            take_ct(0, 0)
            with dve.Fori(0, NB) as i:
                ch.start(i * ch.per)
                for c in range(2, CH):
                    take_xbd(i, c)
                dve.wait_ge(xb_ready, i * 4 + 4)
                V = [dtw[:, q, :, :] for q in range(14)]
                ch.link(dve.tensor_tensor(V[0], xbd[:, :, 2 * XB:XBD],
                                          rw[:, R_DTB:R_DTB + NH].unsqueeze(1).broadcast_to([P, CH, NH]), ALU.add))
                dve.scalar_tensor_tensor(V[1], V[0], -1.0, V[0], ALU.mult, ALU.min).then_inc(na_ready, 1)
                take_ct(i, 1)
                dve.wait_ge(e_ready, i + 1)
                dve.tensor_scalar(V[3], V[2], 1.0, None, ALU.add).then_inc(w1_ready, 1)
                dve.wait_ge(w1_ready, i + 1)
                ch.link(dve.tensor_scalar(V[4], V[3], -1.0, None, ALU.add))
                ch.link(dve.tensor_scalar(V[5], V[4], 0.0, None, ALU.is_equal))
                ch.link(dve.tensor_tensor(V[6], V[4], V[5], ALU.add))
                ch.link(dve.reciprocal(V[7], V[6]))
                ch.link(dve.tensor_tensor(V[8], V[2], V[7], ALU.mult))
                dve.wait_ge(ln_ready, i + 1)
                ch.link(dve.tensor_tensor(V[9], V[13], V[5], ALU.add))
                ch.link(dve.tensor_tensor(V[10], V[8], V[9], ALU.mult))
                dve.scalar_tensor_tensor(V[11], V[0], 0.0, V[10], ALU.max, ALU.add).then_inc(dt_ready, 1)
                dve.wait_ge(dt_ready, i + 1)
                ch.link(dve.tensor_tensor(V[9], V[11], a_neg[:].unsqueeze(1).broadcast_to([P, CH, NH]), ALU.mult))
                dve.tensor_scalar(V[12], V[9], A_MIN, None, ALU.max).then_inc(a_ready, 1)
                take_ct(i, 3)
                dve.wait_ge(da_ready, i + 1)
                ch.link(dve.tensor_copy(parts[:, :, 0, :], V[4]))
                ch.link(dve.tensor_tensor(V[6], V[4], parts[:, :, 0, :], ALU.subtract))
                ch.link(dve.tensor_copy(parts[:, :, 1, :], V[6]))
                ch.link(dve.tensor_tensor(V[7], V[6], parts[:, :, 1, :], ALU.subtract))
                dve.tensor_copy(parts[:, :, 2, :], V[7]).then_inc(parts_ready, 1)
                dve.wait_ge(pt_done, i + 1)
                ptv = X[1][:, :].bitcast(BF16)[0:3 * NH, 0:TB].rearrange("p (c t) -> p c t", c=CH)
                dve.tensor_copy(partsT[:, :, 1:P], ptv[:, :, 1:P]).then_inc(pt_ready, 1)
                norm(i, i + 1)
                second_stats(i)
                for h in range(NH):
                    dve.wait_ge(bc_done, i * 8 + h + 1)
                    dve.tensor_tensor_scan(L[:, h, :], X[(h + 1) % 2][:, :], ident4[:, :, :].rearrange("p c t -> p (c t)"),
                                           0.0, ALU.mult, ALU.add).then_inc(scan_done, 1)
                dve.tensor_tensor(S[:].bitcast(I32).rearrange("p j m -> p (j m)"), S[:].bitcast(I32).rearrange("p j m -> p (j m)"),
                                  keep[:, bass.ds(i, 1)].broadcast_to([P, JH * P]),
                                  ALU.bitwise_and).then_inc(s_reset, 1)

                def mask(c, g):
                    dve.wait_ge(g_done, i * 8 + 2 * c + g + 1)
                    if c == 0 and g == 0:
                        dve.wait_ge(scan_done, i * 8 + 8)
                        dve.wait_ge(hi_ready, i + WEIGHT_SPLITS + 1)
                    if c >= 2:
                        dve.wait_ge(y_done, i * 4 + c - 1)
                    dve.tensor_tensor(M[:, c % 2, g * JH:(g + 1) * JH, :],
                                      W[(2 * c + g) % 2 + 1][:, :].rearrange("p (h t) -> p h t", h=JH),
                                      L[:, g * JH:(g + 1) * JH, c * P:(c + 1) * P], ALU.mult).then_inc(m_ready, 1)

                def finish_a(c):
                    t = i * CH + c
                    ch.link(dve.tensor_scalar(ub[:], xa[:, t, :], mv1[:, t, 0:1], rs1[:, bass.ds(t, 1)],
                                              ALU.subtract, ALU.mult))
                    ch.link(dve.tensor_tensor(ub[:], ub[:], rw[:, R_FB:R_FB + DM], ALU.add))
                    dve.wait_ge(o_done, i * 4 + c + 1)
                    dve.tensor_tensor(o[:], OB[c % 2][:, 0:DM], ub[:], ALU.add).then_inc(o_used, 1)
                    dve.wait_ge(o_used, i * 4 + c + 1)
                    ch.link(dve.bn_stats(st3[:], o[:]), carry)
                    dve.bn_aggr(mv3[:], st3[:]).then_inc(st3_ready, 1)

                def finish_b(c):
                    t = i * CH + c
                    dve.wait_ge(r3_ready, i * 4 + c + 1)
                    ch.link(dve.tensor_scalar(ub[:], o[:], mv3[:, 0:1], r3[:, 1:2], ALU.subtract, ALU.mult))
                    ch.link(dve.tensor_tensor(xa[:, t, :], xa[:, t, :], ub[:], ALU.add), carry)
                    ch.link(dve.bn_stats(stf[:, c, :], xa[:, t, :]))

                mask(0, 0)
                mask(0, 1)
                for c in range(CH):
                    dve.wait_ge(inter_done, i * 4 + c + 1)
                    dve.wait_ge(pwd_ready, i * 3 + 3)
                    if c > 0:
                        dve.wait_ge(t2_done, i * 4 + c)
                    dve.tensor_tensor(
                        t1[:].rearrange("p (g j d) -> p g j d", g=NG, j=JH),
                        I[:, :].rearrange("p (j g d) -> p g j d", g=NG, j=JH),
                        pwd[:, 0, c, :].rearrange("p (g j) -> p g j", g=NG).unsqueeze(3).broadcast_to([P, NG, JH, HD]),
                        ALU.mult).then_inc(t1_done, 1)
                    dve.wait_ge(inc_done, i * 4 + c + 1)
                    dve.wait_ge(s_scaled, i * 4 + c + 1)
                    for g in range(NG):
                        q = slice(g * HD, (g + 1) * HD)
                        dve.tensor_tensor(S[q, :, g * HD:(g + 1) * HD], S[q, :, g * HD:(g + 1) * HD],
                                          X[1][q, 0:JH * HD].rearrange("p (j d) -> p j d", j=JH),
                                          ALU.add).then_inc(s_ready, 1)
                    dve.wait_ge(y_done, i * 4 + c + 1)
                    dve.wait_ge(t1_done, i * 4 + c + 1)
                    if c > 0:
                        dve.wait_ge(yg_ready, i * 4 + c)
                    dve.tensor_tensor(t2[:], t1[:], Y[:, :], ALU.add).then_inc(t2_done, 1)
                    if c > 0:
                        finish_a(c - 1)
                    if c < CH - 1:
                        mask(c + 1, 0)
                        mask(c + 1, 1)
                    if c == 0:
                        norm_out(i + 1)
                    else:
                        finish_b(c - 1)
                take_xbd(i + 1, 0)
                take_xbd(i + 1, 1)
                dve.wait_ge(hst_ready, i * 2 + 4)
                split(hsT[:], hs_made, hr, i + WEIGHT_SPLITS + 1)
                take_ct(i + 1, 0)
                finish_a(CH - 1)
                finish_b(CH - 1)
                ch.end()

            for S_ in phase:
                dve.sem_inc(S_["y_used"], 2)
            def normed(n):
                dve.wait_ge(rsf_ready, n + 2)
                for c in range(CH):
                    t = n * CH + c
                    dve.tensor_scalar(v[:, c, :], xa[:, t, :], mvf[:, t, 0:1], rsf[:, bass.ds(t, 1)],
                                      ALU.subtract, ALU.mult).then_inc(vf_ready, 1)

            normed(0)
            second_stats(NB)
            with dve.Fori(1, NB) as i:
                dve.wait_ge(ft_done, i * 2)
                normed(i)

            def x_to_xf(S_, t, b, s):
                dve.tensor_scalar(xf[:, b, s, :], xa[:, t, :], mvf[:, t, 0:1], rsf[:, bass.ds(t, 1)],
                                  ALU.subtract, ALU.mult).then_inc(xg_ready if b else S_["xf_ready"], 1)

            dve.wait_ge(mvf_ready, NB + 1)
            dve.scalar_tensor_tensor(nmf[:], mvf[:, :, 0], -1.0, rsf[:], ALU.mult, ALU.mult).then_inc(nmf_ready, 1)
            x_to_xf(B, 0, 0, 0)
            x_to_xf(B, 1, 0, 1)
            x_to_xf(B, HT, 1, 0)
            dve.wait_ge(lg_done, NB)
            dve.tensor_copy(RT[0], W[0][:, 0:NT * NE]).then_inc(lg_ready, 1)
            dve.wait_ge(lg_ready, 1)
            def gate(S_, a, n):
                dve.wait_ge(S_["silu_ready"], n)
                dve.tensor_tensor(he[:, a, :], hs_[:, a, :], W[a][:, EI:2 * EI], ALU.mult).then_inc(S_["he_ready"], 1)

            rc = Chain(dve, dve_route, 31)
            link = rc.link
            te = lambda ap: ap.rearrange("p (t e) -> p t e", e=NE)
            by_t = lambda ap: ap.unsqueeze(2).broadcast_to([P, NT, NE])
            first8 = cs[:, C_FIRST:C_FIRST + NE].unsqueeze(1).broadcast_to([P, NT, NE])
            LG, PR, EQ, KY, OH0, OH1, PM, MM = RT
            TOT, INC, RST, OFF, POSA = RC
            et = lambda ap: ap.rearrange("p (e t) -> p e t", e=NE)
            cnt, tiles, ends, starts, one = (tl[:, q, :] for q in range(5))
            link(dve.tensor_reduce(rsm[:, 0, :], te(LG), AX_X, ALU.max))
            dve.tensor_tensor(te(PM), te(LG), by_t(rsm[:, 0, :]), ALU.subtract).then_inc(mx_ready, 1)
            rc.mark(dve.memset(one, 1.0))
            rc.mark(dve.memset(RST, 1.0))
            rc.wait()
            rc.mark(dve.memset(et(RST)[:, :, 0:1], 0.0))
            dve.wait_ge(ex_ready, 1)
            link(dve.tensor_reduce(rsm[:, 1, :], te(EQ), AX_X, ALU.add))
            link(dve.reciprocal(rsm[:, 2, :], rsm[:, 1, :]))
            link(dve.tensor_tensor(te(PR), te(EQ), by_t(rsm[:, 2, :]), ALU.mult))

            def pick(k, src, mark):
                link(dve.tensor_reduce(cw[:, k, :], te(src), AX_X, ALU.max))
                link(dve.tensor_tensor(te(EQ), te(src), by_t(cw[:, k, :]), ALU.is_equal))
                link(dve.tensor_tensor(te(KY), te(EQ), first8, ALU.mult))
                link(dve.tensor_reduce(rsm[:, 3, :], te(KY), AX_X, ALU.max))
                link(dve.tensor_tensor(te(mark), first8, by_t(rsm[:, 3, :]), ALU.is_equal))

            pick(0, PR, OH0)
            link(dve.scalar_tensor_tensor(PM, OH0, -4.0, PR, ALU.mult, ALU.add))
            pick(1, PM, OH1)
            dve.tensor_tensor(MM, OH0, OH1, ALU.add).then_inc(mm_ready, 1)
            gate(B, 0, 1)
            gate(B, 1, 2)
            dve.wait_ge(rk_done, 2)
            link(dve.tensor_copy(et(TOT), W[2][:, 0:NT * NE].rearrange("p (t e) -> p e t", e=NE)))
            link(dve.tensor_tensor_scan(INC, RST, TOT, 0.0, ALU.mult, ALU.add))
            link(dve.tensor_scalar(cnt, et(INC)[:, :, NT - 1], 1.0 / P, None, ALU.mult))
            iota = cs[:, C_IOTA:C_IOTA + P]
            KT = x.shape[0] // P
            g1 = grid[:, 0:NE * KT].rearrange("p (e k) -> p e k", e=NE)
            link(dve.tensor_tensor(g1, cnt.unsqueeze(2).broadcast_to([P, NE, KT]),
                                   iota[:, 0:KT].unsqueeze(1).broadcast_to([P, NE, KT]), ALU.is_gt))
            link(dve.tensor_reduce(tiles, g1, AX_X, ALU.add))
            link(dve.tensor_tensor_scan(ends, one, tiles, 0.0, ALU.mult, ALU.add))
            link(dve.tensor_tensor(starts, ends, tiles, ALU.subtract))
            link(dve.tensor_scalar(cnt, starts, float(P), -1.0, ALU.mult, ALU.add))
            link(dve.tensor_tensor(OFF, INC, TOT, ALU.subtract))
            link(dve.tensor_tensor(et(OFF), et(OFF), cnt.unsqueeze(2).broadcast_to([P, NE, NT]), ALU.add))
            link(dve.tensor_tensor(te(POSA), te(Y[:, 0:NT * NE]), OFF.rearrange("p (e t) -> p t e", e=NE), ALU.add))
            for k, mark in enumerate((OH0, OH1)):
                link(dve.tensor_tensor(KY, mark, POSA, ALU.mult))
                link(dve.tensor_reduce(posf[:, k, :], te(KY), AX_X, ALU.add))
            dve.tensor_copy(pos[:], posf[:]).then_inc(pos_ready, 1)

            def tile_experts():
                gj = grid.rearrange("p (j e) -> p j e", e=NE)
                rc.link(dve.tensor_tensor(gj, ends.unsqueeze(1).broadcast_to([P, SJ, NE]),
                                          iota[:, 0:SJ].unsqueeze(2).broadcast_to([P, SJ, NE]), ALU.is_le))
                rc.link(dve.memset(eidf[:, SJ:], 0.0))
                rc.link(dve.tensor_reduce(eidf[:, 0:SJ], gj, AX_X, ALU.add))
                rc.link(dve.tensor_scalar(eidf[:, 0:SJ], eidf[:, 0:SJ], NE - 1.0, None, ALU.min))
                dve.tensor_copy(eid[:], eidf[:]).then_inc(eid_ready, 1)

            tile_experts()

            def first_half(r, begun):
                for q in range(4):
                    j = r * 4 + q
                    dve.wait_ge(B["het_done"], j * 2 + 1)
                    gate(B, 0, j * 2 + 3)
                    if begun or q >= 2:
                        dve.wait_ge(s_scat[0][(q + 2) % 4], r * 32 + (32 if q >= 2 else 0))
                    x_to_xf(B, j + 2, 0, (q + 2) % 4)
                    dve.wait_ge(B["het_done"], j * 2 + 2)
                    gate(B, 1, j * 2 + 4)
                    if begun or q == 3:
                        dve.wait_ge(s_scat[1][(q + 1) % 4], r * 32 + (32 if q == 3 else 0))
                    x_to_xf(B, j + HT + 1, 1, (q + 1) % 4)
                    dve.wait_ge(B["y_done"], j + 1)
                    dve.tensor_copy(ysh[:, bass.ds(j, 1), :].rearrange("p s d -> p (s d)"), YO[q % 2][:, 0:DM]).then_inc(B["y_used"], 1)

            first_half(0, False)
            with dve.Fori(1, HT // 4) as r:
                first_half(r, True)

            gate(D, 0, 1)
            gate(D, 1, 2)
            def four_tiles(j, begun):
                for q in range(4):
                    n = j * 4 + q
                    dve.wait_ge(D["het_done"], n + 1)
                    gate(D, q % 2, n + 3)
                    dve.wait_ge(D["y_done"], n + 1)
                    if begun:
                        dve.wait_ge(s_store[q], j * 16)
                    dve.tensor_copy(ob[:, q, :], YO[q % 2][:, 0:DM]).then_inc(D["y_used"], 1)

            four_tiles(0, False)
            with dve.Fori(1, SJ // 4) as j:
                four_tiles(j, True)

            gate(E, 0, 1)
            gate(E, 1, 2)
            c5 = Chain(dve, E["step"], 20)

            def mix(m, u):
                j = m * 4 + u
                a = [acc[:, u, b, :] for b in range(2)]
                w = [[cw[:, k, bass.ds(j + b * HT, 1)] for k in range(2)] for b in range(2)]
                dve.wait_ge(s_gath[u][0], m * 32 + 32)
                c5.mark(dve.scalar_tensor_tensor(a[0], gath[u][:, 0, 0, :], w[0][0], ysh[:, bass.ds(j, 1), :].rearrange("p s d -> p (s d)"),
                                                 ALU.mult, ALU.add))
                dve.wait_ge(s_gath[u][1], m * 32 + 32)
                dve.wait_ge(E["y_done"], j + 1)
                dve.scalar_tensor_tensor(a[1], gath[u][:, 1, 0, :], w[1][0], YO[u % 2][:, 0:DM], ALU.mult, ALU.add).then_inc(E["y_used"], 1)
                c5.wait()
                dve.scalar_tensor_tensor(a[0], gath[u][:, 0, 1, :], w[0][1], a[0], ALU.mult, ALU.add).then_inc(gath_used, 1)
                dve.wait_ge(E["y_used"], j + 3)
                dve.scalar_tensor_tensor(a[1], gath[u][:, 1, 1, :], w[1][1], a[1], ALU.mult, ALU.add).then_inc(gath_used, 1)
                for b in range(2):
                    dve.wait_ge(gath_used, j * 2 + b + 1)
                    c5.mark(dve.bn_stats(st4[:, b, :], a[b]))
                c5.wait(carry)
                for b in range(2):
                    dve.bn_aggr(mv5[:, u, b, :], st4[:, b, :]).then_inc(st5_ready, 1)

            def finish_out(m, u):
                j = m * 4 + u
                dve.wait_ge(r5_ready, m * 2 + u // 2 + 1)
                for b in range(2):
                    c5.mark(dve.tensor_scalar(acc[:, u, b, :], acc[:, u, b, :], mv5[:, u, b, 0:1], r5[:, 1, u, b:b + 1],
                                              ALU.subtract, ALU.mult))
                c5.wait()
                for b in range(2):
                    t = j + b * HT
                    dve.tensor_tensor(xa[:, t, :], xa[:, t, :], acc[:, u, b, :], ALU.add).then_inc(out_ready, 1)

            def last_half(m, u, mixes, finishes):
                j = m * 4 + u
                dve.wait_ge(E["het_done"], j * 2 + 1)
                gate(E, 0, j * 2 + 3)
                if mixes:
                    mix(m if u else m - 1, (u - 1) % 4)
                dve.wait_ge(E["het_done"], j * 2 + 2)
                gate(E, 1, j * 2 + 4)
                if finishes:
                    finish_out(m - 1, u)
                    dve.wait_ge(out_ready, j * 2 - 6)

            for u in range(4):
                last_half(0, u, u > 0, False)
            with dve.Fori(1, HT // 4) as m:
                c5.start(m * 20 - 11)
                for u in range(4):
                    last_half(m, u, True, True)
                c5.end()
            c5.start(HT * 5 - 11)
            mix(HT // 4 - 1, 3)
            for u in range(4):
                finish_out(HT // 4 - 1, u)

        @block.scalar
        def _(act):
            win_d = w_in.rearrange("(k p) n -> p k n", p=P)
            act.dma_start(z_w, win_d[:, :, 0:DI]).then_inc(s_win, 16)
            act.dma_start(win_s[:], win_d[:, :, DI:DI + XBD + P]).then_inc(s_win, 16)
            act.dma_start(c_w, win_d[:, :, DI + XBD + P:]).then_inc(s_win, 16)
            act.dma_start(rw[:], rows.broadcast_to([P, NC_R])).then_inc(s_rw, 16)
            act.dma_start(sel_f, sel).then_inc(s_sel, 16)
            act.dma_start(gate_s[:], w12.rearrange("(k p) n -> p k n", p=P)[:, :, GATE:GATE + NE]).then_inc(s_sel, 16)
            act.dma_start(fc1_w, fc1.rearrange("(k p) n -> p k n", p=P)).then_inc(s_fc1, 16)
            act.dma_start(fc2_s, fc2.rearrange("(k p) n -> p k n", p=P)).then_inc(s_fc2, 16)
            act.dma_start(wout_s, w_out.rearrange("(k p) n -> p k n", p=P)).then_inc(s_wout, 16)
            act.wait_ge(s_rw, 16)
            act.activation(a_neg[:], rw[:, R_ALOG:R_ALOG + NH], ACT.Exp).then_inc(aneg_ready, 1)
            act.wait_ge(s_cs, 16)

            def take_hs(n, k):
                act.wait_ge(vt_done, n * 2 + k + 1)
                act.activation(hsT[:, k, :], X[1 - k][:, :], ACT.Identity, bias=lnb[:, k:k + 1],
                               scale=lnw[:, k:k + 1]).then_inc(hst_ready, 1)

            take_hs(0, 0)
            take_hs(0, 1)

            def take_high(made, dst, n):
                act.wait_ge(lo_ready, n + 1)
                act.activation(dst, made, ACT.Copy).then_inc(hi_ready, 1)

            for n in range(WEIGHT_SPLITS):
                _, made, parts_r = weight_splits[n]
                take_high(made, parts_r[:, 0], n)
            take_high(hs_made, hr[:, 0], WEIGHT_SPLITS)
            with act.Fori(0, NB) as i:
                act.wait_ge(na_ready, i + 1)
                act.activation(dtw[:, 2, :, :], dtw[:, 1, :, :], ACT.Exp).then_inc(e_ready, 1)
                act.wait_ge(w1_ready, i + 1)
                act.activation(dtw[:, 13, :, :], dtw[:, 3, :, :], ACT.Ln).then_inc(ln_ready, 1)
                act.wait_ge(ct_done, i * 4 + 3)
                act.activation(cT[:, 2, :], W[2][:, :], ACT.Copy).then_inc(ct2_ready, 1)
                act.wait_ge(a_ready, i + 1)
                act.activation(dtw[:, 4, :, :], dtw[:, 12, :, :], ACT.Exp).then_inc(da_ready, 1)
                act.wait_ge(bt_done, i + 1)
                act.activation(bT[:], X[0][:, :], ACT.Copy).then_inc(bt_ready, 1)
                for c in range(CH):
                    act.wait_ge(z_done, i * 4 + c + 1)
                    act.activation(sz[:, c, :], W[(c + 1) % 3][:, :], ACT.Silu).then_inc(sz_ready, 1)
                act.wait_ge(cum_done, i + 1)
                act.activation(pwd[:].rearrange("p a c h -> p (a c h)"), X[0][:, 0:2 * CH * NH], ACT.Exp).then_inc(pwd_ready, 1)
                for g in range(NG):
                    q = slice(g * HD, (g + 1) * HD)
                    act.activation(dec[q, :, :], X[0][q, 2 * CH * NH:3 * CH * NH].rearrange("p (c g j) -> p g c j", c=CH, g=NG)[:, g],
                                   ACT.Exp).then_inc(pwd_ready, 1)
                for f in range(KF):
                    act.wait_ge(fc1_done, i * 8 + f + 1)
                    act.activation(gT[:, f, :], W[(f + 2) % 3][:, :], ACT.Gelu_apprx_tanh,
                                   bias=f1b[:, f:f + 1]).then_inc(gelu_ready, 1)

                def take_y(c):
                    act.wait_ge(yt_done, i * 4 + c + 1)
                    bk = X[0] if c < 3 else W[2]
                    for k in range(DI // P):
                        ins = act.activation(ynT[:, k, :], bk[:, k * P:(k + 1) * P], ACT.Copy, scale=nrw[:, k:k + 1])
                    ins.then_inc(ynt_ready, 1)

                for c in range(CH):
                    if c > 0:
                        take_y(c - 1)
                    act.wait_ge(yg_ready, i * 4 + c + 1)
                    act.activation(ygn[:], yg[:], ACT.Square, accum_out=rr[:, 0:1]).then_inc(ssq_ready, 1)
                    if c == CH - 1:
                        take_hs(i + 1, 0)
                        take_hs(i + 1, 1)
                    act.wait_ge(rr_ready, i * 4 + c + 1)
                    act.activation(ygn[:], yg[:], ACT.Copy, scale=rr[:, 3:4]).then_inc(ygn_ready, 1)
                take_y(CH - 1)
                take_high(hs_made, hr[:, 0], i + WEIGHT_SPLITS + 1)

            def two_blocks(i, begun):
                for u in range(2):
                    n = i * 2 + u
                    if begun:
                        act.wait_ge(lg_done, n - 1)
                    for k in range(KD):
                        act.wait_ge(ft_done, n * 2 + k + 1)
                        act.activation(fT[u][:, k, :], X[1 - k][:, :], ACT.Copy).then_inc(ft_ready, 1)

            two_blocks(0, False)
            with act.Fori(1, NB // 2) as i:
                two_blocks(i, True)
            act.wait_ge(mx_ready, 1)
            act.activation(RT[2], RT[6], ACT.Exp).then_inc(ex_ready, 1)

            def silu(S_, a, n):
                act.wait_ge(S_["h12_done"], n)
                act.activation(hs_[:, a, :], W[a][:, 0:EI], ACT.Silu).then_inc(S_["silu_ready"], 1)

            def take_h(S_, a, n):
                act.wait_ge(S_["het_done"], n)
                act.activation(heT[:, a].rearrange("p k t -> p (k t)"), X[a][0:EK, 0:2 * P],
                               ACT.Copy).then_inc(S_["het_ready"], 1)

            def take_x(S_, dst, n):
                act.wait_ge(S_["xt_done"], n)
                act.activation(dst.rearrange("p k t -> p (k t)"), I[:, 0:DM], ACT.Copy).then_inc(S_["xt_ready"], 1)

            def normed(j, s):
                t = j + HT
                act.activation(xf[:, 0, s, :], xa[:, bass.ds(t, 1), :].rearrange("p s d -> p (s d)"), ACT.Identity,
                               bias=nmf[:, bass.ds(t, 1)], scale=rsf[:, bass.ds(t, 1)]).then_inc(E["xf_ready"], 1)

            def shared(S_):
                take_x(S_, xfT, 1)
                silu(S_, 0, 1)
                silu(S_, 1, 2)
                take_h(S_, 0, 1)
                take_x(S_, xfT, 2)
                with act.Fori(0, HT // 4) as r:
                    for q in range(4):
                        j = r * 4 + q
                        silu(S_, 0, j * 2 + 3)
                        take_h(S_, 1, j * 2 + 2)
                        if S_ is E:
                            normed(j + 3, (q + 3) % 4)
                        silu(S_, 1, j * 2 + 4)
                        take_x(S_, xfT, j + 3)
                        take_h(S_, 0, j * 2 + 3)

            shared(B)
            for q in range(2):
                take_x(D, xsT[:, q], q + 1)
                silu(D, q, q + 1)
            take_x(D, xsT[:, 0], 3)
            take_h(D, 0, 1)
            with act.Fori(0, SJ // 4) as j:
                for q in range(4):
                    n = j * 4 + q
                    silu(D, q % 2, n + 3)
                    take_x(D, xsT[:, (q + 1) % 2], n + 4)
                    take_h(D, (q + 1) % 2, n + 2)
            for q in range(3):
                normed(q, q)
            shared(E)

        @block.gpsimd
        def _(pool):
            pc = Chain(pool, pool_step, CH * 3)
            pool.memset(nhalf[:], -0.5).then_inc(pool_init, 1)
            pool.wait_ge(pool_init, 1)

            def rsqrt(link, dst, tmp, var, width=1):
                link(pool.tensor_scalar(tmp, var, EPS, 1.0, ALU.add, ALU.mult))
                return pool.tensor_tensor(dst, tmp, nhalf[:, 0:width], ALU.pow)

            def norm_scales(n, link):
                pool.wait_ge(st_ready, n * 4 + 4)
                pool.sem_inc(carry, 1)
                link(pool.tensor_copy(nw[:, 0, :], mvb[:, :, 1]), carry)
                link(rsqrt(link, nw[:, 2, :], nw[:, 1, :], nw[:, 0, :], CH))
                link(pool.tensor_tensor(nw[:, 3, :], nw[:, 2, :], nw[:, 2, :], ALU.mult))
                link(pool.tensor_tensor(nw[:, 3, :], nw[:, 3, :], nw[:, 0, :], ALU.mult), carry)
                pool.tensor_copy(rs1[:, bass.ts(n, CH)], nw[:, 2, :]).then_inc(rs1_ready, 1)
                link(rsqrt(link, nw[:, 4, :], nw[:, 1, :], nw[:, 3, :], CH))
                pool.wait_ge(rs1_ready, n + 1)
                pool.tensor_tensor(nw[:, 5, :], nw[:, 4, :], nw[:, 2, :], ALU.mult).then_inc(rs_ready, 1)

            def second_scales(n, link):
                pool.wait_ge(stf_ready, n * 4 + 4)
                pool.sem_inc(carry, 1)
                link(pool.tensor_scalar(nf[:, 0, :], mvg[:, :, 1], EPS, 1.0, ALU.add, ALU.mult))
                link(pool.tensor_tensor(nf[:, 1, :], nf[:, 0, :], nhalf[:], ALU.pow), carry)
                pool.tensor_copy(rsf_all[:, bass.ds(n * CH, CH)], nf[:, 1, :]).then_inc(rsf_ready, 1)

            PN = 7
            pn = Chain(pool, pool_norm, PN + 2)
            norm_scales(0, pn.link)
            pool.wait_ge(s_rw, 16)
            with pool.Fori(0, NB) as i:
                pc.start(i * pc.per)
                pn.start(i * pn.per + PN)

                def heads(ap):
                    return ap.rearrange("p (g j d) -> p g j d", g=NG, j=JH)

                def bc(ap):
                    return ap.rearrange("p (g j) -> p g j", g=NG).unsqueeze(3).broadcast_to([P, NG, JH, HD])

                def steps(c):
                    xh = xbd[:, c, 0:XB].rearrange("p (g d) -> p g d", g=NG).unsqueeze(2).broadcast_to([P, NG, JH, HD])
                    pool.tensor_tensor(heads(xdt[:, c % 2, :]), xh, bc(dtw[:, 11, c, :]), ALU.mult).then_inc(xdt_ready, 1)
                    pool.wait_ge(pwd_ready, i * 3 + 3)
                    pool.wait_ge(xdt_ready, i * 4 + c + 1)
                    pool.tensor_tensor(heads(xw[:, c % 2, :]), heads(xdt[:, c % 2, :]), bc(pwd[:, 1, c, :]),
                                       ALU.mult).then_inc(xw_ready, 1)

                pool.wait_ge(dt_ready, i + 1)
                norm_scales(i + 1, pn.link)
                steps(0)
                steps(1)
                second_scales(i, pn.link)
                pn.end()

                def finish(c):
                    pool.wait_ge(st3_ready, i * 4 + c + 1)
                    pool.sem_inc(carry, 1)
                    rsqrt(pc.link, r3[:, 1:2], r3[:, 0:1], mv3[:, 1:2]).then_inc(r3_ready, 1)

                for c in range(CH):
                    pool.wait_ge(inter_done, i * 4 + c + 1)
                    pool.tensor_tensor(S[:], S[:], dec[:, c, :].unsqueeze(2).broadcast_to([P, JH, P]),
                                       ALU.mult).then_inc(s_scaled, 1)
                    xh = xbd[:, c, 0:XB].rearrange("p (g d) -> p g d", g=NG).unsqueeze(2).broadcast_to([P, NG, JH, HD])
                    pool.tensor_tensor(heads(dx[:]), xh, bc(rw[:, R_D:R_D + NH]), ALU.mult).then_inc(dx_ready, 1)
                    pool.wait_ge(dx_ready, i * 4 + c + 1)
                    pool.wait_ge(t2_done, i * 4 + c + 1)
                    pc.link(pool.tensor_tensor(t3[:], t2[:], dx[:], ALU.add))
                    if c > 0:
                        pool.wait_ge(ygn_ready, i * 4 + c)
                    pool.wait_ge(sz_ready, i * 4 + 4)
                    pool.tensor_tensor(yg[:], t3[:], sz[:, c, :], ALU.mult).then_inc(yg_ready, 1)
                    if c < 2:
                        steps(c + 2)
                    if c > 0:
                        finish(c - 1)
                    pool.wait_ge(ssq_ready, i * 4 + c + 1)
                    pool.sem_inc(carry, 1)
                    pc.link(pool.tensor_scalar(rr[:, 1:2], rr[:, 0:1], 1.0 / DI, EPS, ALU.mult, ALU.add))
                    pool.tensor_tensor(rr[:, 3:4], rr[:, 1:2], nhalf[:, 0:1], ALU.pow).then_inc(rr_ready, 1)
                finish(CH - 1)
                pc.end()

            pn.start(NB * pn.per + PN)
            second_scales(NB, pn.link)

            def places(j, s, n):
                pool.tensor_copy(posb[:, s], pos[:].rearrange("p k (b t) -> p k b t", b=2)[:, :, :, bass.ds(j, 1)].rearrange("p k b o -> p k (b o)")
                                 ).then_inc(posb_ready, 1)
                pool.wait_ge(posb_ready, n)

            def place(s, b, k):
                return bass.IndirectOffsetOnAxis(ap=posb[:, s, k, b:b + 1].bitcast(U32), axis=0)

            def scatter_four(r, begun):
                for q in range(4):
                    j = r * 4 + q
                    if begun:
                        pool.wait_ge(s_scat[0][q], r * 32)
                        pool.wait_ge(s_scat[1][q], r * 32)
                        pool.sem_inc(carry, 1)
                    places(j, q, j + 1)
                    for b in range(2):
                        pool.wait_ge(xg_ready if b else B["xf_ready"], j + 1)
                        pool.sem_inc(carry, 1)
                        for k in range(2):
                            pool.indirect_dma_start(xs_dram, place(q, b, k), xf[:, b, q, :], None).then_inc(s_scat[b][q], 16)

            pool.wait_ge(pos_ready, 1)
            pool.wait_ge(s_zero, 16)
            scatter_four(0, False)
            with pool.Fori(1, HT // 4) as r:
                scatter_four(r, True)
            for landed in s_scat[0] + s_scat[1]:
                pool.wait_ge(landed, 32 * HT // 4)

            for q in range(4):
                pool.wait_ge(s_store[q], 16 * (SJ // 4))

            def gather(u, b):
                for k in range(2):
                    pool.indirect_dma_start(gath[u][:, b, k, :], None, eo_dram, place(u, b, k)).then_inc(s_gath[u][b], 16)

            def last_scales(n, h):
                s = slice(2 * h, 2 * h + 2)
                pool.wait_ge(st5_ready, n * 4 + 4)
                pool.sem_inc(carry, 1)
                pool.tensor_scalar(r5[:, 0, s, :], mv5[:, s, :, 1], EPS, 1.0, ALU.add, ALU.mult).then_inc(ve5_ready, 1)
                pool.wait_ge(ve5_ready, n + 1)
                pool.tensor_tensor(r5[:, 1, s, :], r5[:, 0, s, :], nhalf[:].rearrange("p (s b) -> p s b", s=2), ALU.pow).then_inc(r5_ready, 1)

            for u in range(4):
                places(u, u, HT + u + 1)
                gather(u, 0)
                gather(u, 1)
            with pool.Fori(0, HT // 4 - 1) as m:
                for u in range(4):
                    j = m * 4 + u
                    pool.wait_ge(gath_used, j * 2 + 2)
                    pool.sem_inc(carry, 1)
                    places(j + 4, u, j + HT + 5)
                    pool.sem_inc(carry, 1)
                    gather(u, 0)
                    if u % 2 == 1:
                        last_scales(m * 2 + u // 2, u // 2)
                    gather(u, 1)
            last_scales(HT // 2 - 2, 0)
            last_scales(HT // 2 - 1, 1)

def kernel(**inputs):
    import concourse.bacc as _bacc
    from concourse.bass_utils import run_bass_kernel_spmd as _run

    a = {k: np.asarray(v) for k, v in inputs.items()}
    g = lambda n: a["L0_attn_" + n]
    f = lambda n: a["L0_ffn_" + n]
    xs = g("hidden_states")
    w_in = g("W_in")
    zc, xc, bcol, cc = DI, XB, XB, DI
    o1 = zc + xc + bcol
    c_cols = w_in[:, o1:o1 + cc].reshape(DM, NG, JH, HD).transpose(0, 2, 1, 3).reshape(DM, cc)
    w_in = np.concatenate([w_in[:, :o1], w_in[:, o1 + cc:], c_cols], 1)
    s1 = f("sw1").reshape(2, EI, DM)
    s2 = f("sw2").reshape(2, EI, DM)
    gates = [s1[0], s2[0], f("gate_w"), s1[1], s2[1]]
    for e in range(NE):
        gates += [f("w1")[e], f("w2")[e]]
    w12 = np.ascontiguousarray(np.concatenate(gates, 0).T)
    w3 = np.concatenate([f("sw3").T, f("w3").transpose(0, 2, 1).reshape(NE * EI, DM)], 0)
    cols = np.concatenate([g("ln_w").reshape(KD, P).T, g("ln_b").reshape(KD, P).T,
                           g("norm_w").reshape(DI // P, P).T, g("fc1_b").reshape(KF, P).T], 1)
    r = np.arange(P)
    masks = np.concatenate([np.eye(P), r[:, None] <= r[None, :], r[:, None] > r[None, :], np.ones((P, P))], 1)
    e8 = np.arange(NE)
    iota = np.broadcast_to(np.concatenate([r, NE - e8])[None], (P, P + NE))
    per_seq = xs.shape[1] // TB
    keep = np.where(np.arange(8) % per_seq == 0, 0, 1).astype(np.float32)
    cst = np.concatenate([masks.astype(np.float32), iota.astype(np.float32), cols,
                          np.broadcast_to(keep[None], (P, 8))], 1)
    rows = np.concatenate([g("dt_bias"), g("A_log"), g("D"), g("fc2_b")])[None]
    sel = np.zeros((3, NH, NH, P), np.float32)
    sel[:, e8, e8] = 1
    arrays = {"x": xs.reshape(-1, DM), "w_in": w_in, "w_out": g("W_out"), "fc1": g("fc1_w"), "fc2": g("fc2_w"),
              "w12": w12, "w3": w3, "cst": cst, "rows": rows, "sel": sel.reshape(3 * NH, NH * P)}
    arrays = {k: np.ascontiguousarray(v) for k, v in arrays.items()}
    nc = _bacc.Bacc("TRN2", target_bir_lowering=False, num_devices=1)
    args = [nc.dram_tensor(n, v.shape, mybir.dt.from_np(v.dtype), kind="ExternalInput").ap() for n, v in arrays.items()]
    out = nc.dram_tensor("out", arrays["x"].shape, F32, kind="ExternalOutput").ap()
    build(nc, *args, out)
    got = _run(nc, [arrays], core_ids=[0])
    return got.results[0]["out"].reshape(xs.shape)
```
